# Optimizing a Trainium2 kernel written in Bass

```python
import numpy as np
import jax
import jax.numpy as jnp

def _softmax(x, axis=-1):
    return jax.nn.softmax(x, axis=axis)

def _gelu(x):
    return jax.nn.gelu(x, approximate=True)

def _silu(x):
    return jax.nn.silu(x)

def _sigmoid(x):
    return jax.nn.sigmoid(x)

def _layernorm(x, axis=-1, eps=1e-05):
    m = jnp.mean(x, axis=axis, keepdims=True)
    v = jnp.var(x, axis=axis, keepdims=True)
    return (x - m) / jnp.sqrt(v + eps)

def _scatter_add(tgt, idx, src, axis=0):
    return tgt.at[idx].add(src)

def _segment_sum(src, seg, n):
    return jax.ops.segment_sum(src, seg, n)
kernel_name = 'mk_decoder_preln_d1_seqx_r8_5c9738'

def setup_inputs(seed: int=0):
    np.random.seed(seed)
    _w = jnp.asarray

    def _rec_inputs():
        import jax
        import jax.numpy as jnp
        _rk = jax.random.key(seed)
        x = -0.0003929 + 0.9999 * jax.random.normal(jax.random.fold_in(_rk, 1), (4, 512, 128), jnp.float32)
        _lenS = 512 - jax.random.randint(jax.random.fold_in(_rk, 7), (4,), 0, max(1, 512 // 4) + 1, jnp.int32)
        _lenS2 = 77 - jax.random.randint(jax.random.fold_in(_rk, 8), (4,), 0, max(1, 77 // 4) + 1, jnp.int32)
        _ctx_1024P = jax.random.normal(jax.random.fold_in(_rk, 11), (4, 16, 128), jnp.float32)
        _ctx_1024c = jax.random.dirichlet(jax.random.fold_in(_rk, 511), 0.3 * jnp.ones((16,), jnp.float32), (4, 77))
        _ctx_1024t = jnp.einsum('bsk,bkd->bsd', _ctx_1024c, _ctx_1024P)
        _ctx_1024t = _ctx_1024t * jax.lax.rsqrt(jnp.mean(jnp.square(_ctx_1024t)) + 1e-12) * 0.953939
        ctx_1024 = 2.81802e-05 + 1.00001 * (_ctx_1024t + 0.3 * jax.random.normal(jax.random.fold_in(_rk, 611), (4, 77, 128), jnp.float32))
        return (x, ctx_1024)
    x, ctx_1024 = _rec_inputs()

    def _L0_attn_setup():
        import jax, jax.numpy as jnp
        import numpy as np
        L, B, E = (256, 4, 128)
        H = 8
        D1 = 256
        HD = D1 // H
        MAX_L = 256
        EPS = 1e-08

        def _simple_rmsnorm(x):
            d = x.shape[-1]
            rms = jnp.linalg.norm(x, axis=-1, keepdims=True) * d ** (-0.5)
            return x / (rms + EPS)

        def _toeplitz_causal_fft(v, zero, pos):
            n = v.shape[-2]
            coef = jnp.concatenate([zero, pos[:, :n - 1]], axis=-1)
            m = 2 * n
            cf = jnp.fft.rfft(coef, m, axis=-1)
            vf = jnp.fft.rfft(v, m, axis=-2)
            out = jnp.fft.irfft(cf[None, :, :, None] * vf, m, axis=-2)
            return out[:, :, :n, :]
        key = jax.random.key(seed)
        ks = jax.random.split(key, 9)
        std = 0.02
        return {'x': jax.random.normal(ks[0], (L, B, E), jnp.float32), 'Wu': jax.random.normal(ks[1], (D1, E), jnp.float32) * std, 'bu': jax.random.normal(ks[2], (D1,), jnp.float32) * std, 'Wv': jax.random.normal(ks[3], (D1, E), jnp.float32) * std, 'bv': jax.random.normal(ks[4], (D1,), jnp.float32) * std, 'Wo': jax.random.normal(ks[5], (E, D1), jnp.float32) * std, 'bo': jax.random.normal(ks[6], (E,), jnp.float32) * std, 'zero': jax.random.normal(ks[7], (H, 1), jnp.float32) * 0.1, 'pos': jax.random.normal(ks[8], (H, MAX_L - 1), jnp.float32) * 0.1}
    _L0_attn_all = _L0_attn_setup()
    _L0_attn_in = {k: v for k, v in _L0_attn_all.items() if k in ('Wu', 'bu', 'Wv', 'bv', 'Wo', 'bo', 'zero', 'pos')}
    del _L0_attn_all

    def _L0_xattn_setup():
        import jax, jax.numpy as jnp
        import numpy as np
        B, L, HID, H, DH, M = (4, 512, 128, 16, 64, 128)
        EPS = 0.001

        def _relu_kernel(x, proj):
            ratio = 1.0 / float(np.sqrt(proj.shape[0]))
            return jax.nn.relu(ratio * jnp.einsum('blhd,md->blhm', x, proj)) + EPS
        key = jax.random.key(seed)
        ks = jax.random.split(key, 7)
        lim = float(np.sqrt(6.0 / (HID + HID)))
        return {'query_input': jax.random.normal(ks[0], (B, L, HID), jnp.float32), 'source_input': jax.random.normal(ks[1], (B, L, HID), jnp.float32), 'Wq': jax.random.uniform(ks[2], (HID, H, DH), jnp.float32, -lim, lim), 'Wk': jax.random.uniform(ks[3], (HID, H, DH), jnp.float32, -lim, lim), 'Wv': jax.random.uniform(ks[4], (HID, H, DH), jnp.float32, -lim, lim), 'Wo': jax.random.uniform(ks[5], (H, DH, HID), jnp.float32, -lim, lim), 'proj': jax.random.normal(ks[6], (M, DH), jnp.float32), 'training': 0}
    _L0_xattn_all = _L0_xattn_setup()
    _L0_xattn_in = {k: v for k, v in _L0_xattn_all.items() if k in ('Wq', 'Wk', 'Wv', 'Wo', 'proj')}
    del _L0_xattn_all

    def _L0_ffn_setup():
        import jax, jax.numpy as jnp
        import numpy as np
        from jax import lax
        DIM = 128
        HID = 256
        E = 8
        K = 2
        B, T = (2, 64)
        key = jax.random.key(seed)
        ks = jax.random.split(key, 5)
        scale = 1.0 / np.sqrt(DIM)
        x = jax.random.normal(ks[0], (B, T, DIM), dtype=jnp.float32)
        router_w = jax.random.normal(ks[1], (E, DIM), dtype=jnp.float32) * scale
        w_gate = jax.random.normal(ks[2], (E, HID, DIM), dtype=jnp.float32) * scale
        w_up = jax.random.normal(ks[3], (E, HID, DIM), dtype=jnp.float32) * scale
        w_down = jax.random.normal(ks[4], (E, DIM, HID), dtype=jnp.float32) * (1.0 / np.sqrt(HID))
        return {'x': x, 'router_w': router_w, 'w_gate': w_gate, 'w_up': w_up, 'w_down': w_down}
    _L0_ffn_all = _L0_ffn_setup()
    _L0_ffn_in = {k: v for k, v in _L0_ffn_all.items() if k in ('router_w', 'w_gate', 'w_up', 'w_down')}
    del _L0_ffn_all
    return {'x': x, 'ctx_1024': ctx_1024, 'L0_attn_Wu': _L0_attn_in['Wu'], 'L0_attn_bu': _L0_attn_in['bu'], 'L0_attn_Wv': _L0_attn_in['Wv'], 'L0_attn_bv': _L0_attn_in['bv'], 'L0_attn_Wo': _L0_attn_in['Wo'], 'L0_attn_bo': _L0_attn_in['bo'], 'L0_attn_zero': _L0_attn_in['zero'], 'L0_attn_pos': _L0_attn_in['pos'], 'L0_xattn_Wq': _L0_xattn_in['Wq'], 'L0_xattn_Wk': _L0_xattn_in['Wk'], 'L0_xattn_Wv': _L0_xattn_in['Wv'], 'L0_xattn_Wo': _L0_xattn_in['Wo'], 'L0_xattn_proj': _L0_xattn_in['proj'], 'L0_ffn_router_w': _L0_ffn_in['router_w'], 'L0_ffn_w_gate': _L0_ffn_in['w_gate'], 'L0_ffn_w_up': _L0_ffn_in['w_up'], 'L0_ffn_w_down': _L0_ffn_in['w_down']}

def reference(x, ctx_1024, L0_attn_Wu, L0_attn_bu, L0_attn_Wv, L0_attn_bv, L0_attn_Wo, L0_attn_bo, L0_attn_zero, L0_attn_pos, L0_xattn_Wq, L0_xattn_Wk, L0_xattn_Wv, L0_xattn_Wo, L0_xattn_proj, L0_ffn_router_w, L0_ffn_w_gate, L0_ffn_w_up, L0_ffn_w_down):
    import jax
    import jax.numpy as jnp

    def _L0_attn_ref(x, Wu, bu, Wv, bv, Wo, bo, zero, pos):
        import jax, jax.numpy as jnp
        import numpy as np
        L, B, E = (256, 4, 128)
        H = 8
        D1 = 256
        HD = D1 // H
        MAX_L = 256
        EPS = 1e-08

        def _simple_rmsnorm(x):
            d = x.shape[-1]
            rms = jnp.linalg.norm(x, axis=-1, keepdims=True) * d ** (-0.5)
            return x / (rms + EPS)

        def _toeplitz_causal_fft(v, zero, pos):
            n = v.shape[-2]
            coef = jnp.concatenate([zero, pos[:, :n - 1]], axis=-1)
            m = 2 * n
            cf = jnp.fft.rfft(coef, m, axis=-1)
            vf = jnp.fft.rfft(v, m, axis=-2)
            out = jnp.fft.irfft(cf[None, :, :, None] * vf, m, axis=-2)
            return out[:, :, :n, :]
        n, b, e = x.shape
        shortcut = x
        xn = _simple_rmsnorm(x)
        u = jax.nn.silu(jnp.einsum('nbe,de->nbd', xn, Wu) + bu)
        v = jax.nn.silu(jnp.einsum('nbe,de->nbd', xn, Wv) + bv)
        vh = v.transpose(1, 0, 2).reshape(b, n, H, HD).transpose(0, 2, 1, 3)
        oh = _toeplitz_causal_fft(vh, zero, pos)
        o = oh.transpose(0, 2, 1, 3).reshape(b, n, D1).transpose(1, 0, 2)
        o = u * o
        out = jnp.einsum('nbd,ed->nbe', o, Wo) + bo + shortcut
        return out

    def _L0_xattn_ref(query_input, source_input, Wq, Wk, Wv, Wo, proj, training):
        import jax, jax.numpy as jnp
        import numpy as np
        B, L, HID, H, DH, M = (4, 512, 128, 16, 64, 128)
        EPS = 0.001

        def _relu_kernel(x, proj):
            ratio = 1.0 / float(np.sqrt(proj.shape[0]))
            return jax.nn.relu(ratio * jnp.einsum('blhd,md->blhm', x, proj)) + EPS
        q = jnp.einsum('bld,dhk->blhk', query_input, Wq)
        k = jnp.einsum('bld,dhk->blhk', source_input, Wk)
        v = jnp.einsum('bld,dhk->blhk', source_input, Wv)
        qp = _relu_kernel(q, proj)
        kp = _relu_kernel(k, proj)
        kvs = jnp.einsum('blhm,blhd->bhmd', kp, v)
        num = jnp.einsum('blhm,bhmd->blhd', qp, kvs)
        ks_sum = jnp.sum(kp, axis=1)
        den = jnp.einsum('blhm,bhm->blh', qp, ks_sum)
        att = num / den[..., None]
        return jnp.einsum('blhd,hdk->blk', att, Wo)

    def _L0_ffn_ref(x, router_w, w_gate, w_up, w_down):
        import jax, jax.numpy as jnp
        import numpy as np
        from jax import lax
        DIM = 128
        HID = 256
        E = 8
        K = 2
        B, T = (2, 64)
        Bb, Tt, D = x.shape
        N = Bb * Tt
        xf = x.reshape(N, D)
        logits = xf @ router_w.T
        routing = jax.nn.softmax(logits, axis=-1)
        top_w, top_i = lax.top_k(routing, K)
        top_w = top_w / jnp.sum(top_w, axis=-1, keepdims=True)
        combine = jnp.zeros((N, E), dtype=x.dtype)
        combine = combine.at[jnp.arange(N)[:, None], top_i].add(top_w)
        g = jnp.einsum('nd,ehd->neh', xf, w_gate)
        u = jnp.einsum('nd,ehd->neh', xf, w_up)
        h = jax.nn.silu(g) * u
        y = jnp.einsum('neh,edh->ned', h, w_down)
        out = jnp.einsum('ned,ne->nd', y, combine)
        return out.reshape(Bb, Tt, D)
    x = x + _L0_attn_ref(_layernorm(x, axis=-1), L0_attn_Wu, L0_attn_bu, L0_attn_Wv, L0_attn_bv, L0_attn_Wo, L0_attn_bo, L0_attn_zero, L0_attn_pos)
    x = x + _L0_xattn_ref(_layernorm(x, axis=-1), ctx_1024, L0_xattn_Wq, L0_xattn_Wk, L0_xattn_Wv, L0_xattn_Wo, L0_xattn_proj, 0)
    x = x + _L0_ffn_ref(_layernorm(x, axis=-1), L0_ffn_router_w, L0_ffn_w_gate, L0_ffn_w_up, L0_ffn_w_down)
    return x

_drawn_inputs = setup_inputs


def setup_inputs(seed=0):
    import zlib

    import numpy as np

    out = dict(_drawn_inputs(seed))
    spreads = {}
    factors = {'L0_attn_Wu': 8.0,
     'L0_attn_bu': 8.0,
     'L0_attn_Wv': 8.0,
     'L0_attn_bv': 8.0,
     'L0_attn_Wo': 8.0,
     'L0_attn_bo': 11.85,
     'L0_attn_zero': 8.0,
     'L0_attn_pos': 8.0}
    for name, (base, spread) in spreads.items():
        noise = np.random.default_rng([zlib.crc32(name.encode()), seed]).standard_normal(out[name].shape)
        drawn = base * np.exp(spread * noise) if base else spread * noise
        out[name] = jnp.asarray(drawn.astype(out[name].dtype))
    for name, factor in factors.items():
        out[name] = (out[name] * factor).astype(out[name].dtype)
    return out
```

```python
import concourse.bass as bass
from concourse import mybir
from contextlib import ExitStack

F32 = mybir.dt.float32
F32R = mybir.dt.float32r
BF16 = mybir.dt.bfloat16
I32 = mybir.dt.int32
U32 = mybir.dt.uint32
ALU = mybir.AluOpType
ACT = mybir.ActivationFunctionType
AX = mybir.AxisListType

P = 128
NB = 4
POS = 512
TPB = POS // P
TILES = NB * TPB
D1 = 256
MH, MHD = 8, 32
CTX = 77
H, DH, M = 16, 64, 128
HA = DH + 2
G = 4
NG = H // G
CH = H * DH // P
E, HID = 8, 256
TOKENS = NB * POS
TOPK = 2
CAP = TOKENS
ROW = P + 2
PAD_ROW = E * CAP
BLOCKS = 40
RING = 8
LN_EPS = 1e-5
RMS_EPS = 1e-8
RELU_EPS = 1e-3
RATIO = float(M) ** -0.5
NO_DEST = TOPK * TOKENS


def decoder_kernel(nc, x, ctxT, wuv, bu, bv, woaT, bo, coef, wqT, wkT, wv, wo, projT, router, wgu, wd,
                   out, xs, ys):
    with ExitStack() as ctx:
        def sb(name, shape, dt=F32, stack=ctx):
            return stack.enter_context(nc.sbuf_tensor(name, shape, dt))

        def sem(name):
            return ctx.enter_context(nc.semaphore(name))

        X = sb("X", [P, TILES, P])
        y2T_hi = sb("y2T_hi", [P, NB, POS], F32R)
        y2T_lo = sb("y2T_lo", [P, NB, POS], F32R)
        wqp_hi = sb("wqp_hi", [P, H, M], F32R)
        wqp_lo = sb("wqp_lo", [P, H, M], F32R)
        kvs_hi = sb("kvs_hi", [P, NB, H * HA], F32R)
        kvs_lo = sb("kvs_lo", [P, NB, H * HA], F32R)
        kbias = sb("kbias", [P, NB, H * HA], F32R)
        wo_hi = sb("wo_hi", [P, CH, P], F32R)
        wo_lo = sb("wo_lo", [P, CH, P], F32R)
        router_sb = sb("router_sb", [P, E])
        outT = sb("outT", [P, POS])
        ident = sb("ident", [P, P])
        mean_of_rows = sb("mean_of_rows", [P, P], F32R)
        stats = sb("stats", [P, TILES, 6])
        moments = sb("moments", [P, TILES, 2])
        moments_b = sb("moments_b", [P, TPB, 2])
        rstd = sb("rstd", [P, TPB])
        var_eps = sb("var_eps", [P, TPB])
        p_mhalf = sb("p_mhalf", [P, TILES])
        iota_e = sb("iota_e", [P, E])
        tri = sb("tri", [P, E, E])
        before = sb("before", [P, P], BF16)
        ones_bf = sb("ones_bf", [P, P], BF16)
        dest = sb("dest", [P, NB, TOPK, TPB], I32)
        seq = sb("seq", [1, BLOCKS])
        pad_row = sb("pad_row", [P, ROW])
        base = sb("base", [P, E])
        table = sb("table", [1, 2, BLOCKS], I32)

        with ExitStack() as first:
            def sa(name, shape, dt=F32):
                return sb(name, shape, dt, first)
            projT_sb = sa("projT_sb", [DH, M])
            wT_sb = sa("wT_sb", [DH, H, P])
            wkp_hi = sa("wkp_hi", [P, H * M], F32R)
            wkp_lo = sa("wkp_lo", [P, H * M], F32R)
            wvo_sb = sa("wvo_sb", [P, CH * P])
            wv_hi = sa("wv_hi", [P, H * DH], F32R)
            wv_lo = sa("wv_lo", [P, H * DH], F32R)
            ctxT_sb = sa("ctxT_sb", [P, NB * CTX])
            ctxT_hi = sa("ctxT_hi", [P, NB * CTX], F32R)
            ctxT_lo = sa("ctxT_lo", [P, NB * CTX], F32R)
            kp = sa("kp", [CTX, H * M])
            v_aug = sa("v_aug", [CTX, H, HA])
            wuv_sb = sa("wuv_sb", [P, 2 * D1])
            wuv_hi = sa("wuv_hi", [P, 2 * D1], F32R)
            wuv_lo = sa("wuv_lo", [P, 2 * D1], F32R)
            woa_sb = sa("woa_sb", [P, 2, P])
            woa_hi = sa("woa_hi", [P, 2, P], F32R)
            woa_lo = sa("woa_lo", [P, 2, P], F32R)
            bias_v = sa("bias_v", [P, 2])
            bias_u = sa("bias_u", [P, 2])
            bias_o = sa("bias_o", [P, 1])
            coef_sb = sa("coef_sb", [P, 2, NB])
            xn = sa("xn", [P, TPB, P])
            y2 = sa("y2", [P, TPB, P])
            xnT_hi = sa("xnT_hi", [P, POS], F32R)
            xnT_lo = sa("xnT_lo", [P, POS], F32R)
            v_hist = sa("v_hist", [P, NB, 2, POS])
            u_sb = sa("u_sb", [P, 2, POS])
            acc = sa("acc", [P, 2, POS])
            o_hi = sa("o_hi", [P, 2, POS], F32R)
            o_lo = sa("o_lo", [P, 2, POS], F32R)
            ones_r = sa("ones_r", [P, P], F32R)
            ln1 = sa("ln1", [P, 9, TILES])
            p_half = sa("p_half", [P, TILES])
            p_mone = sa("p_mone", [P, TILES])
        V_EPS, RSTD, STD, RMS, INV, SCALE, ONE_RSTD, NEG_SHIFT, SHIFT = range(9)

        wgu_hi = sb("wgu_hi", [P, E, 2 * HID], F32R)
        wgu_lo = sb("wgu_lo", [P, E, 2 * HID], F32R)
        wd_hi = sb("wd_hi", [P, E, HID], F32R)
        wd_lo = sb("wd_lo", [P, E, HID], F32R)
        with ExitStack() as second:
            def sc(name, shape, dt=F32):
                return sb(name, shape, dt, second)
            q_hi = sc("q_hi", [P, 3, POS], F32R)
            q_lo = sc("q_lo", [P, 3, POS], F32R)
            rden = sc("rden", [P, TPB, G])
            att = sc("att", [P, 2, TPB, G * DH])
            attT_hi = sc("attT_hi", [P, 2, POS], F32R)
            attT_lo = sc("attT_lo", [P, 2, POS], F32R)
            wgu_raw = sc("wgu_raw", [P, 2, 2 * HID])
            wd_raw = sc("wd_raw", [P, 2, HID])
            rows = sc("rows", [P, TOPK, TPB, ROW])
            y3T = sc("y3T", [P, POS])
            l_max = sc("l_max", [P, TPB])
            l_sub = sc("l_sub", [P, TPB, E])
            l_exp = sc("l_exp", [P, TPB, E])
            l_sum = sc("l_sum", [P, TPB])
            prob = sc("prob", [P, TPB, E])
            top_v = sc("top_v", [P, TPB, 8])
            top_i = sc("top_i", [P, TPB, 8], U32)
            top_f = sc("top_f", [P, TPB, TOPK])
            chosen = sc("chosen", [P, TPB, TOPK, E])
            taken = sc("taken", [P, TPB, E], BF16)
            w_sum = sc("w_sum", [P, TPB])
            slot_e = sc("slot_e", [P, TPB, E])
            slot_k = sc("slot_k", [P, TPB, TOPK, E])
            slot_f = sc("slot_f", [P, TPB, TOPK])
            slot_i = sc("slot_i", [P, TPB, TOPK], I32)
            t_cnt = sc("t_cnt", [1, E], I32)
            t_nb = sc("t_nb", [1, E])
            t_prod = sc("t_prod", [1, E, E])
            t_end = sc("t_end", [1, E])
            t_start = sc("t_start", [1, E])
            t_val = sc("t_val", [1, E])
            t_ge = sc("t_ge", [1, 2, BLOCKS, E])
            t_oh = sc("t_oh", [1, BLOCKS, E])
            t_mul = sc("t_mul", [1, 2, BLOCKS, E])
            t_sum = sc("t_sum", [1, 3, BLOCKS])

        xb = sb("xb", [P, RING, ROW])
        meta = sb("meta", [P, RING, 2], I32)
        xT_hi = sb("xT_hi", [P, RING, P], F32R)
        xT_lo = sb("xT_lo", [P, RING, P], F32R)
        silu_g = sb("silu_g", [P, 2, HID])
        hid = sb("hid", [P, 2, HID])
        hT_hi = sb("hT_hi", [P, 2, HID], F32R)
        hT_lo = sb("hT_lo", [P, 2, HID], F32R)
        yo = sb("yo", [P, RING, P])
        y_back = sb("y_back", [P, TOPK, NB, POS])

        bank = [ctx.enter_context(nc.psum_tensor(f"bank{i}", [P, POS], F32)) for i in range(2)]
        num = ctx.enter_context(nc.psum_tensor("num", [P, TPB, POS], F32))
        bank += [num[:, i, :] for i in range(4)]
        bank += [ctx.enter_context(nc.psum_tensor(f"bank{i}", [P, POS], F32)) for i in (6, 7)]
        bank = [b if i in (2, 3, 4, 5) else b[:, :] for i, b in enumerate(bank)]
        uv_bank, kv_bank, ks_bank, o_bank, t_bank = bank[0:2], bank[2:4], bank[4:6], bank[6], bank[7]
        z_bank = bank[0:2]

        ld_x = [sem(f"ld_x{n}") for n in range(NB)]
        ld_proj, ld_wk, ld_wq, ld_ctx, ld_wuv, ld_wv = map(sem, ("ld_proj", "ld_wk", "ld_wq", "ld_ctx", "ld_wuv", "ld_wv"))
        ld_small, ld_woa, ld_wo = map(sem, ("ld_small", "ld_woa", "ld_wo"))
        ld_moe = [sem("ld_moe_even"), sem("ld_moe_odd")]
        filled = sem("filled")
        waits_passed = sem("waits_passed")
        consts = sem("consts")
        stats_done = sem("stats_done")
        moments_done = sem("moments_done")
        ln1_step = sem("ln1_step")
        ctx_hi_done, ctx_lo_done = sem("ctx_hi_done"), sem("ctx_lo_done")
        wuv_hi_done, wuv_lo_done = sem("wuv_hi_done"), sem("wuv_lo_done")
        wk_full, wk_hi_done, wk_lo_done = sem("wk_full"), sem("wk_hi_done"), sem("wk_lo_done")
        wq_full, wq_hi_done, wq_lo_done = sem("wq_full"), sem("wq_hi_done"), sem("wq_lo_done")
        wv_split, woa_split, wo_split = sem("wv_split"), sem("woa_split"), sem("wo_split")
        xn_done = sem("xn_done")
        xnT_hi_done = sem("xnT_hi_done")
        uv_full, uv_evac = sem("uv_full"), sem("uv_evac")
        kv_full, kv_evac, kp_eps = sem("kv_full"), sem("kv_evac"), sem("kp_eps")
        ks_full, ks_hi_done, ks_free = sem("ks_full"), sem("ks_hi_done"), sem("ks_free")
        t_full, t_free = sem("t_full"), sem("t_free")
        conv_step, o_prod, o_hi_done, o_lo_done = sem("conv_step"), sem("o_prod"), sem("o_hi_done"), sem("o_lo_done")
        o_full, outT_done = sem("o_full"), sem("outT_done")
        ln2_stats, ln2_moments, ln2_step, y2_done, y2T_hi_done = map(sem, ("ln2_stats", "ln2_moments", "ln2_step", "y2_done", "y2T_hi_done"))
        z_full, q_hi_done, q_lo_done, num_done = map(sem, ("z_full", "q_hi_done", "q_lo_done", "num_done"))
        rden_done, att_done = sem("rden_done"), sem("att_done")
        tb_full, attT_hi_done, attT_lo_done, wo_done = map(sem, ("tb_full", "attT_hi_done", "attT_lo_done", "wo_done"))
        out2_done, x2_done = sem("out2_done"), sem("x2_done")
        ln3_stats, ln3_moments, ln3_step, y3_done, y3T_done = map(sem, ("ln3_stats", "ln3_moments", "ln3_step", "y3_done", "y3T_done"))
        logits_full, exp_done, rank_full = sem("logits_full"), sem("exp_done"), sem("rank_full")
        route = sem("route")
        dest_done, sent = sem("dest_done"), sem("sent")
        moe_hi_done, moe_split = sem("moe_hi_done"), sem("moe_split")
        table_step = sem("table_step")
        ld_xb = [sem(f"ld_xb{j}") for j in range(RING)]
        meta_done, tx_full, xT_hi_done, xT_lo_done = map(sem, ("meta_done", "tx_full", "xT_hi_done", "xT_lo_done"))
        gu_full, silu_done, hid_done = sem("gu_full"), sem("silu_done"), sem("hid_done")
        th_full, hT_hi_done, hT_lo_done = sem("th_full"), sem("hT_hi_done"), sem("hT_lo_done")
        dn_full, yo_done = sem("dn_full"), sem("yo_done")
        y_sent = [sem(f"y_sent{j}") for j in range(RING)]
        ld_y = [sem(f"ld_y{n}") for n in range(NB)]
        add_step = sem("add_step")
        stored = sem("stored")

        block = ctx.enter_context(nc.Block())

        def t_job(kind, n):
            order = [("xn", 0)]
            for m in range(1, NB):
                order += [("xn", m), ("out", m - 1), ("y2", m - 1)]
            order += [("out", NB - 1), ("y2", NB - 1)]
            return order.index((kind, n))

        def split_matmul(ps, a_hi, a_lo, b_hi, b_lo, start=True, stop=True):
            nc.tensor.matmul(ps, a_hi, b_hi, start=start, stop=False)
            nc.tensor.matmul(ps, a_hi, b_lo, start=False, stop=False)
            return nc.tensor.matmul(ps, a_lo, b_hi, start=False, stop=stop)

        def batch(t, n):
            return t[:, n, :] if isinstance(n, int) else t[:, bass.ds(n, 1), :].rearrange("p a c -> p (a c)")

        def tile_of(n, t):
            return X[:, TPB * n + t, :] if isinstance(n, int) else \
                X[:, bass.ds(n * TPB + t, 1), :].rearrange("p a c -> p (a c)")

        def tiles_of(n):
            return X[:, bass.ds(n * TPB, TPB), :].rearrange("p a c -> p (a c)")

        xs_blocks = xs.rearrange("(a p) c -> p a c", p=P)
        x_view = x.rearrange("n (t p) d -> n p t d", p=P)
        out_view = out.rearrange("n (t p) d -> n p t d", p=P)
        ys_view = ys.rearrange("(k n t p) d -> k n p t d", k=TOPK, n=NB, p=P)
        FILL_ROWS = xs_blocks.shape[1]

        CONSTS = 18
        ROUTE_STEPS = 24
        FILLS = 3 * 16
        TABLE_STEPS = 15
        LN1_STEPS = 12
        STEPS = 24
        TB_JOBS = CH + 2
        tx_bank, gu_bank, th_bank, dn_bank = bank[6:8], bank[0:2], bank[2:4], bank[4:6]

        def chunk_step(c):
            return G * (c // 2) + 7 + 2 * (c % 2)

        def wait_alone(eng, semaphore, value):
            eng.wait_ge(semaphore, value)
            eng.sem_inc(waits_passed, 1)

        def pipeline(eng, stages):
            depth = max(lag for lag, _ in stages)

            def tick(i, j):
                for lag, fn in stages:
                    s = i * RING + (j - lag)
                    if not isinstance(s, int) or 0 <= s < BLOCKS:
                        fn(s, (j - lag) % RING, i + (j - lag) // RING)
            for j in range(RING):
                tick(0, j)
            with eng.Fori(1, BLOCKS // RING) as i:
                for j in range(RING):
                    tick(i, j)
            for j in range(depth):
                tick(BLOCKS // RING, j)

        @block.sync
        def _(sp):
            sp.dma_start(projT_sb[:, :], projT).then_inc(ld_proj, 16)
            sp.dma_start(wT_sb[:, :, :], wkT).then_inc(ld_wk, 16)
            sp.dma_start(ctxT_sb[:, :], ctxT).then_inc(ld_ctx, 16)
            sp.dma_start(wuv_sb[:, :], wuv).then_inc(ld_wuv, 16)
            sp.dma_start(wvo_sb[:, :], wv).then_inc(ld_wv, 16)
            for dst, src in ((bias_v[:, :], bv), (bias_u[:, :], bu), (bias_o[:, :], bo), (coef_sb[:, :, :], coef)):
                sp.dma_start(dst, src).then_inc(ld_small, 16)
            sp.dma_start(router_sb[:, :], router).then_inc(ld_small, 16)
            sp.dma_start(woa_sb[:, :, :], woaT).then_inc(ld_woa, 16)
            sp.wait_ge(wk_full, NG)
            sp.dma_start(wT_sb[:, :, :], wqT).then_inc(ld_wq, 16)
            sp.wait_ge(consts, CONSTS)
            for a in range(0, FILL_ROWS, 43):
                sp.dma_start(xs_blocks[:, a:a + 43, :],
                             pad_row[:, :].unsqueeze(1).broadcast_to([P, 43, ROW])).then_inc(filled, 16)
            sp.wait_ge(wv_split, 2)
            sp.dma_start(wvo_sb[:, :].rearrange("p (c e) -> p c e", c=CH), wo).then_inc(ld_wo, 16)
            sp.wait_ge(wq_lo_done, NG)
            sp.wait_ge(wo_split, 2)
            sp.wait_ge(y2T_hi_done, NB)
            sp.wait_ge(t_free, 3 * NB)
            sp.wait_ge(o_full, NB)
            sp.wait_ge(ks_free, 2 * NG * NB)
            for e in range(E):
                if e >= 2:
                    sp.wait_ge(moe_split, 2 * (e - 1))
                sp.dma_start(wgu_raw[:, e % 2, :], wgu[:, e, :]).then_inc(ld_moe[e % 2], 16)
                sp.dma_start(wd_raw[:, e % 2, :], wd[:, e, :]).then_inc(ld_moe[e % 2], 16)
            sp.wait_ge(table_step, TABLE_STEPS)
            sp.wait_ge(sent, 16 * TOPK * TPB * NB)

            def load_block(s, j, reused):
                row = sp.value_load(table[0:1, 0, bass.ds(s, 1)], min_val=0, max_val=PAD_ROW)
                if reused:
                    sp.wait_ge(tx_full, s - RING + 1)
                    sp.wait_ge(meta_done, s - RING + 1)
                sp.dma_start(xb[:, j, :], xs[bass.ds(row, P), :]).then_inc(ld_xb[j], 16)

            for j in range(RING):
                load_block(j, j, False)
            with sp.Fori(1, BLOCKS // RING) as i:
                for j in range(RING):
                    load_block(i * RING + j, j, True)
            for j in range(RING):
                sp.wait_ge(y_sent[j], 16 * BLOCKS // RING)
            for n in range(NB):
                for k in range(TOPK):
                    sp.dma_start(y_back[:, k, n, :].rearrange("p (t c) -> p t c", t=TPB),
                                 ys_view[k, n, :, :, :]).then_inc(ld_y[n], 16)
            for n in range(NB):
                sp.wait_ge(add_step, 2 * (n + 1))
                sp.dma_start(out_view[n, :, :, :], X[:, TPB * n:TPB * (n + 1), :]).then_inc(stored, 16)
            sp.wait_ge(stored, 16 * NB)

        @block.gpsimd
        def _(pool):
            g = nc.gpsimd
            made = []

            def const(ins):
                ins.then_inc(consts, 1)
                made.append(ins)

            const(g.memset(ident[:, :], 0.0))
            const(g.memset(p_mhalf[:, :], -0.5))
            const(g.memset(p_half[:, :], 0.5))
            const(g.memset(p_mone[:, :], -1.0))
            const(g.memset(v_aug[:, :, :], 0.0))
            const(g.memset(pad_row[:, :], 0.0))
            const(g.memset(tri[:, :, :], 1.0))
            const(g.memset(before[:, :], 1.0))
            const(g.memset(ones_bf[:, :], 1.0))
            const(g.memset(mean_of_rows[:, :].bitcast(F32), 2.0 / P))
            const(g.memset(ones_r[:, :].bitcast(F32), 1.0))
            const(g.iota(dest[:, :, :, :], [[POS, NB], [TOKENS, TOPK], [P, TPB]], base=0, channel_multiplier=1))
            const(g.iota(iota_e[:, :], [[1, E]], base=0, channel_multiplier=0, allow_small_or_imprecise_dtypes=True))
            pool.wait_ge(consts, 13)
            const(g.affine_select(out=ident[:, :], in_=ident[:, :], compare_op=ALU.not_equal, fill=1.0,
                                  base=0, pattern=[[-1, P]], channel_multiplier=1))
            const(g.memset(v_aug[:, :, DH:DH + 1], 1.0))
            const(g.iota(pad_row[:, P:P + 1].bitcast(I32), [[1, 1]], base=NO_DEST, channel_multiplier=0))
            const(g.affine_select(out=tri[:, :, :], in_=tri[:, :, :], compare_op=ALU.is_ge, fill=0.0,
                                  base=0, pattern=[[1, E], [-1, E]], channel_multiplier=0))
            const(g.affine_select(out=before[:, :], in_=before[:, :], compare_op=ALU.is_gt, fill=0.0,
                                  base=0, pattern=[[1, P]], channel_multiplier=-1))
            assert len(made) == CONSTS
            g.iota(seq[:, :], [[P, BLOCKS]], base=-PAD_ROW, channel_multiplier=0,
                   allow_small_or_imprecise_dtypes=True).then_inc(ln1_step, 1)
            g.iota(base[:, :], [[CAP, E]], base=0, channel_multiplier=0,
                   allow_small_or_imprecise_dtypes=True).then_inc(ln1_step, 1)

            mean, var = moments[:, :, 0], moments[:, :, 1]
            pool.wait_ge(moments_done, TILES)
            steps = [
                lambda: g.tensor_scalar(ln1[:, V_EPS, :], var, LN_EPS, None, ALU.add),
                lambda: g.tensor_tensor(ln1[:, STD, :], var, p_half[:, :], ALU.pow),
                lambda: g.tensor_tensor(ln1[:, RSTD, :], ln1[:, V_EPS, :], p_mhalf[:, :], ALU.pow),
                lambda: g.tensor_tensor(ln1[:, RMS, :], ln1[:, STD, :], ln1[:, RSTD, :], ALU.mult),
                lambda: g.tensor_scalar(ln1[:, STD, :], ln1[:, RMS, :], RMS_EPS, None, ALU.add),
                lambda: g.tensor_tensor(ln1[:, INV, :], ln1[:, STD, :], p_mone[:, :], ALU.pow),
                lambda: g.tensor_tensor(ln1[:, SCALE, :], ln1[:, INV, :], ln1[:, RSTD, :], ALU.mult),
                lambda: g.tensor_scalar(ln1[:, ONE_RSTD, :], ln1[:, RSTD, :], 1.0, None, ALU.add),
                lambda: g.tensor_tensor(ln1[:, NEG_SHIFT, :], mean, ln1[:, RSTD, :], ALU.mult),
                lambda: g.tensor_scalar(ln1[:, SHIFT, :], ln1[:, NEG_SHIFT, :], -1.0, None, ALU.mult),
            ]
            assert len(steps) == LN1_STEPS - 2
            for i, step in enumerate(steps):
                pool.wait_ge(ln1_step, 2 + i)
                step().then_inc(ln1_step, 1)

            def split(dst_hi, dst_lo, src, done, count):
                g.tensor_copy(dst_hi, src).then_inc(done, 1)
                pool.wait_ge(done, count + 1)
                g.tensor_tensor(dst_lo, src, dst_hi, ALU.subtract).then_inc(done, 1)

            pool.wait_ge(ld_wv, 16)
            split(wv_hi[:, :], wv_lo[:, :], wvo_sb[:, :], wv_split, 0)
            pool.wait_ge(ld_woa, 16)
            split(woa_hi[:, :, :], woa_lo[:, :, :], woa_sb[:, :, :], woa_split, 0)

            def ln_rstd(var_ap, step_sem, count):
                g.tensor_scalar(var_eps[:, :], var_ap, LN_EPS, None, ALU.add).then_inc(step_sem, 1)
                pool.wait_ge(step_sem, count + 1)
                g.tensor_tensor(rstd[:, :], var_eps[:, :], p_mhalf[:, 0:TPB], ALU.pow).then_inc(step_sem, 1)

            def ln2(n):
                pool.wait_ge(ln2_moments, TPB * (n + 1))
                ln_rstd(moments_b[:, :, 1], ln2_step, 2 * n)

            for n in range(NB):
                for i in range(NG):
                    pool.wait_ge(kv_evac, 6 * n + i + 1)
                    part = kp[:, POS * i:POS * (i + 1)]
                    g.tensor_scalar(part, part, RELU_EPS, None, ALU.add).then_inc(kp_eps, 1)
                if n:
                    ln2(n - 1)
            ln2(NB - 1)
            pool.wait_ge(ld_wo, 16)
            split(wo_hi[:, :, :], wo_lo[:, :, :], wvo_sb[:, :].rearrange("p (c e) -> p c e", c=CH), wo_split, 0)
            for e in range(E):
                pool.wait_ge(ld_moe[e % 2], 32 * (e // 2 + 1))
                g.tensor_copy(wgu_hi[:, e, :], wgu_raw[:, e % 2, :]).then_inc(moe_hi_done, 1)
                g.tensor_copy(wd_hi[:, e, :], wd_raw[:, e % 2, :]).then_inc(moe_hi_done, 1)
                pool.wait_ge(moe_hi_done, 2 * e + 2)
                g.tensor_tensor(wgu_lo[:, e, :], wgu_raw[:, e % 2, :], wgu_hi[:, e, :], ALU.subtract).then_inc(moe_split, 1)
                g.tensor_tensor(wd_lo[:, e, :], wd_raw[:, e % 2, :], wd_hi[:, e, :], ALU.subtract).then_inc(moe_split, 1)
            pool.wait_ge(filled, FILLS)
            with pool.Fori(0, NB) as n:
                wait_alone(pool, ln3_moments, n * TPB + TPB)
                g.tensor_scalar(var_eps[:, :], moments_b[:, :, 1], LN_EPS, None, ALU.add).then_inc(ln3_step, 1)
                pool.wait_ge(ln3_step, n * 2 + 1)
                g.tensor_tensor(rstd[:, :], var_eps[:, :], p_mhalf[:, 0:TPB], ALU.pow).then_inc(ln3_step, 1)
                wait_alone(pool, y3_done, n * 8 + 8)
                g.tensor_copy(rows[:, :, :, P].bitcast(I32),
                              dest[:, bass.ds(n, 1), :, :].rearrange("p a k t -> p (a k) t")).then_inc(dest_done, 1)
                pool.wait_ge(dest_done, n + 1)
                wait_alone(pool, route, n * ROUTE_STEPS + ROUTE_STEPS + 1)
                for t in range(TPB):
                    for k in range(TOPK):
                        g.indirect_dma_start(
                            out=xs, out_offset=bass.IndirectOffsetOnAxis(ap=slot_i[:, t, k:k + 1], axis=0),
                            in_=rows[:, k, t, :], in_offset=None).then_inc(sent, 16)
                wait_alone(pool, sent, n * 16 * TOPK * TPB + 16 * TOPK * TPB)

            def take_meta(s, j, turn):
                wait_alone(pool, ld_xb[j], turn * 16 + 16)
                if not isinstance(s, int):
                    wait_alone(pool, y_sent[j], turn * 16)
                g.tensor_copy(meta[:, j, :], xb[:, j, P:P + 2].bitcast(I32)).then_inc(meta_done, 1)

            def send(s, j, turn):
                wait_alone(pool, yo_done, s + 1)
                g.indirect_dma_start(
                    out=ys, out_offset=bass.IndirectOffsetOnAxis(ap=meta[:, j, 0:1], axis=0),
                    in_=yo[:, j, :], in_offset=None, bounds_check=NO_DEST - 1, oob_is_err=False).then_inc(y_sent[j], 16)

            pipeline(pool, [(0, take_meta), (3, send)])

        @block.scalar
        def _(act):
            a = nc.scalar
            for n in range(NB):
                act.dma_start(X[:, TPB * n:TPB * (n + 1), :], x_view[n, :, :, :]).then_inc(ld_x[n], 16)
            a.preload_act_table(ACT.Silu)

            def copy(dst, src, **kw):
                return a.activation(dst, src, ACT.Copy, **kw)

            for g in range(NG):
                act.wait_ge(wk_full, g + 1)
                copy(wkp_hi[:, POS * g:POS * (g + 1)], uv_bank[g % 2], scale=RATIO).then_inc(wk_hi_done, 1)
            act.wait_ge(ld_ctx, 16)
            copy(ctxT_hi[:, :], ctxT_sb[:, :]).then_inc(ctx_hi_done, 1)
            act.wait_ge(ld_wuv, 16)
            copy(wuv_hi[:, :], wuv_sb[:, :]).then_inc(wuv_hi_done, 1)
            act.wait_ge(ld_small, 16 * 5)
            act.wait_ge(consts, CONSTS)

            def y2T_high(n):
                act.wait_ge(t_full, t_job("y2", n) + 1)
                copy(y2T_hi[:, n, :], t_bank).then_inc(y2T_hi_done, 1)

            for n in range(NB):
                for i in range(NG):
                    act.wait_ge(kv_full, 6 * n + i + 1)
                    if n:
                        act.wait_ge(ks_full, 2 * NG * (n - 1) + i + 1)
                    a.activation(kp[:, POS * i:POS * (i + 1)], kv_bank[i % 2][0:CTX, :], ACT.Relu).then_inc(kv_evac, 1)
                act.wait_ge(t_full, t_job("xn", n) + 1)
                if n:
                    act.wait_ge(uv_full, 4 * n)
                copy(xnT_hi[:, :], t_bank).then_inc(xnT_hi_done, 1)
                for i in range(4):
                    act.wait_ge(uv_full, 4 * n + i + 1)
                    if n and i == 2:
                        act.wait_ge(o_prod, n)
                    dst, bias = (v_hist[:, n, i, :], bias_v) if i < 2 else (u_sb[:, i - 2, :], bias_u)
                    a.activation(dst, uv_bank[i % 2], ACT.Silu, bias=bias[:, i % 2:i % 2 + 1]).then_inc(uv_evac, 1)
                for i in range(2):
                    act.wait_ge(kv_full, 6 * n + 4 + i + 1)
                    if n:
                        act.wait_ge(ks_full, 2 * NG * (n - 1) + NG)
                    copy(v_aug[:, 8 * i:8 * i + 8, 0:DH],
                         kv_bank[i % 2][0:CTX, :].rearrange("p (h d) -> p h d", h=8)).then_inc(kv_evac, 1)

                def kvs_high(g):
                    act.wait_ge(ks_full, 2 * NG * n + g + 1)
                    copy(kvs_hi[:, n, G * HA * g:G * HA * (g + 1)], ks_bank[g % 2][:, 0:G * HA]).then_inc(ks_hi_done, 1)
                kvs_high(0)
                kvs_high(1)
                act.wait_ge(o_prod, n + 1)
                if n:
                    act.wait_ge(o_full, n)
                copy(o_hi[:, :, :], acc[:, :, :]).then_inc(o_hi_done, 1)
                if n:
                    y2T_high(n - 1)
                kvs_high(2)
                kvs_high(3)
                act.wait_ge(o_full, n + 1)
                if n:
                    act.wait_ge(t_full, t_job("out", n - 1) + 1)
                a.activation(outT[:, :], o_bank, ACT.Identity, bias=bias_o[:, 0:1]).then_inc(outT_done, 1)
                for g in range(NG):
                    act.wait_ge(ks_full, 2 * NG * n + NG + g + 1)
                    copy(kbias[:, n, G * HA * g:G * HA * (g + 1)], ks_bank[g % 2][:, 0:G * HA],
                         scale=RELU_EPS).then_inc(ks_hi_done, 1)
            for g in range(NG):
                if g == 2:
                    y2T_high(NB - 1)
                act.wait_ge(wq_full, g + 1)
                copy(wqp_hi[:, G * g:G * (g + 1), :].rearrange("p h m -> p (h m)"), uv_bank[g % 2],
                     scale=RATIO).then_inc(wq_hi_done, 1)

            a.preload_act_table(ACT.Exp)
            act.wait_ge(t_free, 3 * NB)
            act.wait_ge(ks_free, 2 * NG * NB)
            act.wait_ge(wq_lo_done, NG)
            with act.Fori(0, NB) as n:
                for k in range(STEPS):
                    if k < H:
                        act.wait_ge(z_full, n * H + k + 1)
                        if k >= 3:
                            act.wait_ge(num_done, n * H + k - 2)
                        a.activation(q_hi[:, k % 3, :], z_bank[k % 2], ACT.Relu).then_inc(q_hi_done, 1)
                    for c in range(CH):
                        if k == chunk_step(c):
                            act.wait_ge(tb_full, n * TB_JOBS + c + 1)
                            if c >= 2:
                                act.wait_ge(wo_done, n * CH + c - 1)
                            copy(attT_hi[:, c % 2, :], t_bank).then_inc(attT_hi_done, 1)
                act.wait_ge(wo_done, n * CH + CH)
                copy(outT[:, :], o_bank).then_inc(out2_done, 1)
                act.wait_ge(tb_full, n * TB_JOBS + CH + 2)
                copy(y3T[:, :], t_bank).then_inc(y3T_done, 1)
                act.wait_ge(route, n * ROUTE_STEPS + 3)
                a.activation(l_exp[:, :, :], l_sub[:, :, :], ACT.Exp).then_inc(exp_done, 1)

            a.preload_act_table(ACT.Silu)

            def x_high(s, j, turn):
                act.wait_ge(tx_full, s + 1)
                copy(xT_hi[:, j, :], tx_bank[j % 2][:, 0:P]).then_inc(xT_hi_done, 1)

            def gate(s, j, turn):
                act.wait_ge(gu_full, s + 1)
                a.activation(silu_g[:, j % 2, :], gu_bank[j % 2][:, 0:HID], ACT.Silu).then_inc(silu_done, 1)

            def h_high(s, j, turn):
                act.wait_ge(th_full, s + 1)
                copy(hT_hi[:, j % 2, :], th_bank[j % 2][:, 0:HID]).then_inc(hT_hi_done, 1)

            def weigh(s, j, turn):
                act.wait_ge(dn_full, s + 1)
                act.wait_ge(meta_done, s + 1)
                a.activation(yo[:, j, :], dn_bank[j % 2][:, 0:P], ACT.Copy,
                             scale=meta[:, j, 1:2].bitcast(F32)).then_inc(yo_done, 1)

            pipeline(act, [(0, x_high), (1, gate), (2, h_high), (3, weigh)])

        @block.vector
        def _(dve):
            v = nc.vector

            def lo(dst, src, hi, scale=1.0, op=ALU.mult):
                return v.scalar_tensor_tensor(dst, src, scale, hi, op, ALU.subtract)

            for n in range(NB):
                dve.wait_ge(ld_x[n], 16)
                for t in range(TPB * n, TPB * (n + 1)):
                    v.bn_stats(stats[:, t, :], X[:, t, :]).then_inc(stats_done, 1)
            for t in range(TILES):
                if t == 0:
                    dve.wait_ge(stats_done, TILES)
                v.bn_aggr(moments[:, t, :], stats[:, t, :]).then_inc(moments_done, 1)
            for g in range(NG):
                dve.wait_ge(wk_hi_done, g + 1)
                part = slice(POS * g, POS * (g + 1))
                lo(wkp_lo[:, part], uv_bank[g % 2], wkp_hi[:, part], RATIO).then_inc(wk_lo_done, 1)
            dve.wait_ge(ctx_hi_done, 1)
            lo(ctxT_lo[:, :], ctxT_sb[:, :], ctxT_hi[:, :]).then_inc(ctx_lo_done, 1)
            dve.wait_ge(wuv_hi_done, 1)
            lo(wuv_lo[:, :], wuv_sb[:, :], wuv_hi[:, :]).then_inc(wuv_lo_done, 1)

            def normalise(n):
                for t in range(TPB):
                    i = TPB * n + t
                    v.tensor_scalar(xn[:, t, :], X[:, i, :], moments[:, i, 0:1], ln1[:, SCALE, i:i + 1],
                                    ALU.subtract, ALU.mult).then_inc(xn_done, 1)

            dve.wait_ge(ln1_step, LN1_STEPS)
            normalise(0)
            steps = [0]

            def conv(ins):
                steps[0] += 1
                ins.then_inc(conv_step, 1)

            def residual(n):
                dve.wait_ge(t_full, t_job("out", n) + 1)
                dve.wait_ge(xn_done, min(TPB * (2 * n + 3), 2 * TILES))
                part = X[:, TPB * n:TPB * (n + 1), :].rearrange("p t c -> p (t c)")
                v.tensor_tensor(part, part, t_bank, ALU.add).then_inc(t_free, 1)
                dve.wait_ge(t_free, t_job("out", n) + 1)
                for t in range(TPB):
                    v.bn_stats(stats[:, t, :], X[:, TPB * n + t, :]).then_inc(ln2_stats, 1)
                dve.wait_ge(ln2_stats, TPB * (n + 1))
                for t in range(TPB):
                    v.bn_aggr(moments_b[:, t, :], stats[:, t, :]).then_inc(ln2_moments, 1)

            def second_norm(n):
                dve.wait_ge(ln2_step, 2 * (n + 1))
                for t in range(TPB):
                    v.tensor_scalar(y2[:, t, :], X[:, TPB * n + t, :], moments_b[:, t, 0:1], rstd[:, t:t + 1],
                                    ALU.subtract, ALU.mult).then_inc(y2_done, 1)

            def y2T_low(n):
                dve.wait_ge(y2T_hi_done, n + 1)
                lo(y2T_lo[:, n, :], t_bank, y2T_hi[:, n, :]).then_inc(t_free, 1)

            for n in range(NB):
                dve.wait_ge(xnT_hi_done, n + 1)
                lo(xnT_lo[:, :], t_bank, xnT_hi[:, :]).then_inc(t_free, 1)
                if n + 1 < NB:
                    normalise(n + 1)
                for t in range(TPB):
                    i = TPB * n + t
                    v.tensor_scalar(X[:, i, :], X[:, i, :], ln1[:, ONE_RSTD, i:i + 1], ln1[:, SHIFT, i:i + 1],
                                    ALU.mult, ALU.add).then_inc(xn_done, 1)
                dve.wait_ge(uv_evac, 4 * n + 2)
                if n:
                    dve.wait_ge(o_hi_done, n)
                for j in range(2):
                    conv(v.tensor_scalar(acc[:, j, :], v_hist[:, n, j, :], coef_sb[:, j, 0:1], None, ALU.mult))
                for m in range(1, n + 1):
                    for j in range(2):
                        dve.wait_ge(conv_step, steps[0] - 1)
                        conv(v.scalar_tensor_tensor(acc[:, j, :], v_hist[:, n - m, j, :], coef_sb[:, j, m:m + 1],
                                                    acc[:, j, :], ALU.mult, ALU.add))
                dve.wait_ge(uv_evac, 4 * n + 4)
                dve.wait_ge(conv_step, steps[0])
                v.tensor_tensor(acc[:, :, :], acc[:, :, :], u_sb[:, :, :], ALU.mult).then_inc(o_prod, 1)
                dve.wait_ge(o_hi_done, n + 1)
                v.tensor_tensor(o_lo[:, :, :], acc[:, :, :], o_hi[:, :, :], ALU.subtract).then_inc(o_lo_done, 1)

                def kvs_low(g):
                    dve.wait_ge(ks_hi_done, 2 * NG * n + g + 1)
                    part = slice(G * HA * g, G * HA * (g + 1))
                    lo(kvs_lo[:, n, part], ks_bank[g % 2][:, 0:G * HA], kvs_hi[:, n, part]).then_inc(ks_free, 1)
                if n:
                    residual(n - 1)
                kvs_low(0)
                kvs_low(1)
                if n:
                    second_norm(n - 1)
                kvs_low(2)
                if n:
                    y2T_low(n - 1)
                kvs_low(3)
                for g in range(NG):
                    dve.wait_ge(ks_hi_done, 2 * NG * n + NG + g + 1)
                    part = kbias[P // 2:P, n, G * HA * g:G * HA * (g + 1)]
                    lo(part, ks_bank[g % 2][P // 2:P, 0:G * HA], part, RELU_EPS).then_inc(ks_free, 1)

            def wq_low(g):
                dve.wait_ge(wq_hi_done, g + 1)
                lo(wqp_lo[:, G * g:G * (g + 1), :].rearrange("p h m -> p (h m)"), uv_bank[g % 2],
                   wqp_hi[:, G * g:G * (g + 1), :].rearrange("p h m -> p (h m)"), RATIO).then_inc(wq_lo_done, 1)
            residual(NB - 1)
            wq_low(0)
            wq_low(1)
            second_norm(NB - 1)
            y2T_low(NB - 1)
            wq_low(2)
            wq_low(3)

            v.memset(l_max[:, :], 0.0).then_inc(route, 1)
            with dve.Fori(0, NB) as n:
                for k in range(STEPS):
                    if k < H:
                        dve.wait_ge(q_hi_done, n * H + k + 1)
                        v.scalar_tensor_tensor(q_lo[:, k % 3, :], z_bank[k % 2], 0.0, q_hi[:, k % 3, :],
                                               ALU.max, ALU.subtract).then_inc(q_lo_done, 1)
                    g = (k - 5) // G
                    if (k - 5) % G == 0 and 0 <= g < NG:
                        dve.wait_ge(num_done, n * H + G * (g + 1))
                        if g >= 2:
                            dve.wait_ge(tb_full, n * TB_JOBS + 2 * (g - 1))
                        groups = num[:, :, 0:G * HA].rearrange("p t (h c) -> p t h c", h=G)
                        v.reciprocal(rden[:, :, :], groups[:, :, :, DH]).then_inc(rden_done, 1)
                        dve.wait_ge(rden_done, n * NG + g + 1)
                        for t in range(TPB):
                            v.tensor_tensor(att[:, g % 2, t, :].rearrange("p (h c) -> p h c", h=G),
                                            groups[:, t, :, 0:DH],
                                            rden[:, t, :].unsqueeze(2).broadcast_to([P, G, DH]),
                                            ALU.mult).then_inc(att_done, 1)
                    for c in range(CH):
                        if k == chunk_step(c):
                            dve.wait_ge(attT_hi_done, n * CH + c + 1)
                            lo(attT_lo[:, c % 2, :], t_bank, attT_hi[:, c % 2, :]).then_inc(attT_lo_done, 1)
                dve.wait_ge(tb_full, n * TB_JOBS + CH + 1)
                v.tensor_tensor(tiles_of(n), tiles_of(n), t_bank, ALU.add).then_inc(x2_done, 1)
                wait_alone(dve, x2_done, n + 1)
                for t in range(TPB):
                    v.bn_stats(stats[:, t, :], tile_of(n, t)).then_inc(ln3_stats, 1)
                wait_alone(dve, ln3_stats, n * TPB + TPB)
                for t in range(TPB):
                    v.bn_aggr(moments_b[:, t, :], stats[:, t, :]).then_inc(ln3_moments, 1)
                dve.wait_ge(ln3_step, n * 2 + 2)
                for t in range(TPB):
                    for k in range(TOPK):
                        v.tensor_scalar(rows[:, k, t, 0:P], tile_of(n, t), moments_b[:, t, 0:1], rstd[:, t:t + 1],
                                        ALU.subtract, ALU.mult).then_inc(y3_done, 1)
                count = [0]

                def step(ins, wait=True):
                    count[0] += 1
                    ins.then_inc(route, 1)
                    if wait:
                        wait_alone(dve, route, n * ROUTE_STEPS + count[0] + 1)

                def over(ap, dim, shape):
                    return ap.unsqueeze(dim).broadcast_to(shape)
                logits = o_bank[:, 0:TPB * E].rearrange("p (t e) -> p t e", e=E)
                rank = o_bank[:, 64:64 + TPB * E].rearrange("p (t e) -> p t e", e=E)
                total = o_bank[:, 128:128 + E]
                dve.wait_ge(logits_full, n + 1)
                step(v.tensor_reduce(l_max[:, :], logits, AX.X, ALU.max))
                step(v.tensor_tensor(l_sub[:, :, :], logits, over(l_max[:, :], 2, [P, TPB, E]), ALU.subtract), False)
                dve.wait_ge(exp_done, n + 1)
                step(v.tensor_reduce(l_sum[:, :], l_exp[:, :, :], AX.X, ALU.add))
                step(v.reciprocal(l_sum[:, :], l_sum[:, :]))
                step(v.tensor_tensor(prob[:, :, :], l_exp[:, :, :], over(l_sum[:, :], 2, [P, TPB, E]), ALU.mult))
                for t in range(TPB):
                    step(v.max(top_v[:, t, :], prob[:, t, :]), t == TPB - 1)
                for t in range(TPB):
                    step(v.max_index(top_i[:, t, :], top_v[:, t, :], prob[:, t, :]), t == TPB - 1)
                step(v.tensor_copy(top_f[:, :, :], top_i[:, :, 0:TOPK]))
                step(v.tensor_tensor(chosen[:, :, :, :], over(top_f[:, :, :], 3, [P, TPB, TOPK, E]),
                                     iota_e[:, :].unsqueeze(1).unsqueeze(1).broadcast_to([P, TPB, TOPK, E]), ALU.is_equal))
                step(v.tensor_tensor(taken[:, :, :], chosen[:, :, 0, :], chosen[:, :, 1, :], ALU.add), False)
                step(v.tensor_tensor(w_sum[:, :], top_v[:, :, 0], top_v[:, :, 1], ALU.add))
                step(v.reciprocal(w_sum[:, :], w_sum[:, :]))
                step(v.tensor_tensor(rows[:, :, :, P + 1].rearrange("p k t -> p t k"), top_v[:, :, 0:TOPK],
                                     over(w_sum[:, :], 2, [P, TPB, TOPK]), ALU.mult), False)
                dve.wait_ge(rank_full, n + 1)
                step(v.tensor_tensor(slot_e[:, :, :], rank, over(base[:, :], 1, [P, TPB, E]), ALU.add))
                step(v.tensor_tensor(base[:, :], base[:, :], total, ALU.add), False)
                step(v.tensor_tensor(slot_k[:, :, :, :], chosen[:, :, :, :], over(slot_e[:, :, :], 2, [P, TPB, TOPK, E]), ALU.mult))
                step(v.tensor_reduce(slot_f[:, :, :], slot_k[:, :, :, :], AX.X, ALU.add))
                step(v.tensor_copy(slot_i[:, :, :], slot_f[:, :, :]), False)
                assert count[0] == ROUTE_STEPS, count[0]

            tcount = [0]

            def tstep(ins):
                tcount[0] += 1
                ins.then_inc(table_step, 1)
                dve.wait_ge(table_step, tcount[0])
            dve.wait_ge(route, NB * ROUTE_STEPS + 1)
            o = slice(0, 1)
            sh = [1, BLOCKS, E]
            tstep(v.scalar_tensor_tensor(t_val[o, :], iota_e[o, :], -float(CAP), base[o, :], ALU.mult, ALU.add))
            tstep(v.tensor_scalar(t_cnt[o, :], t_val[o, :], float(P - 1), None, ALU.add))
            tstep(v.tensor_scalar(t_cnt[o, :], t_cnt[o, :], 7, None, ALU.arith_shift_right))
            tstep(v.tensor_copy(t_nb[o, :], t_cnt[o, :]))
            tstep(v.tensor_tensor(t_prod[o, :, :], tri[o, :, :], t_nb[o, :].unsqueeze(1).broadcast_to([1, E, E]), ALU.mult))
            tstep(v.tensor_reduce(t_end[o, :], t_prod[o, :, :], AX.X, ALU.add))
            tstep(v.tensor_tensor(t_start[o, :], t_end[o, :], t_nb[o, :], ALU.subtract))
            tstep(v.tensor_scalar(t_val[o, :], t_start[o, :], -float(P), None, ALU.mult))
            tstep(v.scalar_tensor_tensor(t_val[o, :], iota_e[o, :], float(CAP), t_val[o, :], ALU.mult, ALU.add))
            tstep(v.tensor_scalar(t_sum[o, 0, 0:E], t_start[o, :], float(P), -float(PAD_ROW), ALU.mult, ALU.add))
            tstep(v.tensor_scalar(t_sum[o, 1, 0:E], t_end[o, :], float(P), -float(PAD_ROW), ALU.mult, ALU.add))
            for i in range(2):
                v.tensor_tensor(t_ge[o, i, :, :], seq[o, :].unsqueeze(2).broadcast_to(sh),
                                t_sum[o, i, 0:E].unsqueeze(1).broadcast_to(sh), ALU.is_ge).then_inc(rden_done, 1)
            dve.wait_ge(rden_done, NB * NG + 2)
            tstep(v.tensor_tensor(t_oh[o, :, :], t_ge[o, 0, :, :], t_ge[o, 1, :, :], ALU.subtract))
            v.tensor_tensor(t_mul[o, 0, :, :], t_oh[o, :, :], t_val[o, :].unsqueeze(1).broadcast_to(sh), ALU.mult).then_inc(rden_done, 1)
            v.tensor_tensor(t_mul[o, 1, :, :], t_oh[o, :, :], iota_e[o, :].unsqueeze(1).broadcast_to(sh), ALU.mult).then_inc(rden_done, 1)
            v.tensor_reduce(t_sum[o, 0, :], t_oh[o, :, :], AX.X, ALU.add).then_inc(rden_done, 1)
            dve.wait_ge(rden_done, NB * NG + 5)
            tstep(v.tensor_reduce(t_sum[o, 1:3, :], t_mul[o, :, :, :], AX.X, ALU.add))
            v.tensor_tensor(t_sum[o, 0, :], t_sum[o, 0, :], seq[o, :], ALU.mult).then_inc(rden_done, 1)
            dve.wait_ge(rden_done, NB * NG + 6)
            v.tensor_tensor(t_sum[o, 1, :], t_sum[o, 1, :], t_sum[o, 0, :], ALU.add).then_inc(rden_done, 1)
            dve.wait_ge(rden_done, NB * NG + 7)
            tstep(v.tensor_scalar(table[o, 0, :], t_sum[o, 1, :], float(PAD_ROW), None, ALU.add))
            tstep(v.tensor_copy(table[o, 1, :], t_sum[o, 2, :]))
            assert tcount[0] == TABLE_STEPS, tcount[0]

            def x_low(s, j, turn):
                dve.wait_ge(xT_hi_done, s + 1)
                lo(xT_lo[:, j, :], tx_bank[j % 2][:, 0:P], xT_hi[:, j, :]).then_inc(xT_lo_done, 1)

            def hidden(s, j, turn):
                dve.wait_ge(silu_done, s + 1)
                v.tensor_tensor(hid[:, j % 2, :], gu_bank[j % 2][:, HID:2 * HID], silu_g[:, j % 2, :], ALU.mult).then_inc(hid_done, 1)

            def h_low(s, j, turn):
                dve.wait_ge(hT_hi_done, s + 1)
                lo(hT_lo[:, j % 2, :], th_bank[j % 2][:, 0:HID], hT_hi[:, j % 2, :]).then_inc(hT_lo_done, 1)

            pipeline(dve, [(0, x_low), (1, hidden), (2, h_low)])
            for n in range(NB):
                dve.wait_ge(ld_y[n], 16 * TOPK)
                part = X[:, TPB * n:TPB * (n + 1), :].rearrange("p t c -> p (t c)")
                for k in range(TOPK):
                    v.tensor_tensor(part, part, y_back[:, k, n, :], ALU.add).then_inc(add_step, 1)
                    if k == 0:
                        dve.wait_ge(add_step, 2 * n + 1)

        @block.tensor
        def _(pe):
            def transposes(dst, srcs):
                for i, src in enumerate(srcs):
                    last = nc.tensor.transpose(dst[:, P * i:P * (i + 1)], src, ident[:, :])
                return last

            pe.wait_ge(ld_proj, 16)
            pe.wait_ge(ld_wk, 16)

            def project(w, g):
                for h in range(G * g, G * (g + 1)):
                    last = nc.tensor.matmul(uv_bank[g % 2][:, M * (h % G):M * (h % G + 1)], w[:, h, :], projT_sb[:, :],
                                            start=True, stop=True)
                return last
            for g in range(NG):
                if g >= 2:
                    pe.wait_ge(wk_lo_done, g - 1)
                project(wT_sb, g).then_inc(wk_full, 1)

            def turn(kind, n):
                if t_job(kind, n):
                    pe.wait_ge(t_free, t_job(kind, n))

            def out_back(n):
                pe.wait_ge(outT_done, n + 1)
                turn("out", n)
                transposes(t_bank, [outT[:, P * t:P * (t + 1)] for t in range(TPB)]).then_inc(t_full, 1)

            def y2_back(n):
                pe.wait_ge(y2_done, TPB * (n + 1))
                turn("y2", n)
                transposes(t_bank, [y2[:, t, :] for t in range(TPB)]).then_inc(t_full, 1)

            def kv_turn(n, i):
                job = 6 * n + i
                if job >= 2:
                    pe.wait_ge(kv_evac, job - 1)

            for n in range(NB):
                c_hi, c_lo = (c[:, CTX * n:CTX * (n + 1)] for c in (ctxT_hi, ctxT_lo))
                if n == 0:
                    pe.wait_ge(ctx_lo_done, 1)
                for i in range(NG):
                    if n == 0:
                        pe.wait_ge(wk_lo_done, i + 1)
                    kv_turn(n, i)
                    part = slice(POS * i, POS * (i + 1))
                    split_matmul(kv_bank[i % 2][0:CTX, :], c_hi, c_lo, wkp_hi[:, part], wkp_lo[:, part]).then_inc(kv_full, 1)
                if n == 0:
                    pe.wait_ge(consts, CONSTS)
                    pe.wait_ge(xn_done, TPB)
                else:
                    pe.wait_ge(xn_done, 2 * TPB * n)
                turn("xn", n)
                transposes(t_bank, [xn[:, t, :] for t in range(TPB)]).then_inc(t_full, 1)
                if n == 0:
                    pe.wait_ge(wuv_lo_done, 1)
                pe.wait_ge(t_free, t_job("xn", n) + 1)
                for i in range(4):
                    if 4 * n + i >= 2:
                        pe.wait_ge(uv_evac, 4 * n + i - 1)
                    w = slice(P * ((i + 2) % 4), P * ((i + 2) % 4 + 1))
                    split_matmul(uv_bank[i % 2], wuv_hi[:, w], wuv_lo[:, w], xnT_hi[:, :], xnT_lo[:, :]).then_inc(uv_full, 1)
                if n:
                    out_back(n - 1)
                for i in range(2):
                    if n == 0:
                        pe.wait_ge(wv_split, 2)
                    kv_turn(n, 4 + i)
                    part = slice(POS * i, POS * (i + 1))
                    split_matmul(kv_bank[i % 2][0:CTX, :], c_hi, c_lo, wv_hi[:, part], wv_lo[:, part]).then_inc(kv_full, 1)

                def kvs(g):
                    job = 2 * NG * n + g
                    if job >= 2:
                        pe.wait_ge(ks_free, job - 1)
                    pe.wait_ge(kp_eps, NG * n + g + 1)
                    pe.wait_ge(kv_evac, 6 * n + 5 + g // 2)
                    for h in range(G * g, G * (g + 1)):
                        last = nc.tensor.matmul(ks_bank[g % 2][:, HA * (h % G):HA * (h % G + 1)],
                                                kp[:, M * h:M * (h + 1)], v_aug[:, h, :], start=True, stop=True)
                    last.then_inc(ks_full, 1)
                kvs(0)
                kvs(1)
                if n:
                    y2_back(n - 1)
                kvs(2)
                kvs(3)
                pe.wait_ge(o_lo_done, n + 1)
                if n == 0:
                    pe.wait_ge(woa_split, 2)
                else:
                    pe.wait_ge(outT_done, n)
                for j in range(2):
                    last = split_matmul(o_bank, woa_hi[:, j, :], woa_lo[:, j, :], o_hi[:, j, :], o_lo[:, j, :],
                                        start=j == 0, stop=j == 1)
                last.then_inc(o_full, 1)
                for g in range(NG):
                    pe.wait_ge(ks_free, 2 * NG * n + NG + g - 1)
                    part = slice(G * HA * g, G * HA * (g + 1))
                    ps = ks_bank[g % 2][:, 0:G * HA]
                    nc.tensor.matmul(ps, ones_r[:, :], kvs_hi[:, n, part], start=True, stop=False)
                    nc.tensor.matmul(ps, ones_r[:, :], kvs_lo[:, n, part], start=False, stop=True).then_inc(ks_full, 1)
            out_back(NB - 1)
            pe.wait_ge(ld_wq, 16)
            pe.wait_ge(uv_evac, 4 * NB)
            for g in range(NG):
                if g == 2:
                    y2_back(NB - 1)
                if g >= 2:
                    pe.wait_ge(wq_lo_done, g - 1)
                project(wT_sb, g).then_inc(wq_full, 1)

            pe.wait_ge(wq_lo_done, NG)
            pe.wait_ge(t_free, 3 * NB)
            pe.wait_ge(ks_free, 2 * NG * NB)
            pe.wait_ge(outT_done, NB)
            pe.wait_ge(wo_split, 2)
            with pe.Fori(0, NB) as n:
                def features(h):
                    if h >= 2:
                        pe.wait_ge(q_lo_done, n * H + h - 1)
                    split_matmul(z_bank[h % 2], wqp_hi[:, h, :], wqp_lo[:, h, :], batch(y2T_hi, n), batch(y2T_lo, n)
                                 ).then_inc(z_full, 1)

                def numerators(h):
                    g = h // G
                    r = h % 3
                    if h % G == 0:
                        for t in range(TPB):
                            if g:
                                pe.wait_ge(att_done, n * NG * TPB + g * TPB + t + 1 - TPB)
                            nc.tensor.matmul(num[:, t, 0:G * HA], mean_of_rows[:, :],
                                             kbias[:, bass.ds(n, 1), G * HA * g:G * HA * (g + 1)].rearrange("p a c -> p (a c)"),
                                             start=True, stop=False)
                    pe.wait_ge(q_lo_done, n * H + h + 1)
                    cols = slice(HA * (h % G), HA * (h % G + 1))
                    kh, kl = (k[:, bass.ds(n, 1), HA * h:HA * (h + 1)].rearrange("p a c -> p (a c)") for k in (kvs_hi, kvs_lo))
                    for t in range(TPB):
                        part = slice(P * t, P * (t + 1))
                        last = split_matmul(num[:, t, cols], q_hi[:, r, part], q_lo[:, r, part], kh, kl,
                                            start=False, stop=h % G == G - 1)
                    last.then_inc(num_done, 1)

                def chunk(c):
                    pe.wait_ge(att_done, n * NG * TPB + (c // 2 + 1) * TPB)
                    if c:
                        pe.wait_ge(attT_lo_done, n * CH + c)
                    transposes(t_bank, [att[:, (c // 2) % 2, t, P * (c % 2):P * (c % 2 + 1)] for t in range(TPB)]
                               ).then_inc(tb_full, 1)

                def project_out(c):
                    if c == 0:
                        pe.wait_ge(route, n * ROUTE_STEPS + 1)
                    pe.wait_ge(attT_lo_done, n * CH + c + 1)
                    split_matmul(o_bank, wo_hi[:, c, :], wo_lo[:, c, :], attT_hi[:, c % 2, :], attT_lo[:, c % 2, :],
                                 start=c == 0, stop=c == CH - 1).then_inc(wo_done, 1)
                for k in range(STEPS):
                    if k < H:
                        features(k)
                    if 2 <= k < H + 2:
                        numerators(k - 2)
                    for c in range(CH):
                        if k == chunk_step(c) + 2:
                            project_out(c)
                    for c in range(CH):
                        if k == chunk_step(c):
                            chunk(c)
                pe.wait_ge(out2_done, n + 1)
                transposes(t_bank, [outT[:, P * t:P * (t + 1)] for t in range(TPB)]).then_inc(tb_full, 1)
                pe.wait_ge(y3_done, n * 8 + 8)
                pe.wait_ge(x2_done, n + 1)
                transposes(t_bank, [rows[:, 0, t, 0:P] for t in range(TPB)]).then_inc(tb_full, 1)
                pe.wait_ge(y3T_done, n + 1)
                for t in range(TPB):
                    last = nc.tensor.matmul(o_bank[:, E * t:E * (t + 1)], y3T[:, P * t:P * (t + 1)], router_sb[:, :],
                                            start=t == 0, stop=t == TPB - 1, skip_group_check=True)
                last.then_inc(logits_full, 1)
                pe.wait_ge(route, n * ROUTE_STEPS + 17)
                nc.tensor.matmul(o_bank[:, 64:64 + TPB * E], before[:, :], taken[:, :, :].rearrange("p t e -> p (t e)"),
                                 start=True, stop=False, skip_group_check=True)
                for t in range(TPB):
                    if t + 1 < TPB:
                        nc.tensor.matmul(o_bank[:, 64 + E * (t + 1):64 + E * TPB].rearrange("p (a e) -> p a e", e=E), ones_bf[:, :],
                                         taken[:, t, :].unsqueeze(1).broadcast_to([P, TPB - 1 - t, E]),
                                         start=False, stop=False, skip_group_check=True)
                    last = nc.tensor.matmul(o_bank[:, 128:128 + E], ones_bf[:, :], taken[:, t, :],
                                            start=False, stop=t == TPB - 1, skip_group_check=True)
                last.then_inc(rank_full, 1)

            pe.wait_ge(table_step, TABLE_STEPS)
            pe.wait_ge(moe_split, 2 * E)

            def turn_x(s, j, turn):
                pe.wait_ge(ld_xb[j], turn * 16 + 16)
                if not isinstance(s, int) or s >= 2:
                    pe.wait_ge(xT_lo_done, s - 1)
                nc.tensor.transpose(tx_bank[j % 2][:, 0:P], xb[:, j, 0:P], ident[:, :]).then_inc(tx_full, 1)

            def gate_up(s, j, turn):
                e = pe.value_load(table[0:1, 1, bass.ds(s, 1)], min_val=0, max_val=E - 1)
                pe.wait_ge(xT_lo_done, s + 1)
                if not isinstance(s, int) or s >= 2:
                    pe.wait_ge(hid_done, s - 1)
                split_matmul(gu_bank[j % 2], xT_hi[:, j, :], xT_lo[:, j, :], batch_r(wgu_hi, e), batch_r(wgu_lo, e)
                             ).then_inc(gu_full, 1)

            def turn_h(s, j, turn):
                pe.wait_ge(hid_done, s + 1)
                if not isinstance(s, int) or s >= 2:
                    pe.wait_ge(hT_lo_done, s - 1)
                transposes(th_bank[j % 2], [hid[:, j % 2, P * c:P * (c + 1)] for c in range(2)]).then_inc(th_full, 1)

            def down(s, j, turn):
                e = pe.value_load(table[0:1, 1, bass.ds(s, 1)], min_val=0, max_val=E - 1)
                pe.wait_ge(hT_lo_done, s + 1)
                if not isinstance(s, int) or s >= 2:
                    pe.wait_ge(yo_done, s - 1)
                for c in range(2):
                    part = slice(P * c, P * (c + 1))
                    last = split_matmul(dn_bank[j % 2][:, 0:P], hT_hi[:, j % 2, part], hT_lo[:, j % 2, part],
                                        wd_hi[:, bass.ds(e, 1), part].rearrange("p a c -> p (a c)"),
                                        wd_lo[:, bass.ds(e, 1), part].rearrange("p a c -> p (a c)"),
                                        start=c == 0, stop=c == 1)
                last.then_inc(dn_full, 1)

            def batch_r(t, e):
                return t[:, bass.ds(e, 1), :].rearrange("p a c -> p (a c)")

            pipeline(pe, [(0, turn_x), (1, gate_up), (2, turn_h), (3, down)])




def kernel(**inputs):
    import numpy as np
    import concourse.bacc as bacc
    from concourse.bass_utils import run_bass_kernel_spmd

    w = {k.replace("L0_", ""): np.asarray(v) for k, v in inputs.items()}
    coef = np.concatenate([w["attn_zero"], w["attn_pos"][:, :NB - 1]], axis=1)
    arrays = {
        "x": w["x"],
        "ctxT": w["ctx_1024"].transpose(2, 0, 1).reshape(P, NB * CTX),
        "wuv": np.concatenate([w["attn_Wu"].T, w["attn_Wv"].T], axis=1),
        "bu": w["attn_bu"].reshape(2, P).T,
        "bv": w["attn_bv"].reshape(2, P).T,
        "woaT": w["attn_Wo"].T.reshape(2, P, P).transpose(1, 0, 2),
        "bo": w["attn_bo"].reshape(P, 1),
        "coef": np.repeat(coef, MHD, axis=0).reshape(2, P, NB).transpose(1, 0, 2),
        "wqT": w["xattn_Wq"].transpose(2, 1, 0),
        "wkT": w["xattn_Wk"].transpose(2, 1, 0),
        "wv": w["xattn_Wv"].reshape(P, H * DH),
        "wo": w["xattn_Wo"].reshape(CH, P, P).transpose(1, 0, 2),
        "projT": w["xattn_proj"].T,
        "router": w["ffn_router_w"].T,
        "wgu": np.concatenate([w["ffn_w_gate"].transpose(2, 0, 1), w["ffn_w_up"].transpose(2, 0, 1)], axis=2),
        "wd": w["ffn_w_down"].transpose(2, 0, 1).reshape(2, P, E, P).transpose(1, 2, 0, 3).reshape(P, E, HID),
    }
    nc = bacc.Bacc("TRN2", target_bir_lowering=False, num_devices=1)
    feed, args = {}, []
    for name, a in arrays.items():
        feed["in_" + name] = np.ascontiguousarray(a)
        args.append(nc.dram_tensor("in_" + name, a.shape, F32, kind="ExternalInput").ap())
    out = nc.dram_tensor("out", (NB, POS, P), F32, kind="ExternalOutput").ap()
    dispatched = nc.dram_tensor("dispatched", (PAD_ROW + P, ROW), F32, kind="Internal").ap()
    expert_out = nc.dram_tensor("expert_out", (TOPK * TOKENS, P), F32, kind="Internal").ap()
    decoder_kernel(nc, *args, out, dispatched, expert_out)
    r = run_bass_kernel_spmd(nc, [feed], core_ids=[0])
    return r.results[0]["out"]
```

```python
import concourse.bass as bass
from concourse import mybir
from contextlib import ExitStack

F32 = mybir.dt.float32
F32R = mybir.dt.float32r
BF16 = mybir.dt.bfloat16
I32 = mybir.dt.int32
U32 = mybir.dt.uint32
ALU = mybir.AluOpType
ACT = mybir.ActivationFunctionType
AX = mybir.AxisListType

P = 128
NB = 4
POS = 512
TPB = POS // P
TILES = NB * TPB
D1 = 256
MH, MHD = 8, 32
CTX = 77
H, DH, M = 16, 64, 128
HA = P + 2
G = 4
NG = H // G
UNITS = H // 2
LAG = 3
E, HID = 8, 256
TOKENS = NB * POS
TOPK = 2
CAP = TOKENS
ROW = P + 2
PAD_ROW = E * CAP
BLOCKS = 40
RING = 8
EBITS = 3
LN_EPS = 1e-5
RMS_EPS = 1e-8
RELU_EPS = 1e-3
RATIO = float(M) ** -0.5
NO_DEST = TOPK * TOKENS


def decoder_kernel(nc, x, ctxT, wuv, bu, bv, woaT, bo, coef, wkv, wqo, projT, router, wgu, wd,
                   out, xs, ys):
    with ExitStack() as ctx:
        def sb(name, shape, dt=F32, stack=ctx):
            return stack.enter_context(nc.sbuf_tensor(name, shape, dt))

        def sem(name):
            return ctx.enter_context(nc.semaphore(name))

        X = sb("X", [P, TILES, P])
        y2T_hi = sb("y2T_hi", [P, NB, POS], F32R)
        y2T_lo = sb("y2T_lo", [P, NB, POS], F32R)
        feat_hi = sb("feat_hi", [P, H * M], F32R)
        feat_lo = sb("feat_lo", [P, H * M], F32R)
        kvw_hi = sb("kvw_hi", [P, NB, H * HA], F32R)
        kvw_lo = sb("kvw_lo", [P, NB, H * HA], F32R)
        router_sb = sb("router_sb", [P, E])
        outT = sb("outT", [P, POS])
        y2 = sb("y2", [P, TPB, P])
        ident = sb("ident", [P, P])
        stats = sb("stats", [P, TILES, 6])
        moments = sb("moments", [P, TILES, 2])
        moments_b = sb("moments_b", [P, TPB, 2])
        rstd = sb("rstd", [P, TPB])
        l_max = sb("l_max", [P, TPB])
        var_eps = sb("var_eps", [P, TPB])
        p_mhalf = sb("p_mhalf", [P, TILES])
        iota_e = sb("iota_e", [P, E])
        tri = sb("tri", [P, E, E])
        before = sb("before", [P, P], BF16)
        ones_bf = sb("ones_bf", [P, P], BF16)
        dest = sb("dest", [P, NB, TOPK, TPB], I32)
        seq = sb("seq", [1, BLOCKS])
        pad_row = sb("pad_row", [P, ROW])
        base = sb("base", [P, E])
        table = sb("table", [1, BLOCKS], I32)
        word_of = sb("word_of", [1, BLOCKS // RING], I32)
        shifts = sb("shifts", [1, BLOCKS // RING, RING])

        with ExitStack() as first:
            def sa(name, shape, dt=F32):
                return sb(name, shape, dt, first)
            woa_hi = sa("woa_hi", [P, 2, P], F32R)
            woa_lo = sa("woa_lo", [P, 2, P], F32R)
            bias_o = sa("bias_o", [P, 1])
            acc = sa("acc", [P, 2, 2, POS])
            wuv_sb = acc[:, 1, 0, :]
            o_hi = sa("o_hi", [P, 2, POS], F32R)
            o_lo = sa("o_lo", [P, 2, POS], F32R)
            projT_sb = sa("projT_sb", [DH, M])
            wkv_sb = sa("wkv_sb", [P, H, P])
            wqo_sb = sa("wqo_sb", [P, H, P])
            wvo_hi = sa("wvo_hi", [P, H * P], F32R)
            wvo_lo = sa("wvo_lo", [P, H * P], F32R)
            ctxT_sb = sa("ctxT_sb", [P, NB * CTX])
            ctxT_hi = sa("ctxT_hi", [P, NB * CTX], F32R)
            ctxT_lo = sa("ctxT_lo", [P, NB * CTX], F32R)
            kp = sa("kp", [CTX, 2, G * M])
            vw = sa("vw", [CTX, 2, G, HA])
            wuv_hi = sa("wuv_hi", [P, 2 * D1], F32R)
            wuv_lo = sa("wuv_lo", [P, 2 * D1], F32R)
            woa_sb = sa("woa_sb", [P, 2, P])
            bias_v = sa("bias_v", [P, 2])
            bias_u = sa("bias_u", [P, 2])
            coef_sb = sa("coef_sb", [P, 2, NB])
            xn = sa("xn", [P, TPB, P])
            xnT_hi = sa("xnT_hi", [P, POS], F32R)
            xnT_lo = sa("xnT_lo", [P, POS], F32R)
            v_hist = sa("v_hist", [P, NB, 2, POS])
            u_sb = sa("u_sb", [P, 2, POS])
            ln1 = sa("ln1", [P, 9, TILES])
            p_half = sa("p_half", [P, TILES])
            p_mone = sa("p_mone", [P, TILES])
        V_EPS, RSTD, STD, RMS, INV, SCALE, ONE_RSTD, NEG_SHIFT, SHIFT = range(9)

        wgu_hi = sb("wgu_hi", [P, E, 2 * HID], F32R)
        wgu_lo = sb("wgu_lo", [P, E, 2 * HID], F32R)
        wd_hi = sb("wd_hi", [P, E, HID], F32R)
        wd_lo = sb("wd_lo", [P, E, HID], F32R)
        with ExitStack() as second:
            def sc(name, shape, dt=F32):
                return sb(name, shape, dt, second)
            relu_z = sc("relu_z", [P, 2, POS])
            q = sc("q", [P, 2, POS])
            q_hi = sc("q_hi", [P, 4, POS], F32R)
            q_lo = sc("q_lo", [P, 4, POS], F32R)
            rden = sc("rden", [P, 2, TPB])
            wgu_raw = sc("wgu_raw", [P, 2, 2 * HID])
            wd_raw = sc("wd_raw", [P, 2, HID])
            rows = sc("rows", [P, TOPK, TPB, ROW])
            y3T = sc("y3T", [P, POS])
            l_sub = sc("l_sub", [P, TPB, E])
            l_exp = sc("l_exp", [P, TPB, E])
            l_sum = sc("l_sum", [P, TPB])
            prob = sc("prob", [P, TPB, E])
            top_v = sc("top_v", [P, TPB, 8])
            top_i = sc("top_i", [P, TPB, 8], U32)
            top_f = sc("top_f", [P, TPB, TOPK])
            chosen = sc("chosen", [P, TPB, TOPK, E])
            taken = sc("taken", [P, TPB, E], BF16)
            w_sum = sc("w_sum", [P, TPB])
            slot_e = sc("slot_e", [P, TPB, E])
            slot_k = sc("slot_k", [P, TPB, TOPK, E])
            slot_f = sc("slot_f", [P, TPB, TOPK])
            slot_i = sc("slot_i", [P, TPB, TOPK], I32)
            t_cnt = sc("t_cnt", [1, E], I32)
            t_nb = sc("t_nb", [1, E])
            t_prod = sc("t_prod", [1, E, E])
            t_end = sc("t_end", [1, E])
            t_start = sc("t_start", [1, E])
            t_val = sc("t_val", [1, E])
            t_ge = sc("t_ge", [1, 2, BLOCKS, E])
            t_oh = sc("t_oh", [1, BLOCKS, E])
            t_mul = sc("t_mul", [1, 2, BLOCKS, E])
            t_sum = sc("t_sum", [1, 3, BLOCKS])

        xb = sb("xb", [P, RING, ROW])
        meta = sb("meta", [P, RING, 2], I32)
        xT_hi = sb("xT_hi", [P, RING, P], F32R)
        xT_lo = sb("xT_lo", [P, RING, P], F32R)
        silu_g = sb("silu_g", [P, 2, HID])
        hid = sb("hid", [P, 2, HID])
        hT_hi = sb("hT_hi", [P, 2, HID], F32R)
        hT_lo = sb("hT_lo", [P, 2, HID], F32R)
        yo = sb("yo", [P, RING, P])
        y_back = sb("y_back", [P, TOPK, NB, POS])

        bank = [ctx.enter_context(nc.psum_tensor(f"bank{i}", [P, POS], F32)) for i in range(2)]
        num = ctx.enter_context(nc.psum_tensor("num", [P, TPB, POS], F32))
        bank += [num[:, i, :] for i in range(4)]
        bank += [ctx.enter_context(nc.psum_tensor(f"bank{i}", [P, POS], F32)) for i in (6, 7)]
        bank = [b if i in (2, 3, 4, 5) else b[:, :] for i, b in enumerate(bank)]
        uv_bank, kv_bank, ks_bank, o_bank, t_bank = bank[0:2], bank[2:4], bank[4:6], bank[6], bank[7]
        fold_bank = uv_bank + ks_bank
        z_bank = bank[0:2]

        ld_x = [sem(f"ld_x{n}") for n in range(NB)]
        ld_proj, ld_wqo, ld_ctx, ld_wuv = map(sem, ("ld_proj", "ld_wqo", "ld_ctx", "ld_wuv"))
        ld_wkv = [sem(f"ld_wkv{g}") for g in range(NG)]
        ld_small, ld_woa = map(sem, ("ld_small", "ld_woa"))
        ld_moe = [sem("ld_moe_even"), sem("ld_moe_odd")]
        filled = sem("filled")
        waits_passed = sem("waits_passed")
        consts = sem("consts")
        stats_done = sem("stats_done")
        moments_done = sem("moments_done")
        ln1_step = sem("ln1_step")
        ctx_hi_done, ctx_lo_done = sem("ctx_hi_done"), sem("ctx_lo_done")
        wuv_hi_done, wuv_lo_done = sem("wuv_hi_done"), sem("wuv_lo_done")
        wk_full, wk_hi_done, wk_lo_done = sem("wk_full"), sem("wk_hi_done"), sem("wk_lo_done")
        wvo_full, wvo_hi_done, wvo_lo_done = sem("wvo_full"), sem("wvo_hi_done"), sem("wvo_lo_done")
        wq_full, wq_hi_done, wq_lo_done = sem("wq_full"), sem("wq_hi_done"), sem("wq_lo_done")
        woa_split = sem("woa_split")
        xn_done, shortcut_done = sem("xn_done"), sem("shortcut_done")
        xnT_hi_done = sem("xnT_hi_done")
        uv_full, uv_evac = sem("uv_full"), sem("uv_evac")
        kp_full, kp_done, vw_full, vw_done = sem("kp_full"), sem("kp_done"), sem("vw_full"), sem("vw_done")
        ks_full, ks_hi_done, ks_free = sem("ks_full"), sem("ks_hi_done"), sem("ks_free")
        t_full, t_free = sem("t_full"), sem("t_free")
        conv_step, o_prod, o_hi_done, o_lo_done = sem("conv_step"), sem("o_prod"), sem("o_hi_done"), sem("o_lo_done")
        o_full, outT_done = sem("o_full"), sem("outT_done")
        ln2_stats, ln2_moments, ln2_step, y2_done, y2T_hi_done = map(sem, ("ln2_stats", "ln2_moments", "ln2_step", "y2_done", "y2T_hi_done"))
        z_full, relu_done, q_done, q_hi_done, q_lo_done, q_lo_late = map(
            sem, ("z_full", "relu_done", "q_done", "q_hi_done", "q_lo_done", "q_lo_late"))
        num_done, rden_done, att_done = sem("num_done"), sem("rden_done"), sem("att_done")
        tb_full = sem("tb_full")
        ln3_stats, ln3_moments, ln3_step, y3_done, y3T_done, y3_twice = map(
            sem, ("ln3_stats", "ln3_moments", "ln3_step", "y3_done", "y3T_done", "y3_twice"))
        logits_full, exp_done, rank_full = sem("logits_full"), sem("exp_done"), sem("rank_full")
        route = sem("route")
        dest_done, sent = sem("dest_done"), sem("sent")
        moe_hi_done, moe_split = sem("moe_hi_done"), sem("moe_split")
        table_step = sem("table_step")
        ld_xb = [sem(f"ld_xb{j}") for j in range(RING)]
        meta_done, tx_full, xT_hi_done, xT_lo_done = map(sem, ("meta_done", "tx_full", "xT_hi_done", "xT_lo_done"))
        gu_full, silu_done, hid_done = sem("gu_full"), sem("silu_done"), sem("hid_done")
        th_full, hT_hi_done, hT_lo_done = sem("th_full"), sem("hT_hi_done"), sem("hT_lo_done")
        dn_full, yo_done = sem("dn_full"), sem("yo_done")
        y_sent = [sem(f"y_sent{j}") for j in range(RING)]
        ld_y = [sem(f"ld_y{n}") for n in range(NB)]
        add_step = sem("add_step")
        stored = sem("stored")

        block = ctx.enter_context(nc.Block())

        def t_job(kind, n):
            order = [("xn", 0)]
            for m in range(1, NB):
                order += [("xn", m), ("out", m - 1), ("y2", m - 1)]
            order += [("out", NB - 1), ("y2", NB - 1)]
            return order.index((kind, n))

        def split_matmul(ps, a_hi, a_lo, b_hi, b_lo, start=True, stop=True):
            nc.tensor.matmul(ps, a_hi, b_hi, start=start, stop=False)
            nc.tensor.matmul(ps, a_hi, b_lo, start=False, stop=False)
            return nc.tensor.matmul(ps, a_lo, b_hi, start=False, stop=stop)

        def batch(t, n):
            return t[:, n, :] if isinstance(n, int) else t[:, bass.ds(n, 1), :].rearrange("p a c -> p (a c)")

        def tile_of(n, t):
            return X[:, TPB * n + t, :] if isinstance(n, int) else \
                X[:, bass.ds(n * TPB + t, 1), :].rearrange("p a c -> p (a c)")

        xs_blocks = xs.rearrange("(a p) c -> p a c", p=P)
        x_view = x.rearrange("n (t p) d -> n p t d", p=P)
        out_view = out.rearrange("n (t p) d -> n p t d", p=P)
        ys_view = ys.rearrange("(k n t p) d -> k n p t d", k=TOPK, n=NB, p=P)
        FILL_ROWS = xs_blocks.shape[1]

        CONSTS = 16 + RING
        PE_MIXER, PE_OUT, PE_Y2, ACT_Y2, DVE_Y2, POOL_LN2 = 1, 2, 6, 6, 3, 2
        SPLIT = (3, 4, 6, 7, 9, 10, 12, 13)
        DVE_SPLIT = tuple(k - 2 for k in SPLIT)
        POOL_NORM = 3
        SCATTER = (13, 13, 14, 15)
        LATE_LO = (13, 14, 15)
        EARLY_LO = H - len(LATE_LO)
        DVE_NORM = 1
        DVE_ROUTE = (3, 4, 5, 5, 6, 6, 7, 7, 9, 9)
        ACT_Y3 = 6
        ACT_EXP = 8
        PE_Y3, PE_LOGITS, PE_RANKS = 6, 7, 12
        ROUTE_STEPS = 24
        TAKEN_STEP = 16
        FILLS = 3 * 16
        TABLE_STEPS = 17
        LN1_STEPS = 10
        tx_bank, gu_bank, th_bank, dn_bank = bank[6:8], bank[0:2], bank[2:4], bank[4:6]

        def wait_past(eng, semaphore, value):
            if not isinstance(value, int) or value > 0:
                eng.wait_ge(semaphore, value)

        def wait_lo(eng, n, h):
            if h < 0:
                n, h = n - 1, h + H
            if isinstance(n, int) and n < 0:
                return
            if h in LATE_LO:
                eng.wait_ge(q_lo_late, n * len(LATE_LO) + LATE_LO.index(h) + 1)
            else:
                eng.wait_ge(q_lo_done, n * EARLY_LO + h + 1)

        def over_batches(eng, body, end):
            body(0, None)
            with eng.Fori(1, NB) as n:
                body(n, n - 1)
            end()

        def wait_alone(eng, semaphore, value):
            eng.wait_ge(semaphore, value)
            if not isinstance(value, int):
                eng.sem_inc(waits_passed, 1)

        def pipeline(eng, stages, window=None):
            depth = max(lag for lag, _ in stages)

            def tick(i, j):
                for lag, fn in stages:
                    s = i * RING + (j - lag)
                    if not isinstance(s, int) or 0 <= s < BLOCKS:
                        fn(s, (j - lag) % RING, i + (j - lag) // RING, *((j - lag,) if window else ()))
            if window:
                window(0)
            for j in range(RING):
                tick(0, j)
            with eng.Fori(1, BLOCKS // RING) as i:
                if window:
                    window(i)
                for j in range(RING):
                    tick(i, j)
            if window:
                window(BLOCKS // RING)
            for j in range(depth):
                tick(BLOCKS // RING, j)

        @block.sync
        def _(sp):
            sp.dma_start(projT_sb[:, :], projT).then_inc(ld_proj, 16)
            for g in range(NG):
                sp.dma_start(wkv_sb[:, G * g:G * (g + 1), :], wkv[:, G * g:G * (g + 1), :]).then_inc(ld_wkv[g], 16)
            sp.dma_start(ctxT_sb[:, :], ctxT).then_inc(ld_ctx, 16)
            sp.dma_start(wqo_sb[:, :, :], wqo).then_inc(ld_wqo, 16)
            sp.dma_start(wuv_sb, wuv).then_inc(ld_wuv, 16)
            for dst, src in ((bias_v[:, :], bv), (bias_u[:, :], bu), (bias_o[:, :], bo), (coef_sb[:, :, :], coef)):
                sp.dma_start(dst, src).then_inc(ld_small, 16)
            sp.dma_start(router_sb[:, :], router).then_inc(ld_small, 16)
            sp.dma_start(woa_sb[:, :, :], woaT).then_inc(ld_woa, 16)
            sp.wait_ge(consts, CONSTS)
            for a in range(0, FILL_ROWS, 43):
                sp.dma_start(xs_blocks[:, a:a + 43, :],
                             pad_row[:, :].unsqueeze(1).broadcast_to([P, 43, ROW])).then_inc(filled, 16)
            sp.wait_ge(wq_lo_done, NG)
            sp.wait_ge(o_full, NB)
            sp.wait_ge(ks_free, UNITS * NB)
            for e in range(E):
                if e >= 2:
                    sp.wait_ge(moe_split, 2 * (e - 1))
                sp.dma_start(wgu_raw[:, e % 2, :], wgu[:, e, :]).then_inc(ld_moe[e % 2], 16)
                sp.dma_start(wd_raw[:, e % 2, :], wd[:, e, :]).then_inc(ld_moe[e % 2], 16)
            sp.wait_ge(table_step, TABLE_STEPS - 3)
            sp.wait_ge(sent, 16 * TOPK * TPB * NB)

            def load_block(s, j, reused):
                row = sp.value_load(table[0:1, bass.ds(s, 1)], min_val=0, max_val=PAD_ROW)
                if reused:
                    sp.wait_ge(tx_full, s - RING + 1)
                    sp.wait_ge(meta_done, s - RING + 1)
                sp.dma_start(xb[:, j, :], xs[bass.ds(row, P), :]).then_inc(ld_xb[j], 16)

            for j in range(RING):
                load_block(j, j, False)
            with sp.Fori(1, BLOCKS // RING) as i:
                for j in range(RING):
                    load_block(i * RING + j, j, True)
            for j in range(RING):
                sp.wait_ge(y_sent[j], 16 * BLOCKS // RING)
            for n in range(NB):
                for k in range(TOPK):
                    sp.dma_start(y_back[:, k, n, :].rearrange("p (t c) -> p t c", t=TPB),
                                 ys_view[k, n, :, :, :]).then_inc(ld_y[n], 16)
            for n in range(NB):
                sp.wait_ge(add_step, 2 * (n + 1))
                sp.dma_start(out_view[n, :, :, :], X[:, TPB * n:TPB * (n + 1), :]).then_inc(stored, 16)
            sp.wait_ge(stored, 16 * NB)

        @block.gpsimd
        def _(pool):
            g = nc.gpsimd
            made = []

            def const(ins):
                ins.then_inc(consts, 1)
                made.append(ins)

            const(g.memset(ident[:, :], 0.0))
            const(g.memset(p_mhalf[:, :], -0.5))
            const(g.memset(p_half[:, :], 0.5))
            const(g.memset(p_mone[:, :], -1.0))
            const(g.memset(vw[:, :, :, :], 0.0))
            const(g.memset(pad_row[:, :], 0.0))
            const(g.memset(tri[:, :, :], 1.0))
            const(g.memset(before[:, :], 1.0))
            const(g.memset(ones_bf[:, :], 1.0))
            const(g.iota(dest[:, :, :, :], [[POS, NB], [TOKENS, TOPK], [P, TPB]], base=0, channel_multiplier=1))
            const(g.iota(iota_e[:, :], [[1, E]], base=0, channel_multiplier=0, allow_small_or_imprecise_dtypes=True))
            pool.wait_ge(consts, 11)
            const(g.affine_select(out=ident[:, :], in_=ident[:, :], compare_op=ALU.not_equal, fill=1.0,
                                  base=0, pattern=[[-1, P]], channel_multiplier=1))
            const(g.memset(vw[:, :, :, P:P + 1], 1.0))
            const(g.iota(pad_row[:, P:P + 1].bitcast(I32), [[1, 1]], base=NO_DEST, channel_multiplier=0))
            const(g.affine_select(out=tri[:, :, :], in_=tri[:, :, :], compare_op=ALU.is_ge, fill=0.0,
                                  base=0, pattern=[[1, E], [-1, E]], channel_multiplier=0))
            const(g.affine_select(out=before[:, :], in_=before[:, :], compare_op=ALU.is_gt, fill=0.0,
                                  base=0, pattern=[[1, P]], channel_multiplier=-1))
            for j in range(RING):
                const(g.memset(shifts[:, :, j:j + 1], float(1 << EBITS * j)))
            assert len(made) == CONSTS
            g.iota(seq[:, :], [[P, BLOCKS]], base=-PAD_ROW, channel_multiplier=0,
                   allow_small_or_imprecise_dtypes=True).then_inc(ln1_step, 1)
            g.iota(base[:, :], [[CAP, E]], base=0, channel_multiplier=0,
                   allow_small_or_imprecise_dtypes=True).then_inc(ln1_step, 1)

            def ln1_chain(tiles, before):
                mean, var = moments[:, tiles, 0], moments[:, tiles, 1]
                steps = [
                    lambda: g.tensor_scalar(ln1[:, V_EPS, tiles], var, LN_EPS, None, ALU.add),
                    lambda: g.tensor_tensor(ln1[:, STD, tiles], var, p_half[:, tiles], ALU.pow),
                    lambda: g.tensor_tensor(ln1[:, RSTD, tiles], ln1[:, V_EPS, tiles], p_mhalf[:, tiles], ALU.pow),
                    lambda: g.tensor_tensor(ln1[:, RMS, tiles], ln1[:, STD, tiles], ln1[:, RSTD, tiles], ALU.mult),
                    lambda: g.tensor_scalar(ln1[:, STD, tiles], ln1[:, RMS, tiles], RMS_EPS, None, ALU.add),
                    lambda: g.tensor_tensor(ln1[:, INV, tiles], ln1[:, STD, tiles], p_mone[:, tiles], ALU.pow),
                    lambda: g.tensor_tensor(ln1[:, SCALE, tiles], ln1[:, INV, tiles], ln1[:, RSTD, tiles], ALU.mult),
                    lambda: g.tensor_scalar(ln1[:, ONE_RSTD, tiles], ln1[:, RSTD, tiles], 1.0, None, ALU.add),
                    lambda: g.tensor_tensor(ln1[:, NEG_SHIFT, tiles], mean, ln1[:, RSTD, tiles], ALU.mult),
                    lambda: g.tensor_scalar(ln1[:, SHIFT, tiles], ln1[:, NEG_SHIFT, tiles], -1.0, None, ALU.mult),
                ]
                assert len(steps) == LN1_STEPS
                for i, step in enumerate(steps):
                    pool.wait_ge(ln1_step, before + i)
                    step().then_inc(ln1_step, 1)

            pool.wait_ge(moments_done, TPB)
            ln1_chain(slice(0, TPB), 2)
            pool.wait_ge(moments_done, TILES)
            ln1_chain(slice(TPB, TILES), LN1_STEPS + 2)

            def split(dst_hi, dst_lo, src, done, count):
                g.tensor_copy(dst_hi, src).then_inc(done, 1)
                pool.wait_ge(done, count + 1)
                g.tensor_tensor(dst_lo, src, dst_hi, ALU.subtract).then_inc(done, 1)

            pool.wait_ge(ld_woa, 16)
            split(woa_hi[:, :, :], woa_lo[:, :, :], woa_sb[:, :, :], woa_split, 0)

            def ln_rstd(var_ap, step_sem, count):
                g.tensor_scalar(var_eps[:, :], var_ap, LN_EPS, None, ALU.add).then_inc(step_sem, 1)
                pool.wait_ge(step_sem, count + 1)
                g.tensor_tensor(rstd[:, :], var_eps[:, :], p_mhalf[:, 0:TPB], ALU.pow).then_inc(step_sem, 1)

            def ln2(n):
                pool.wait_ge(ln2_moments, TPB * (n + 1))
                ln_rstd(moments_b[:, :, 1], ln2_step, 2 * n)

            for n in range(NB):
                if n == 0:
                    pool.wait_ge(ln1_step, 2 * LN1_STEPS + 2)
                pool.wait_ge(xn_done, TPB * (n + 1))
                for t in range(TPB):
                    i = TPB * n + t
                    g.tensor_scalar(X[:, i, :], X[:, i, :], ln1[:, ONE_RSTD, i:i + 1], ln1[:, SHIFT, i:i + 1],
                                    ALU.mult, ALU.add).then_inc(shortcut_done, 1)
                if n + 1 < NB:
                    pool.wait_ge(t_full, t_job("xn", n) + 1)
                    for t in range(TPB * (n + 1), TPB * (n + 2)):
                        g.tensor_scalar(xn[:, t % TPB, :], X[:, t, :], moments[:, t, 0:1], ln1[:, SCALE, t:t + 1],
                                        ALU.subtract, ALU.mult).then_inc(xn_done, 1)
                if n:
                    ln2(n - 1)
                pool.wait_ge(o_hi_done, n + 1)
                g.tensor_tensor(o_lo[:, :, :], acc[:, n % 2, :, :], o_hi[:, :, :], ALU.subtract).then_inc(o_lo_done, 1)
            pool.wait_ge(filled, FILLS)

            def third_norm(m):
                wait_alone(pool, ln3_moments, m * TPB + TPB)
                g.tensor_scalar(var_eps[:, :], moments_b[:, :, 1], LN_EPS, None, ALU.add).then_inc(ln3_step, 1)
                if not isinstance(m, int) or m > 0:
                    wait_alone(pool, sent, m * 16 * TOPK * TPB)
                pool.wait_ge(ln3_step, m * 2 + 1)
                g.tensor_tensor(rstd[:, :], var_eps[:, :], p_mhalf[:, 0:TPB], ALU.pow).then_inc(ln3_step, 1)
                g.tensor_copy(rows[:, :, :, P].bitcast(I32),
                              batch4(dest, m).rearrange("p a k t -> p (a k) t")).then_inc(dest_done, 1)

            def batch4(t, m):
                return t[:, m:m + 1, :, :] if isinstance(m, int) else t[:, bass.ds(m, 1), :, :]

            def scatter(m, t):
                if t == 0:
                    pool.wait_ge(dest_done, m + 1)
                    pool.sem_inc(waits_passed, 1)
                    wait_alone(pool, y3_twice, m + 1)
                    wait_alone(pool, route, m * ROUTE_STEPS + ROUTE_STEPS + 1)
                for k in range(TOPK):
                    g.indirect_dma_start(
                        out=xs, out_offset=bass.IndirectOffsetOnAxis(ap=slot_i[:, t, k:k + 1], axis=0),
                        in_=rows[:, k, t, :], in_offset=None).then_inc(sent, 16)

            def attention(n, m):
                for k in range(H):
                    if m is None and k == POOL_LN2:
                        ln2(NB - 1)
                    if m is not None and k == POOL_NORM:
                        third_norm(m)
                    for t in range(TPB):
                        if m is not None and k == SCATTER[t]:
                            scatter(m, t)
                    if k not in LATE_LO:
                        f = n * H + k
                        pool.wait_ge(q_hi_done, f + 1)
                        wait_past(pool, num_done, (f - 3) * TPB)
                        g.tensor_tensor(q_lo[:, k % 4, :], q[:, k % 2, :], q_hi[:, k % 4, :], ALU.subtract).then_inc(q_lo_done, 1)
            def last_routing():
                third_norm(NB - 1)
                for t in range(TPB):
                    scatter(NB - 1, t)
                pool.wait_ge(sent, NB * 16 * TOPK * TPB)
                pool.sem_inc(waits_passed, 1)

            over_batches(pool, attention, last_routing)

            def take_meta(s, j, turn):
                wait_alone(pool, ld_xb[j], turn * 16 + 16)
                if not isinstance(s, int):
                    wait_alone(pool, y_sent[j], turn * 16)
                g.tensor_copy(meta[:, j, :], xb[:, j, P:P + 2].bitcast(I32)).then_inc(meta_done, 1)

            def send(s, j, turn):
                wait_alone(pool, yo_done, s + 1)
                g.indirect_dma_start(
                    out=ys, out_offset=bass.IndirectOffsetOnAxis(ap=meta[:, j, 0:1], axis=0),
                    in_=yo[:, j, :], in_offset=None, bounds_check=NO_DEST - 1, oob_is_err=False).then_inc(y_sent[j], 16)

            pipeline(pool, [(0, take_meta), (3, send)])

        @block.scalar
        def _(act):
            a = nc.scalar
            for n in range(NB):
                act.dma_start(X[:, TPB * n:TPB * (n + 1), :], x_view[n, :, :, :]).then_inc(ld_x[n], 16)
            a.preload_act_table(ACT.Silu)

            def copy(dst, src, **kw):
                return a.activation(dst, src, ACT.Copy, **kw)

            for g in range(NG):
                act.wait_ge(wk_full, g + 1)
                copy(feat_hi[:, POS * g:POS * (g + 1)], fold_bank[g], scale=RATIO).then_inc(wk_hi_done, 1)
            act.wait_ge(ld_ctx, 16)
            copy(ctxT_hi[:, :], ctxT_sb[:, :]).then_inc(ctx_hi_done, 1)
            for g in range(NG):
                act.wait_ge(wvo_full, g + 1)
                copy(wvo_hi[:, POS * g:POS * (g + 1)], fold_bank[g]).then_inc(wvo_hi_done, 1)
            act.wait_ge(ld_wuv, 16)
            copy(wuv_hi[:, :], wuv_sb).then_inc(wuv_hi_done, 1)
            act.wait_ge(ld_small, 16 * 5)
            act.wait_ge(consts, CONSTS)

            def y2T_high(n):
                act.wait_ge(t_full, t_job("y2", n) + 1)
                copy(y2T_hi[:, n, :], t_bank).then_inc(y2T_hi_done, 1)

            def mixer_output(n):
                act.wait_ge(o_full, n + 1)
                if n:
                    act.wait_ge(t_full, t_job("out", n - 1) + 1)
                a.activation(outT[:, :], o_bank, ACT.Identity, bias=bias_o[:, 0:1]).then_inc(outT_done, 1)

            def wq_high(g):
                act.wait_ge(wq_full, g + 1)
                copy(feat_hi[:, POS * g:POS * (g + 1)], uv_bank[g % 2], scale=RATIO).then_inc(wq_hi_done, 1)

            for n in range(NB):
                def values(i):
                    f = NG * n + i
                    act.wait_ge(vw_full, f + 1)
                    if f >= 2:
                        act.wait_ge(ks_full, 2 * (f - 1))
                    copy(vw[:, i % 2, :, 0:P], kv_bank[1][0:CTX, :].rearrange("p (h d) -> p h d", h=G)).then_inc(vw_done, 1)

                def kvw_high(u):
                    act.wait_ge(ks_full, UNITS * n + u + 1)
                    copy(kvw_hi[:, n, 2 * HA * u:2 * HA * (u + 1)], ks_bank[u % 2][:, 0:2 * HA]).then_inc(ks_hi_done, 1)

                values(0)
                act.wait_ge(t_full, t_job("xn", n) + 1)
                if n:
                    act.wait_ge(uv_full, 4 * n)
                copy(xnT_hi[:, :], t_bank).then_inc(xnT_hi_done, 1)
                values(1)
                for i in range(4):
                    act.wait_ge(uv_full, 4 * n + i + 1)
                    if n and i == 2:
                        act.wait_ge(o_prod, n)
                    dst, bias = (v_hist[:, n, i, :], bias_v) if i < 2 else (u_sb[:, i - 2, :], bias_u)
                    a.activation(dst, uv_bank[i % 2], ACT.Silu, bias=bias[:, i % 2:i % 2 + 1]).then_inc(uv_evac, 1)
                    if n and i == 0:
                        mixer_output(n - 1)
                kvw_high(0)
                kvw_high(1)
                values(2)
                kvw_high(2)
                kvw_high(3)
                values(3)
                kvw_high(4)
                kvw_high(5)
                kvw_high(6)
                kvw_high(7)
                if n == NB - 1:
                    wq_high(0)
                    wq_high(1)
                if n:
                    y2T_high(n - 1)
                act.wait_ge(o_prod, n + 1)
                if n:
                    act.wait_ge(o_full, n)
                copy(o_hi[:, :, :], acc[:, n % 2, :, :]).then_inc(o_hi_done, 1)
            wq_high(2)
            wq_high(3)

            a.preload_act_table(ACT.Exp)
            act.wait_ge(ks_free, UNITS * NB)
            act.wait_ge(wq_lo_done, NG)

            def q_high(f, slot):
                act.wait_ge(q_done, f + 1)
                wait_past(act, num_done, (f - 3) * TPB)
                copy(q_hi[:, slot % 4, :], q[:, slot % 2, :]).then_inc(q_hi_done, 1)

            def turned_rows(m):
                act.wait_ge(tb_full, m + 1)
                copy(y3T[:, :], t_bank).then_inc(y3T_done, 1)

            def second_rows(m):
                act.wait_ge(y3_done, m * TPB + TPB)
                copy(rows[:, 1, :, 0:P], rows[:, 0, :, 0:P]).then_inc(y3_twice, 1)

            def exponentials(m):
                act.wait_ge(route, m * ROUTE_STEPS + 3)
                a.activation(l_exp[:, :, :], l_sub[:, :, :], ACT.Exp).then_inc(exp_done, 1)

            def attention(n, m):
                for k in range(H):
                    f = n * H + k
                    act.wait_ge(z_full, f + 1)
                    wait_past(act, q_done, f - 1)
                    a.activation(relu_z[:, k % 2, :], z_bank[k % 2], ACT.Relu).then_inc(relu_done, 1)
                    if k or m is not None:
                        q_high(f - 1, (k - 1) % H)
                    wait_lo(act, n, k - 2)
                    act.wait_ge(relu_done, f + 1)
                    copy(q[:, k % 2, :], relu_z[:, k % 2, :], bias=RELU_EPS).then_inc(q_done, 1)
                    if m is None and k in SPLIT:
                        e = SPLIT.index(k)
                        act.wait_ge(ld_moe[e % 2], 32 * (e // 2 + 1))
                        copy(wgu_hi[:, e, :], wgu_raw[:, e % 2, :]).then_inc(moe_hi_done, 1)
                        copy(wd_hi[:, e, :], wd_raw[:, e % 2, :]).then_inc(moe_hi_done, 1)
                    if m is None and k == PE_MIXER:
                        mixer_output(NB - 1)
                    if m is None and k == ACT_Y2:
                        y2T_high(NB - 1)
                    if m is not None and k == ACT_Y3:
                        turned_rows(m)
                        second_rows(m)
                    if m is not None and k == ACT_EXP:
                        exponentials(m)

            def last_routing():
                q_high(NB * H - 1, H - 1)
                turned_rows(NB - 1)
                second_rows(NB - 1)
                exponentials(NB - 1)

            over_batches(act, attention, last_routing)

            a.preload_act_table(ACT.Silu)

            def x_high(s, j, turn):
                act.wait_ge(tx_full, s + 1)
                copy(xT_hi[:, j, :], tx_bank[j % 2][:, 0:P]).then_inc(xT_hi_done, 1)

            def gate(s, j, turn):
                act.wait_ge(gu_full, s + 1)
                a.activation(silu_g[:, j % 2, :], gu_bank[j % 2][:, 0:HID], ACT.Silu).then_inc(silu_done, 1)

            def h_high(s, j, turn):
                act.wait_ge(th_full, s + 1)
                copy(hT_hi[:, j % 2, :], th_bank[j % 2][:, 0:HID]).then_inc(hT_hi_done, 1)

            def weigh(s, j, turn):
                act.wait_ge(dn_full, s + 1)
                act.wait_ge(meta_done, s + 1)
                a.activation(yo[:, j, :], dn_bank[j % 2][:, 0:P], ACT.Copy,
                             scale=meta[:, j, 1:2].bitcast(F32)).then_inc(yo_done, 1)

            pipeline(act, [(0, x_high), (1, gate), (2, h_high), (3, weigh)])

        @block.vector
        def _(dve):
            v = nc.vector

            def lo(dst, src, hi, scale=1.0, op=ALU.mult):
                return v.scalar_tensor_tensor(dst, src, scale, hi, op, ALU.subtract)

            def first_moments(n):
                dve.wait_ge(ld_x[n], 16)
                for t in range(TPB * n, TPB * (n + 1)):
                    v.bn_stats(stats[:, t, :], X[:, t, :]).then_inc(stats_done, 1)
                dve.wait_ge(stats_done, TPB * (n + 1))
                for t in range(TPB * n, TPB * (n + 1)):
                    v.bn_aggr(moments[:, t, :], stats[:, t, :]).then_inc(moments_done, 1)

            def wk_low(g):
                dve.wait_ge(wk_hi_done, g + 1)
                part = slice(POS * g, POS * (g + 1))
                lo(feat_lo[:, part], fold_bank[g], feat_hi[:, part], RATIO).then_inc(wk_lo_done, 1)

            def wvo_low(g):
                dve.wait_ge(wvo_hi_done, g + 1)
                part = slice(POS * g, POS * (g + 1))
                lo(wvo_lo[:, part], fold_bank[g], wvo_hi[:, part]).then_inc(wvo_lo_done, 1)

            first_moments(0)
            wk_low(0)
            wk_low(1)
            first_moments(1)
            wk_low(2)
            wk_low(3)
            dve.wait_ge(ctx_hi_done, 1)
            lo(ctxT_lo[:, :], ctxT_sb[:, :], ctxT_hi[:, :]).then_inc(ctx_lo_done, 1)
            first_moments(2)
            wvo_low(0)
            wvo_low(1)
            first_moments(3)
            wvo_low(2)
            wvo_low(3)
            dve.wait_ge(wuv_hi_done, 1)
            lo(wuv_lo[:, :], wuv_sb, wuv_hi[:, :]).then_inc(wuv_lo_done, 1)

            dve.wait_ge(ln1_step, LN1_STEPS + 2)
            for t in range(TPB):
                v.tensor_scalar(xn[:, t, :], X[:, t, :], moments[:, t, 0:1], ln1[:, SCALE, t:t + 1],
                                ALU.subtract, ALU.mult).then_inc(xn_done, 1)
            steps = [0]

            def conv(ins):
                steps[0] += 1
                ins.then_inc(conv_step, 1)

            def residual(n):
                dve.wait_ge(t_full, t_job("out", n) + 1)
                dve.wait_ge(shortcut_done, TPB * (n + 1))
                part = X[:, TPB * n:TPB * (n + 1), :].rearrange("p t c -> p (t c)")
                v.tensor_tensor(part, part, t_bank, ALU.add).then_inc(t_free, 1)
                dve.wait_ge(t_free, t_job("out", n) + 1)
                for t in range(TPB):
                    v.bn_stats(stats[:, t, :], X[:, TPB * n + t, :]).then_inc(ln2_stats, 1)
                dve.wait_ge(ln2_stats, TPB * (n + 1))
                for t in range(TPB):
                    v.bn_aggr(moments_b[:, t, :], stats[:, t, :]).then_inc(ln2_moments, 1)

            def second_norm(n):
                dve.wait_ge(ln2_step, 2 * (n + 1))
                for t in range(TPB):
                    v.tensor_scalar(y2[:, t, :], X[:, TPB * n + t, :], moments_b[:, t, 0:1], rstd[:, t:t + 1],
                                    ALU.subtract, ALU.mult).then_inc(y2_done, 1)

            def y2T_low(n):
                dve.wait_ge(y2T_hi_done, n + 1)
                lo(y2T_lo[:, n, :], t_bank, y2T_hi[:, n, :]).then_inc(t_free, 1)

            def wq_low(g):
                dve.wait_ge(wq_hi_done, g + 1)
                part = slice(POS * g, POS * (g + 1))
                lo(feat_lo[:, part], uv_bank[g % 2], feat_hi[:, part], RATIO).then_inc(wq_lo_done, 1)

            for n in range(NB):
                def keys(i):
                    f = NG * n + i
                    dve.wait_ge(kp_full, f + 1)
                    if f >= 2:
                        dve.wait_ge(ks_full, 2 * (f - 1))
                    v.tensor_scalar(kp[:, i % 2, :], kv_bank[0][0:CTX, :], 0.0, RELU_EPS, ALU.max, ALU.add).then_inc(kp_done, 1)

                def kvw_low(u):
                    dve.wait_ge(ks_hi_done, UNITS * n + u + 1)
                    part = slice(2 * HA * u, 2 * HA * (u + 1))
                    lo(kvw_lo[:, n, part], ks_bank[u % 2][:, 0:2 * HA], kvw_hi[:, n, part]).then_inc(ks_free, 1)

                def convolve(m):
                    for j in range(2):
                        if m == n:
                            conv(v.tensor_scalar(acc[:, n % 2, j, :], v_hist[:, 0, j, :], coef_sb[:, j, m:m + 1], None, ALU.mult))
                        else:
                            dve.wait_ge(conv_step, steps[0] - 1)
                            conv(v.scalar_tensor_tensor(acc[:, n % 2, j, :], v_hist[:, n - m, j, :], coef_sb[:, j, m:m + 1],
                                                        acc[:, n % 2, j, :], ALU.mult, ALU.add))

                keys(0)
                dve.wait_ge(xnT_hi_done, n + 1)
                lo(xnT_lo[:, :], t_bank, xnT_hi[:, :]).then_inc(t_free, 1)
                keys(1)
                if n >= 2:
                    dve.wait_ge(o_lo_done, n - 1)
                if n:
                    convolve(n)
                    residual(n - 1)
                if n >= 2:
                    convolve(n - 1)
                kvw_low(0)
                kvw_low(1)
                keys(2)
                if n >= 3:
                    convolve(n - 2)
                kvw_low(2)
                kvw_low(3)
                keys(3)
                if n:
                    second_norm(n - 1)
                kvw_low(4)
                kvw_low(5)
                dve.wait_ge(uv_evac, 4 * n + 4)
                convolve(0)
                kvw_low(6)
                kvw_low(7)
                if n == NB - 1:
                    wq_low(0)
                    wq_low(1)
                if n:
                    y2T_low(n - 1)
                dve.wait_ge(conv_step, steps[0])
                v.tensor_tensor(acc[:, n % 2, :, :], acc[:, n % 2, :, :], u_sb[:, :, :], ALU.mult).then_inc(o_prod, 1)

            wq_low(2)
            wq_low(3)

            v.memset(l_max[:, :], 0.0).then_inc(route, 1)

            def over(ap, dim, shape):
                return ap.unsqueeze(dim).broadcast_to(shape)
            logits = o_bank[:, 0:TPB * E].rearrange("p (t e) -> p t e", e=E)
            rank = o_bank[:, 64:64 + TPB * E].rearrange("p (t e) -> p t e", e=E)
            total = o_bank[:, 128:128 + E]

            def weighted_sum(n, h):
                f = n * H + h
                dve.wait_ge(num_done, f * TPB + TPB)
                banks = num[:, 2 * (h % 2):2 * (h % 2) + 2, 0:2 * HA].rearrange("p b (t c) -> p b t c", t=2)
                v.reciprocal(rden[:, h % 2, :].rearrange("p (b t) -> p b t", t=2), banks[:, :, :, P]).then_inc(rden_done, 1)
                wait_past(dve, att_done, f * TPB)
                dve.wait_ge(rden_done, f + 1)
                for t in range(TPB):
                    v.scalar_tensor_tensor(tile_of(n, t), banks[:, t // 2, t % 2, 0:P], rden[:, h % 2, t:t + 1], tile_of(n, t),
                                           ALU.mult, ALU.add).then_inc(att_done, 1)

            def third_moments(m):
                wait_alone(dve, att_done, m * H * TPB + H * TPB)
                for t in range(TPB):
                    v.bn_stats(stats[:, t, :], tile_of(m, t)).then_inc(ln3_stats, 1)
                wait_alone(dve, ln3_stats, m * TPB + TPB)
                for t in range(TPB):
                    v.bn_aggr(moments_b[:, t, :], stats[:, t, :]).then_inc(ln3_moments, 1)

            def third_norm(m):
                dve.wait_ge(ln3_step, m * 2 + 2)
                for t in range(TPB):
                    v.tensor_scalar(rows[:, 0, t, 0:P], tile_of(m, t), moments_b[:, t, 0:1], rstd[:, t:t + 1],
                                    ALU.subtract, ALU.mult).then_inc(y3_done, 1)

            def routing(m):
                count = [0]

                def step(make, wait=True):
                    if wait:
                        wait_alone(dve, route, m * ROUTE_STEPS + count[0] + 1)
                    count[0] += 1
                    make().then_inc(route, 1)
                kk, ke, e3 = [P, TPB, TOPK], [P, TPB, TOPK, E], [P, TPB, E]

                def softmax_start():
                    dve.wait_ge(logits_full, m + 1)
                    step(lambda: v.tensor_reduce(l_max[:, :], logits, AX.X, ALU.max), False)
                    step(lambda: v.tensor_tensor(l_sub[:, :, :], logits, over(l_max[:, :], 2, e3), ALU.subtract))

                def softmax_sum():
                    dve.wait_ge(exp_done, m + 1)
                    step(lambda: v.tensor_reduce(l_sum[:, :], l_exp[:, :, :], AX.X, ALU.add), False)
                    step(lambda: v.reciprocal(l_sum[:, :], l_sum[:, :]))

                def softmax_end():
                    step(lambda: v.tensor_tensor(prob[:, :, :], l_exp[:, :, :], over(l_sum[:, :], 2, e3), ALU.mult))

                def top():
                    for t in range(TPB):
                        step(lambda: v.max(top_v[:, t, :], prob[:, t, :]), t == 0)

                def top_index():
                    for t in range(TPB):
                        step(lambda: v.max_index(top_i[:, t, :], top_v[:, t, :], prob[:, t, :]), t == 0)

                def choose():
                    step(lambda: v.tensor_copy(top_f[:, :, :], top_i[:, :, 0:TOPK]))
                    step(lambda: v.tensor_tensor(chosen[:, :, :, :], over(top_f[:, :, :], 3, ke),
                                                 iota_e[:, :].unsqueeze(1).unsqueeze(1).broadcast_to(ke), ALU.is_equal))

                def take():
                    step(lambda: v.tensor_tensor(taken[:, :, :], chosen[:, :, 0, :], chosen[:, :, 1, :], ALU.add))
                    step(lambda: v.tensor_tensor(w_sum[:, :], top_v[:, :, 0], top_v[:, :, 1], ALU.add), False)

                def weights():
                    step(lambda: v.reciprocal(w_sum[:, :], w_sum[:, :]))
                    step(lambda: v.tensor_tensor(rows[:, :, :, P + 1].rearrange("p k t -> p t k"), top_v[:, :, 0:TOPK],
                                                 over(w_sum[:, :], 2, kk), ALU.mult))

                def slots():
                    dve.wait_ge(rank_full, m + 1)
                    step(lambda: v.tensor_tensor(slot_e[:, :, :], rank, over(base[:, :], 1, e3), ALU.add), False)
                    step(lambda: v.tensor_tensor(slot_k[:, :, :, :], chosen[:, :, :, :], over(slot_e[:, :, :], 2, ke), ALU.mult))

                def places():
                    step(lambda: v.tensor_reduce(slot_f[:, :, :], slot_k[:, :, :, :], AX.X, ALU.add))
                    step(lambda: v.tensor_tensor(base[:, :], base[:, :], total, ALU.add), False)
                    step(lambda: v.tensor_copy(slot_i[:, :, :], slot_f[:, :, :]))
                    assert count[0] == ROUTE_STEPS, count[0]
                return [softmax_start, softmax_sum, softmax_end, top, top_index, choose, take, weights, slots, places]

            def attention(n, m):
                if m is not None:
                    third_moments(m)
                    steps = list(zip(DVE_ROUTE, routing(m), strict=True))
                for k in range(H):
                    if k + 2 in LATE_LO:
                        low_part(n, k + 2)
                    if m is None and k == 0:
                        residual(NB - 1)
                    weighted_sum(n, k)
                    if m is None and k == 0:
                        second_norm(NB - 1)
                    if m is None and k == DVE_Y2:
                        y2T_low(NB - 1)
                    if m is None and k in DVE_SPLIT:
                        e = DVE_SPLIT.index(k)
                        dve.wait_ge(moe_hi_done, 2 * e + 2)
                        v.tensor_tensor(wgu_lo[:, e, :], wgu_raw[:, e % 2, :], wgu_hi[:, e, :], ALU.subtract).then_inc(moe_split, 1)
                        v.tensor_tensor(wd_lo[:, e, :], wd_raw[:, e % 2, :], wd_hi[:, e, :], ALU.subtract).then_inc(moe_split, 1)
                    if m is not None:
                        if k == DVE_NORM:
                            third_norm(m)
                        for at, step in steps:
                            if at == k:
                                step()

            def low_part(n, h):
                f = n * H + h
                dve.wait_ge(q_hi_done, f + 1)
                wait_past(dve, num_done, (f - 3) * TPB)
                v.tensor_tensor(q_lo[:, h % 4, :], q[:, h % 2, :], q_hi[:, h % 4, :], ALU.subtract).then_inc(q_lo_late, 1)

            def last_routing():
                third_moments(NB - 1)
                third_norm(NB - 1)
                for step in routing(NB - 1):
                    step()

            over_batches(dve, attention, last_routing)

            tcount = [0]

            def tstep(ins):
                tcount[0] += 1
                ins.then_inc(table_step, 1)
                dve.wait_ge(table_step, tcount[0])
            dve.wait_ge(route, NB * ROUTE_STEPS + 1)
            o = slice(0, 1)
            sh = [1, BLOCKS, E]
            tstep(v.scalar_tensor_tensor(t_val[o, :], iota_e[o, :], -float(CAP), base[o, :], ALU.mult, ALU.add))
            tstep(v.tensor_scalar(t_cnt[o, :], t_val[o, :], float(P - 1), None, ALU.add))
            tstep(v.tensor_scalar(t_cnt[o, :], t_cnt[o, :], 7, None, ALU.arith_shift_right))
            tstep(v.tensor_copy(t_nb[o, :], t_cnt[o, :]))
            tstep(v.tensor_tensor(t_prod[o, :, :], tri[o, :, :], t_nb[o, :].unsqueeze(1).broadcast_to([1, E, E]), ALU.mult))
            tstep(v.tensor_reduce(t_end[o, :], t_prod[o, :, :], AX.X, ALU.add))
            tstep(v.tensor_tensor(t_start[o, :], t_end[o, :], t_nb[o, :], ALU.subtract))
            tstep(v.tensor_scalar(t_val[o, :], t_start[o, :], -float(P), None, ALU.mult))
            tstep(v.scalar_tensor_tensor(t_val[o, :], iota_e[o, :], float(CAP), t_val[o, :], ALU.mult, ALU.add))
            tstep(v.tensor_scalar(t_sum[o, 0, 0:E], t_start[o, :], float(P), -float(PAD_ROW), ALU.mult, ALU.add))
            tstep(v.tensor_scalar(t_sum[o, 1, 0:E], t_end[o, :], float(P), -float(PAD_ROW), ALU.mult, ALU.add))
            for i in range(2):
                v.tensor_tensor(t_ge[o, i, :, :], seq[o, :].unsqueeze(2).broadcast_to(sh),
                                t_sum[o, i, 0:E].unsqueeze(1).broadcast_to(sh), ALU.is_ge).then_inc(rden_done, 1)
            dve.wait_ge(rden_done, NB * H + 2)
            tstep(v.tensor_tensor(t_oh[o, :, :], t_ge[o, 0, :, :], t_ge[o, 1, :, :], ALU.subtract))
            v.tensor_tensor(t_mul[o, 0, :, :], t_oh[o, :, :], t_val[o, :].unsqueeze(1).broadcast_to(sh), ALU.mult).then_inc(rden_done, 1)
            v.tensor_tensor(t_mul[o, 1, :, :], t_oh[o, :, :], iota_e[o, :].unsqueeze(1).broadcast_to(sh), ALU.mult).then_inc(rden_done, 1)
            v.tensor_reduce(t_sum[o, 0, :], t_oh[o, :, :], AX.X, ALU.add).then_inc(rden_done, 1)
            dve.wait_ge(rden_done, NB * H + 5)
            tstep(v.tensor_reduce(t_sum[o, 1:3, :], t_mul[o, :, :, :], AX.X, ALU.add))
            v.tensor_tensor(t_sum[o, 0, :], t_sum[o, 0, :], seq[o, :], ALU.mult).then_inc(rden_done, 1)
            dve.wait_ge(rden_done, NB * H + 6)
            v.tensor_tensor(t_sum[o, 1, :], t_sum[o, 1, :], t_sum[o, 0, :], ALU.add).then_inc(rden_done, 1)
            dve.wait_ge(rden_done, NB * H + 7)
            tstep(v.tensor_scalar(table[o, :], t_sum[o, 1, :], float(PAD_ROW), None, ALU.add))
            tstep(v.tensor_tensor(t_sum[o, 2, :], t_sum[o, 2, :], shifts[o, :, :].rearrange("p a b -> p (a b)"), ALU.mult))
            tstep(v.tensor_reduce(t_sum[o, 0, 0:BLOCKS // RING], t_sum[o, 2, :].rearrange("p (a b) -> p a b", b=RING),
                                  AX.X, ALU.add))
            tstep(v.tensor_copy(word_of[o, :], t_sum[o, 0, 0:BLOCKS // RING]))
            assert tcount[0] == TABLE_STEPS, tcount[0]

            def x_low(s, j, turn):
                dve.wait_ge(xT_hi_done, s + 1)
                lo(xT_lo[:, j, :], tx_bank[j % 2][:, 0:P], xT_hi[:, j, :]).then_inc(xT_lo_done, 1)

            def hidden(s, j, turn):
                dve.wait_ge(silu_done, s + 1)
                v.tensor_tensor(hid[:, j % 2, :], gu_bank[j % 2][:, HID:2 * HID], silu_g[:, j % 2, :], ALU.mult).then_inc(hid_done, 1)

            def h_low(s, j, turn):
                dve.wait_ge(hT_hi_done, s + 1)
                lo(hT_lo[:, j % 2, :], th_bank[j % 2][:, 0:HID], hT_hi[:, j % 2, :]).then_inc(hT_lo_done, 1)

            pipeline(dve, [(0, x_low), (1, hidden), (2, h_low)])
            for n in range(NB):
                dve.wait_ge(ld_y[n], 16 * TOPK)
                part = X[:, TPB * n:TPB * (n + 1), :].rearrange("p t c -> p (t c)")
                for k in range(TOPK):
                    v.tensor_tensor(part, part, y_back[:, k, n, :], ALU.add).then_inc(add_step, 1)
                    if k == 0:
                        dve.wait_ge(add_step, 2 * n + 1)

        @block.tensor
        def _(pe):
            def transposes(dst, srcs):
                for i, src in enumerate(srcs):
                    last = nc.tensor.transpose(dst[:, P * i:P * (i + 1)], src, ident[:, :])
                return last

            pe.wait_ge(ld_proj, 16)

            def project(ps, w, g):
                for h in range(G * g, G * (g + 1)):
                    last = nc.tensor.matmul(ps[:, M * (h % G):M * (h % G + 1)], w[0:DH, h, :], projT_sb[:, :],
                                            start=True, stop=True)
                return last
            for g in range(NG):
                pe.wait_ge(ld_wkv[g], 16)
                project(fold_bank[g], wkv_sb, g).then_inc(wk_full, 1)
            pe.wait_ge(ld_wqo, 16)
            for g in range(NG):
                pe.wait_ge(wk_lo_done, g + 1)
                for h in range(G * g, G * (g + 1)):
                    last = nc.tensor.matmul(fold_bank[g][:, P * (h % G):P * (h % G + 1)], wkv_sb[DH:P, h, :],
                                            wqo_sb[DH:P, h, :], start=True, stop=True)
                last.then_inc(wvo_full, 1)

            def turn(kind, n):
                if t_job(kind, n):
                    pe.wait_ge(t_free, t_job(kind, n))

            def out_back(n):
                pe.wait_ge(outT_done, n + 1)
                turn("out", n)
                transposes(t_bank, [outT[:, P * t:P * (t + 1)] for t in range(TPB)]).then_inc(t_full, 1)

            def mixer_out(n):
                pe.wait_ge(o_lo_done, n + 1)
                if n == 0:
                    pe.wait_ge(woa_split, 2)
                else:
                    pe.wait_ge(outT_done, n)
                for j in range(2):
                    last = split_matmul(o_bank, woa_hi[:, j, :], woa_lo[:, j, :], o_hi[:, j, :], o_lo[:, j, :],
                                        start=j == 0, stop=j == 1)
                last.then_inc(o_full, 1)

            def y2_back(n):
                pe.wait_ge(y2_done, TPB * (n + 1))
                turn("y2", n)
                transposes(t_bank, [y2[:, t, :] for t in range(TPB)]).then_inc(t_full, 1)

            for n in range(NB):
                c_hi, c_lo = (c[:, CTX * n:CTX * (n + 1)] for c in (ctxT_hi, ctxT_lo))

                def context(i):
                    f = NG * n + i
                    part = slice(POS * i, POS * (i + 1))
                    if n == 0:
                        pe.wait_ge(wk_lo_done, i + 1)
                    if f:
                        pe.wait_ge(kp_done, f)
                    split_matmul(kv_bank[0][0:CTX, :], c_hi, c_lo, feat_hi[:, part], feat_lo[:, part]).then_inc(kp_full, 1)
                    if n == 0:
                        pe.wait_ge(wvo_lo_done, i + 1)
                    if f:
                        pe.wait_ge(vw_done, f)
                    split_matmul(kv_bank[1][0:CTX, :], c_hi, c_lo, wvo_hi[:, part], wvo_lo[:, part]).then_inc(vw_full, 1)

                def kvw(u):
                    job = UNITS * n + u
                    if job >= 2:
                        pe.wait_ge(ks_free, job - 1)
                    pe.wait_ge(kp_done, NG * n + u // 2 + 1)
                    pe.wait_ge(vw_done, NG * n + u // 2 + 1)
                    for i in range(2):
                        h = 2 * (u % 2) + i
                        last = nc.tensor.matmul(ks_bank[u % 2][:, HA * i:HA * (i + 1)], kp[:, (u // 2) % 2, M * h:M * (h + 1)],
                                                vw[:, (u // 2) % 2, h, :], start=True, stop=True)
                    last.then_inc(ks_full, 1)

                if n == 0:
                    pe.wait_ge(ctx_lo_done, 1)
                context(0)
                if n == 0:
                    pe.wait_ge(consts, CONSTS)
                pe.wait_ge(xn_done, TPB * (n + 1))
                turn("xn", n)
                transposes(t_bank, [xn[:, t, :] for t in range(TPB)]).then_inc(t_full, 1)
                context(1)
                if n == 0:
                    pe.wait_ge(wuv_lo_done, 1)
                pe.wait_ge(t_free, t_job("xn", n) + 1)
                for i in range(4):
                    if 4 * n + i >= 2:
                        pe.wait_ge(uv_evac, 4 * n + i - 1)
                    w = slice(P * ((i + 2) % 4), P * ((i + 2) % 4 + 1))
                    split_matmul(uv_bank[i % 2], wuv_hi[:, w], wuv_lo[:, w], xnT_hi[:, :], xnT_lo[:, :]).then_inc(uv_full, 1)
                    if n and i == 0:
                        mixer_out(n - 1)
                if n:
                    out_back(n - 1)
                kvw(0)
                kvw(1)
                context(2)
                kvw(2)
                kvw(3)
                context(3)
                kvw(4)
                kvw(5)
                if n:
                    y2_back(n - 1)
                kvw(6)
                kvw(7)
            pe.wait_ge(uv_evac, 4 * NB)
            for g in range(NG):
                if g >= 2:
                    pe.wait_ge(wq_lo_done, g - 1)
                project(uv_bank[g % 2], wqo_sb, g).then_inc(wq_full, 1)

            pe.wait_ge(wq_lo_done, NG)
            pe.wait_ge(ks_free, UNITS * NB)

            def features(n, h):
                wait_past(pe, relu_done, n * H + h - 1)
                part = slice(M * h, M * (h + 1))
                split_matmul(z_bank[h % 2], feat_hi[:, part], feat_lo[:, part], batch(y2T_hi, n), batch(y2T_lo, n)
                             ).then_inc(z_full, 1)

            def numerators(n, h):
                f = n * H + h
                wait_lo(pe, n, h)
                kh, kl = (batch(k[:, :, HA * h:HA * (h + 1)], n) for k in (kvw_hi, kvw_lo))
                for t in range(TPB):
                    part = slice(P * t, P * (t + 1))
                    if t % 2 == 0:
                        wait_past(pe, att_done, (f - 2) * TPB + t + 2)
                    split_matmul(num[:, 2 * (h % 2) + t // 2, HA * (t % 2):HA * (t % 2 + 1)], q_hi[:, h % 4, part], q_lo[:, h % 4, part], kh, kl).then_inc(num_done, 1)

            def turn_rows(m):
                pe.wait_ge(y3_done, m * TPB + TPB)
                transposes(t_bank, [rows[:, 0, t, 0:P] for t in range(TPB)]).then_inc(tb_full, 1)

            def router_logits(m):
                pe.wait_ge(y3T_done, m + 1)
                pe.wait_ge(route, m * ROUTE_STEPS + 1)
                for t in range(TPB):
                    last = nc.tensor.matmul(o_bank[:, E * t:E * (t + 1)], y3T[:, P * t:P * (t + 1)], router_sb[:, :],
                                            start=t == 0, stop=t == TPB - 1, skip_group_check=True)
                last.then_inc(logits_full, 1)

            def ranks(m):
                pe.wait_ge(route, m * ROUTE_STEPS + TAKEN_STEP + 1)
                nc.tensor.matmul(o_bank[:, 64:64 + TPB * E], before[:, :], taken[:, :, :].rearrange("p t e -> p (t e)"),
                                 start=True, stop=False, skip_group_check=True)
                for t in range(TPB):
                    if t + 1 < TPB:
                        nc.tensor.matmul(o_bank[:, 64 + E * (t + 1):64 + E * TPB].rearrange("p (a e) -> p a e", e=E), ones_bf[:, :],
                                         taken[:, t, :].unsqueeze(1).broadcast_to([P, TPB - 1 - t, E]),
                                         start=False, stop=False, skip_group_check=True)
                    last = nc.tensor.matmul(o_bank[:, 128:128 + E], ones_bf[:, :], taken[:, t, :],
                                            start=False, stop=t == TPB - 1, skip_group_check=True)
                last.then_inc(rank_full, 1)

            def attention(n, m):
                for k in range(H):
                    features(n, k)
                    if k >= LAG:
                        numerators(n, k - LAG)
                    elif m is not None:
                        numerators(m, k - LAG + H)
                    if m is None:
                        if k == PE_MIXER:
                            mixer_out(NB - 1)
                        if k == PE_OUT:
                            out_back(NB - 1)
                        if k == PE_Y2:
                            y2_back(NB - 1)
                        if k == H - 1:
                            pe.wait_ge(t_free, 3 * NB)
                    else:
                        if k == PE_Y3:
                            turn_rows(m)
                        if k == PE_LOGITS:
                            router_logits(m)
                        if k == PE_RANKS:
                            ranks(m)

            def last_routing():
                for h in range(H - LAG, H):
                    numerators(NB - 1, h)
                turn_rows(NB - 1)
                router_logits(NB - 1)
                ranks(NB - 1)

            over_batches(pe, attention, last_routing)

            pe.wait_ge(table_step, TABLE_STEPS)
            pe.wait_ge(moe_split, 2 * E)

            def turn_x(s, j, turn, offset):
                pe.wait_ge(ld_xb[j], turn * 16 + 16)
                if not isinstance(s, int) or s >= 2:
                    pe.wait_ge(xT_lo_done, s - 1)
                nc.tensor.transpose(tx_bank[j % 2][:, 0:P], xb[:, j, 0:P], ident[:, :]).then_inc(tx_full, 1)

            def gate_up(s, j, turn, offset):
                e = expert(offset)
                pe.wait_ge(xT_lo_done, s + 1)
                if not isinstance(s, int) or s >= 2:
                    pe.wait_ge(hid_done, s - 1)
                split_matmul(gu_bank[j % 2], xT_hi[:, j, :], xT_lo[:, j, :], batch_r(wgu_hi, e), batch_r(wgu_lo, e)
                             ).then_inc(gu_full, 1)

            def turn_h(s, j, turn, offset):
                pe.wait_ge(hid_done, s + 1)
                if not isinstance(s, int) or s >= 2:
                    pe.wait_ge(hT_lo_done, s - 1)
                transposes(th_bank[j % 2], [hid[:, j % 2, P * c:P * (c + 1)] for c in range(2)]).then_inc(th_full, 1)

            def down(s, j, turn, offset):
                e = expert(offset)
                pe.wait_ge(hT_lo_done, s + 1)
                if not isinstance(s, int) or s >= 2:
                    pe.wait_ge(yo_done, s - 1)
                for c in range(2):
                    part = slice(P * c, P * (c + 1))
                    last = split_matmul(dn_bank[j % 2][:, 0:P], hT_hi[:, j % 2, part], hT_lo[:, j % 2, part],
                                        wd_hi[:, bass.ds(e, 1), part].rearrange("p a c -> p (a c)"),
                                        wd_lo[:, bass.ds(e, 1), part].rearrange("p a c -> p (a c)"),
                                        start=c == 0, stop=c == 1)
                last.then_inc(dn_full, 1)

            words = []

            def load_experts(i):
                words[:] = [pe.value_load(word_of[0:1, bass.ds(w, 1)]) if not isinstance(w, int) or 0 <= w < BLOCKS // RING
                            else None for w in (i - 1, i)]

            def expert(offset):
                word = words[0] if offset < 0 else words[1]
                return ((word >> (EBITS * (offset % RING))) & (E - 1)).with_bounds(min_val=0, max_val=E - 1)

            def batch_r(t, e):
                return t[:, bass.ds(e, 1), :].rearrange("p a c -> p (a c)")

            pipeline(pe, [(0, turn_x), (1, gate_up), (2, turn_h), (3, down)], load_experts)




def kernel(**inputs):
    import numpy as np
    import concourse.bacc as bacc
    from concourse.bass_utils import run_bass_kernel_spmd

    w = {k.replace("L0_", ""): np.asarray(v) for k, v in inputs.items()}
    coef = np.concatenate([w["attn_zero"], w["attn_pos"][:, :NB - 1]], axis=1)
    arrays = {
        "x": w["x"],
        "ctxT": w["ctx_1024"].transpose(2, 0, 1).reshape(P, NB * CTX),
        "wuv": np.concatenate([w["attn_Wu"].T, w["attn_Wv"].T], axis=1),
        "bu": w["attn_bu"].reshape(2, P).T,
        "bv": w["attn_bv"].reshape(2, P).T,
        "woaT": w["attn_Wo"].T.reshape(2, P, P).transpose(1, 0, 2),
        "bo": w["attn_bo"].reshape(P, 1),
        "coef": np.repeat(coef, MHD, axis=0).reshape(2, P, NB).transpose(1, 0, 2),
        "wkv": np.concatenate([w["xattn_Wk"].transpose(2, 1, 0), w["xattn_Wv"].transpose(2, 1, 0)], axis=0),
        "wqo": np.concatenate([w["xattn_Wq"].transpose(2, 1, 0), w["xattn_Wo"].transpose(1, 0, 2)], axis=0),
        "projT": w["xattn_proj"].T,
        "router": w["ffn_router_w"].T,
        "wgu": np.concatenate([w["ffn_w_gate"].transpose(2, 0, 1), w["ffn_w_up"].transpose(2, 0, 1)], axis=2),
        "wd": w["ffn_w_down"].transpose(2, 0, 1).reshape(2, P, E, P).transpose(1, 2, 0, 3).reshape(P, E, HID),
    }
    nc = bacc.Bacc("TRN2", target_bir_lowering=False, num_devices=1)
    feed, args = {}, []
    for name, a in arrays.items():
        feed["in_" + name] = np.ascontiguousarray(a)
        args.append(nc.dram_tensor("in_" + name, a.shape, F32, kind="ExternalInput").ap())
    out = nc.dram_tensor("out", (NB, POS, P), F32, kind="ExternalOutput").ap()
    dispatched = nc.dram_tensor("dispatched", (PAD_ROW + P, ROW), F32, kind="Internal").ap()
    expert_out = nc.dram_tensor("expert_out", (TOPK * TOKENS, P), F32, kind="Internal").ap()
    decoder_kernel(nc, *args, out, dispatched, expert_out)
    r = run_bass_kernel_spmd(nc, [feed], core_ids=[0])
    return r.results[0]["out"]
```

```python
import concourse.bass as bass
from concourse import mybir
from contextlib import ExitStack

F32 = mybir.dt.float32
F32R = mybir.dt.float32r
BF16 = mybir.dt.bfloat16
I32 = mybir.dt.int32
U32 = mybir.dt.uint32
ALU = mybir.AluOpType
ACT = mybir.ActivationFunctionType
AX = mybir.AxisListType

P = 128
NB = 4
POS = 512
TPB = POS // P
TILES = NB * TPB
D1 = 256
MH, MHD = 8, 32
CTX = 77
H, DH, M = 16, 64, 128
HA = P + 2
G = 4
NG = H // G
UNITS = H // 2
LAG = 3
E, HID = 8, 256
TOKENS = NB * POS
TOPK = 2
CAP = TOKENS
ROW = P + 2
PAD_ROW = E * CAP
BLOCKS = 40
RING = 8
EARLY = 2 * RING
LATE = BLOCKS - EARLY
EBITS = 3
LN_EPS = 1e-5
RMS_EPS = 1e-8
RELU_EPS = 1e-3
RATIO = float(M) ** -0.5
NO_DEST = TOPK * TOKENS


def decoder_kernel(nc, x, ctxT, wuv, bu, bv, woaT, bo, coef, wkv, wqo, projT, router, wgu, wd,
                   out, xs, ys):
    with ExitStack() as ctx:
        def sb(name, shape, dt=F32, stack=ctx):
            return stack.enter_context(nc.sbuf_tensor(name, shape, dt))

        def sem(name):
            return ctx.enter_context(nc.semaphore(name))

        X = sb("X", [P, TILES, P])
        y2T_hi = sb("y2T_hi", [P, NB, POS], F32R)
        y2T_lo = sb("y2T_lo", [P, NB, POS], F32R)
        feat_hi = sb("feat_hi", [P, H * M], F32R)
        feat_lo = sb("feat_lo", [P, H * M], F32R)
        kvw_hi = sb("kvw_hi", [P, NB, H * HA], F32R)
        kvw_lo = sb("kvw_lo", [P, NB, H * HA], F32R)
        router_sb = sb("router_sb", [P, E])
        outT = sb("outT", [P, POS])
        y2 = sb("y2", [P, TPB, P])
        ident = sb("ident", [P, P])
        stats = sb("stats", [P, TILES, 6])
        moments = sb("moments", [P, TILES, 2])
        moments_b = sb("moments_b", [P, TPB, 2])
        rstd = sb("rstd", [P, TPB])
        l_max = sb("l_max", [P, TPB])
        var_eps = sb("var_eps", [P, TPB])
        p_mhalf = sb("p_mhalf", [P, TILES])
        iota_e = sb("iota_e", [P, E])
        tri = sb("tri", [P, E, E])
        before = sb("before", [P, P], BF16)
        ones_bf = sb("ones_bf", [P, P], BF16)
        dest = sb("dest", [P, NB, TOPK, TPB], I32)
        seq = sb("seq", [1, LATE])
        pad_row = sb("pad_row", [P, ROW])
        base = sb("base", [P, E])
        table = sb("table", [1, BLOCKS], I32)
        word_of = sb("word_of", [1, BLOCKS // RING], I32)
        shifts = sb("shifts", [1, BLOCKS // RING, RING])

        with ExitStack() as first:
            def sa(name, shape, dt=F32):
                return sb(name, shape, dt, first)
            woa_hi = sa("woa_hi", [P, 2, P], F32R)
            woa_lo = sa("woa_lo", [P, 2, P], F32R)
            bias_o = sa("bias_o", [P, 1])
            acc = sa("acc", [P, 2, 2, POS])
            wuv_sb = acc[:, 1, 0, :]
            o_hi = sa("o_hi", [P, 2, POS], F32R)
            o_lo = sa("o_lo", [P, 2, POS], F32R)
            projT_sb = sa("projT_sb", [DH, M])
            wkv_sb = sa("wkv_sb", [P, H, P])
            wqo_sb = sa("wqo_sb", [P, H, P])
            wvo_hi = sa("wvo_hi", [P, H * P], F32R)
            wvo_lo = sa("wvo_lo", [P, H * P], F32R)
            ctxT_sb = sa("ctxT_sb", [P, NB * CTX])
            ctxT_hi = sa("ctxT_hi", [P, NB * CTX], F32R)
            ctxT_lo = sa("ctxT_lo", [P, NB * CTX], F32R)
            kp = sa("kp", [CTX, 2, G * M])
            vw = sa("vw", [CTX, 2, G, HA])
            wuv_hi = sa("wuv_hi", [P, 2 * D1], F32R)
            wuv_lo = sa("wuv_lo", [P, 2 * D1], F32R)
            woa_sb = sa("woa_sb", [P, 2, P])
            bias_v = sa("bias_v", [P, 2])
            bias_u = sa("bias_u", [P, 2])
            coef_sb = sa("coef_sb", [P, 2, NB])
            xn = sa("xn", [P, TPB, P])
            xnT_hi = sa("xnT_hi", [P, POS], F32R)
            xnT_lo = sa("xnT_lo", [P, POS], F32R)
            v_hist = sa("v_hist", [P, NB, 2, POS])
            u_sb = sa("u_sb", [P, 2, POS])
            ln1 = sa("ln1", [P, 9, TILES])
            p_half = sa("p_half", [P, TILES])
            p_mone = sa("p_mone", [P, TILES])
        V_EPS, RSTD, STD, RMS, INV, SCALE, ONE_RSTD, NEG_SHIFT, SHIFT = range(9)

        wgu_hi = sb("wgu_hi", [P, E, 2 * HID], F32R)
        wgu_lo = sb("wgu_lo", [P, E, 2 * HID], F32R)
        wd_hi = sb("wd_hi", [P, E, HID], F32R)
        wd_lo = sb("wd_lo", [P, E, HID], F32R)
        rows = sb("rows", [P, TOPK, TPB, ROW])
        y3T = sb("y3T", [P, POS])
        l_sub = sb("l_sub", [P, TPB, E])
        l_exp = sb("l_exp", [P, TPB, E])
        l_sum = sb("l_sum", [P, TPB])
        prob = sb("prob", [P, TPB, E])
        top_v = sb("top_v", [P, TPB, 8])
        top_i = sb("top_i", [P, TPB, 8], U32)
        top_f = sb("top_f", [P, TPB, TOPK])
        chosen = sb("chosen", [P, TPB, TOPK, E])
        taken = sb("taken", [P, TPB, E], BF16)
        w_sum = sb("w_sum", [P, TPB])
        slot_e = sb("slot_e", [P, TPB, E])
        slot_k = sb("slot_k", [P, TPB, TOPK, E])
        slot_f = sb("slot_f", [P, TPB, TOPK])
        slot_i = sb("slot_i", [P, TPB, TOPK], I32)
        t_cnt = sb("t_cnt", [1, E], I32)
        t_nb = sb("t_nb", [1, E])
        t_prod = sb("t_prod", [1, E, E])
        t_end = sb("t_end", [1, E])
        t_start = sb("t_start", [1, E])
        t_val = sb("t_val", [1, E])
        t_ge = sb("t_ge", [1, 2, LATE, E])
        t_oh = sb("t_oh", [1, LATE, E])
        t_mul = sb("t_mul", [1, 2, LATE, E])
        t_sum = sb("t_sum", [1, 3, LATE])
        t_tmp = sb("t_tmp", [1, E])
        t_used = sb("t_used", [1, E])
        with ExitStack() as second:
            def sc(name, shape, dt=F32):
                return sb(name, shape, dt, second)
            relu_z = sc("relu_z", [P, 2, POS])
            q = sc("q", [P, 2, POS])
            q_hi = sc("q_hi", [P, 4, POS], F32R)
            q_lo = sc("q_lo", [P, 4, POS], F32R)
            rden = sc("rden", [P, 2, TPB])
            wgu_raw = sc("wgu_raw", [P, 2, 2 * HID])
            wd_raw = sc("wd_raw", [P, 2, HID])
        xb = sb("xb", [P, RING, ROW])
        meta = sb("meta", [P, RING, 2], I32)
        xT_hi = sb("xT_hi", [P, 2, P], F32R)
        xT_lo = sb("xT_lo", [P, 2, P], F32R)
        silu_g = sb("silu_g", [P, 2, HID])
        hid = sb("hid", [P, 2, HID])
        hT_hi = sb("hT_hi", [P, 2, HID], F32R)
        hT_lo = sb("hT_lo", [P, 2, HID], F32R)
        yo = sb("yo", [P, RING, P])
        y_back = sb("y_back", [P, TOPK, NB, POS])

        bank = [ctx.enter_context(nc.psum_tensor(f"bank{i}", [P, POS], F32)) for i in range(2)]
        num = ctx.enter_context(nc.psum_tensor("num", [P, TPB, POS], F32))
        bank += [num[:, i, :] for i in range(4)]
        bank += [ctx.enter_context(nc.psum_tensor(f"bank{i}", [P, POS], F32)) for i in (6, 7)]
        bank = [b if i in (2, 3, 4, 5) else b[:, :] for i, b in enumerate(bank)]
        uv_bank, kv_bank, ks_bank, o_bank, t_bank = bank[0:2], bank[2:4], bank[4:6], bank[6], bank[7]
        fold_bank = uv_bank + ks_bank
        z_bank = bank[0:2]

        ld_x = [sem(f"ld_x{n}") for n in range(NB)]
        ld_proj, ld_wqo, ld_ctx, ld_wuv = map(sem, ("ld_proj", "ld_wqo", "ld_ctx", "ld_wuv"))
        ld_wkv = [sem(f"ld_wkv{g}") for g in range(NG)]
        ld_small, ld_woa = map(sem, ("ld_small", "ld_woa"))
        ld_moe = [sem("ld_moe_even"), sem("ld_moe_odd")]
        filled = sem("filled")
        waits_passed = sem("waits_passed")
        consts = sem("consts")
        stats_done = sem("stats_done")
        moments_done = sem("moments_done")
        ln1_step = sem("ln1_step")
        ctx_hi_done, ctx_lo_done = sem("ctx_hi_done"), sem("ctx_lo_done")
        wuv_hi_done, wuv_lo_done = sem("wuv_hi_done"), sem("wuv_lo_done")
        wk_full, wk_hi_done, wk_lo_done = sem("wk_full"), sem("wk_hi_done"), sem("wk_lo_done")
        wvo_full, wvo_hi_done, wvo_lo_done = sem("wvo_full"), sem("wvo_hi_done"), sem("wvo_lo_done")
        wq_full, wq_hi_done, wq_lo_done = sem("wq_full"), sem("wq_hi_done"), sem("wq_lo_done")
        woa_split = sem("woa_split")
        xn_done, shortcut_done = sem("xn_done"), sem("shortcut_done")
        xnT_hi_done = sem("xnT_hi_done")
        uv_full, uv_evac = sem("uv_full"), sem("uv_evac")
        kp_full, kp_done, vw_full, vw_done = sem("kp_full"), sem("kp_done"), sem("vw_full"), sem("vw_done")
        ks_full, ks_hi_done, ks_free = sem("ks_full"), sem("ks_hi_done"), sem("ks_free")
        t_full, t_free = sem("t_full"), sem("t_free")
        conv_step, o_prod, o_hi_done, o_lo_done = sem("conv_step"), sem("o_prod"), sem("o_hi_done"), sem("o_lo_done")
        o_full, outT_done = sem("o_full"), sem("outT_done")
        ln2_stats, ln2_moments, ln2_step, y2_done, y2T_hi_done = map(sem, ("ln2_stats", "ln2_moments", "ln2_step", "y2_done", "y2T_hi_done"))
        z_full, relu_done, q_done, q_hi_done, q_lo_done, q_lo_late = map(
            sem, ("z_full", "relu_done", "q_done", "q_hi_done", "q_lo_done", "q_lo_late"))
        num_done, rden_done, att_done = sem("num_done"), sem("rden_done"), sem("att_done")
        tb_full = sem("tb_full")
        ln3_stats, ln3_moments, ln3_step, y3_done, y3T_done, y3_twice = map(
            sem, ("ln3_stats", "ln3_moments", "ln3_step", "y3_done", "y3T_done", "y3_twice"))
        logits_full, exp_done, rank_full = sem("logits_full"), sem("exp_done"), sem("rank_full")
        route = sem("route")
        dest_done, sent = sem("dest_done"), sem("sent")
        moe_hi_done, moe_split = sem("moe_hi_done"), sem("moe_split")
        table_step = sem("table_step")
        ld_xb = [sem(f"ld_xb{j}") for j in range(RING)]
        meta_done, tx_full, xT_hi_done, xT_lo_done = map(sem, ("meta_done", "tx_full", "xT_hi_done", "xT_lo_done"))
        gu_full, silu_done, hid_done = sem("gu_full"), sem("silu_done"), sem("hid_done")
        th_full, hT_hi_done, hT_lo_done = sem("th_full"), sem("hT_hi_done"), sem("hT_lo_done")
        dn_full, yo_done = sem("dn_full"), sem("yo_done")
        y_sent = [sem(f"y_sent{j}") for j in range(RING)]
        ld_y = [sem(f"ld_y{n}") for n in range(NB)]
        add_step = sem("add_step")
        stored = sem("stored")

        block = ctx.enter_context(nc.Block())

        def t_job(kind, n):
            order = [("xn", 0)]
            for m in range(1, NB):
                order += [("xn", m), ("out", m - 1), ("y2", m - 1)]
            order += [("out", NB - 1), ("y2", NB - 1)]
            return order.index((kind, n))

        def split_matmul(ps, a_hi, a_lo, b_hi, b_lo, start=True, stop=True):
            nc.tensor.matmul(ps, a_hi, b_hi, start=start, stop=False)
            nc.tensor.matmul(ps, a_hi, b_lo, start=False, stop=False)
            return nc.tensor.matmul(ps, a_lo, b_hi, start=False, stop=stop)

        def batch(t, n):
            return t[:, n, :] if isinstance(n, int) else t[:, bass.ds(n, 1), :].rearrange("p a c -> p (a c)")

        def tile_of(n, t):
            return X[:, TPB * n + t, :] if isinstance(n, int) else \
                X[:, bass.ds(n * TPB + t, 1), :].rearrange("p a c -> p (a c)")

        xs_blocks = xs.rearrange("(a p) c -> p a c", p=P)
        x_view = x.rearrange("n (t p) d -> n p t d", p=P)
        out_view = out.rearrange("n (t p) d -> n p t d", p=P)
        ys_view = ys.rearrange("(k n t p) d -> k n p t d", k=TOPK, n=NB, p=P)
        FILL_ROWS = xs_blocks.shape[1]

        CONSTS = 16 + RING
        PE_MIXER, PE_OUT, PE_Y2, ACT_Y2, DVE_Y2, POOL_LN2 = 1, 2, 6, 6, 3, 2
        SPLIT = (3, 4, 6, 7, 9, 10, 12, 13)
        DVE_SPLIT = tuple(k - 2 for k in SPLIT)
        POOL_NORM = 3
        SCATTER = (13, 13, 14, 15)
        LATE_LO = (13, 14, 15)
        EARLY_LO = H - len(LATE_LO)
        DVE_NORM = 1
        DVE_ROUTE = (3, 4, 5, 5, 6, 6, 7, 7, 9, 9)
        ACT_Y3 = 6
        ACT_EXP = 8
        PE_Y3, PE_LOGITS, PE_RANKS = 6, 7, 12
        ROUTE_STEPS = 24
        TAKEN_STEP = 16
        FILLS = 3 * 16
        ROWS_EARLY, WORDS_EARLY, ROWS_LATE, WORDS_LATE = 21, 24, 50, 53
        LN1_STEPS = 10
        gu_bank, tx_bank, th_bank, dn_bank = bank[0:2], bank[2], bank[3:5], bank[5]

        def wait_past(eng, semaphore, value):
            if not isinstance(value, int) or value > 0:
                eng.wait_ge(semaphore, value)

        def wait_lo(eng, n, h):
            if h < 0:
                n, h = n - 1, h + H
            if isinstance(n, int) and n < 0:
                return
            if h in LATE_LO:
                eng.wait_ge(q_lo_late, n * len(LATE_LO) + LATE_LO.index(h) + 1)
            else:
                eng.wait_ge(q_lo_done, n * EARLY_LO + h + 1)

        def over_batches(eng, body, end):
            body(0, None)
            with eng.Fori(1, NB - 1) as n:
                body(n, n - 1)
            body(NB - 1, NB - 2)
            end()

        def wait_alone(eng, semaphore, value):
            eng.wait_ge(semaphore, value)
            if not isinstance(value, int):
                eng.sem_inc(waits_passed, 1)

        def pipeline(eng, stages, window=None, beside=None, late=None):
            depth = max(lag for lag, _ in stages)

            def tick(i, j):
                for lag, fn in stages:
                    s = i * RING + (j - lag)
                    if not isinstance(s, int) or 0 <= s < BLOCKS:
                        fn(s, (j - lag) % RING, i + (j - lag) // RING, *((j - lag,) if window else ()))
            for i in range(EARLY // RING):
                if window:
                    window(i)
                for j in range(RING):
                    tick(i, j)
                    for step in (beside or {}).get(i * RING + j, ()):
                        step()
            if late:
                late()
            with eng.Fori(EARLY // RING, BLOCKS // RING) as i:
                if window:
                    window(i)
                for j in range(RING):
                    tick(i, j)
            if window:
                window(BLOCKS // RING)
            for j in range(depth):
                tick(BLOCKS // RING, j)

        @block.sync
        def _(sp):
            sp.dma_start(projT_sb[:, :], projT).then_inc(ld_proj, 16)
            for g in range(NG):
                sp.dma_start(wkv_sb[:, G * g:G * (g + 1), :], wkv[:, G * g:G * (g + 1), :]).then_inc(ld_wkv[g], 16)
            sp.dma_start(ctxT_sb[:, :], ctxT).then_inc(ld_ctx, 16)
            sp.dma_start(wqo_sb[:, :, :], wqo).then_inc(ld_wqo, 16)
            sp.dma_start(wuv_sb, wuv).then_inc(ld_wuv, 16)
            for dst, src in ((bias_v[:, :], bv), (bias_u[:, :], bu), (bias_o[:, :], bo), (coef_sb[:, :, :], coef)):
                sp.dma_start(dst, src).then_inc(ld_small, 16)
            sp.dma_start(router_sb[:, :], router).then_inc(ld_small, 16)
            sp.dma_start(woa_sb[:, :, :], woaT).then_inc(ld_woa, 16)
            sp.wait_ge(consts, CONSTS)
            for a in range(0, FILL_ROWS, 43):
                sp.dma_start(xs_blocks[:, a:a + 43, :],
                             pad_row[:, :].unsqueeze(1).broadcast_to([P, 43, ROW])).then_inc(filled, 16)
            sp.wait_ge(wq_lo_done, NG)
            sp.wait_ge(o_full, NB)
            sp.wait_ge(ks_free, UNITS * NB)
            for e in range(E):
                if e >= 2:
                    sp.wait_ge(moe_split, 2 * (e - 1))
                sp.dma_start(wgu_raw[:, e % 2, :], wgu[:, e, :]).then_inc(ld_moe[e % 2], 16)
                sp.dma_start(wd_raw[:, e % 2, :], wd[:, e, :]).then_inc(ld_moe[e % 2], 16)
            sp.wait_ge(table_step, ROWS_EARLY)
            sp.wait_ge(sent, 16 * TOPK * TPB * (NB - 1))
            sp.wait_ge(num_done, NB * H * TPB)

            def load_block(s, j, reused):
                row = sp.value_load(table[0:1, bass.ds(s, 1)], min_val=0, max_val=PAD_ROW)
                if reused:
                    sp.wait_ge(tx_full, s - RING + 1)
                    sp.wait_ge(meta_done, s - RING + 1)
                sp.dma_start(xb[:, j, :], xs[bass.ds(row, P), :]).then_inc(ld_xb[j], 16)

            for j in range(RING):
                load_block(j, j, False)
            for s in range(RING, EARLY):
                load_block(s, s % RING, True)
            sp.wait_ge(table_step, ROWS_LATE)
            sp.wait_ge(sent, 16 * TOPK * TPB * NB)
            with sp.Fori(EARLY // RING, BLOCKS // RING) as i:
                for j in range(RING):
                    load_block(i * RING + j, j, True)
            for j in range(RING):
                sp.wait_ge(y_sent[j], 16 * BLOCKS // RING)
            for n in range(NB):
                for k in range(TOPK):
                    sp.dma_start(y_back[:, k, n, :].rearrange("p (t c) -> p t c", t=TPB),
                                 ys_view[k, n, :, :, :]).then_inc(ld_y[n], 16)
            for n in range(NB):
                sp.wait_ge(add_step, 2 * (n + 1))
                sp.dma_start(out_view[n, :, :, :], X[:, TPB * n:TPB * (n + 1), :]).then_inc(stored, 16)
            sp.wait_ge(stored, 16 * NB)

        @block.gpsimd
        def _(pool):
            g = nc.gpsimd
            made = []

            def const(ins):
                ins.then_inc(consts, 1)
                made.append(ins)

            const(g.memset(ident[:, :], 0.0))
            const(g.memset(p_mhalf[:, :], -0.5))
            const(g.memset(p_half[:, :], 0.5))
            const(g.memset(p_mone[:, :], -1.0))
            const(g.memset(vw[:, :, :, :], 0.0))
            const(g.memset(pad_row[:, :], 0.0))
            const(g.memset(tri[:, :, :], 1.0))
            const(g.memset(before[:, :], 1.0))
            const(g.memset(ones_bf[:, :], 1.0))
            const(g.iota(dest[:, :, :, :], [[POS, NB], [TOKENS, TOPK], [P, TPB]], base=0, channel_multiplier=1))
            const(g.iota(iota_e[:, :], [[1, E]], base=0, channel_multiplier=0, allow_small_or_imprecise_dtypes=True))
            pool.wait_ge(consts, 11)
            const(g.affine_select(out=ident[:, :], in_=ident[:, :], compare_op=ALU.not_equal, fill=1.0,
                                  base=0, pattern=[[-1, P]], channel_multiplier=1))
            const(g.memset(vw[:, :, :, P:P + 1], 1.0))
            const(g.iota(pad_row[:, P:P + 1].bitcast(I32), [[1, 1]], base=NO_DEST, channel_multiplier=0))
            const(g.affine_select(out=tri[:, :, :], in_=tri[:, :, :], compare_op=ALU.is_ge, fill=0.0,
                                  base=0, pattern=[[1, E], [-1, E]], channel_multiplier=0))
            const(g.affine_select(out=before[:, :], in_=before[:, :], compare_op=ALU.is_gt, fill=0.0,
                                  base=0, pattern=[[1, P]], channel_multiplier=-1))
            for j in range(RING):
                const(g.memset(shifts[:, :, j:j + 1], float(1 << EBITS * j)))
            assert len(made) == CONSTS
            g.iota(seq[:, :], [[P, LATE]], base=-PAD_ROW, channel_multiplier=0,
                   allow_small_or_imprecise_dtypes=True).then_inc(ln1_step, 1)
            g.iota(base[:, :], [[CAP, E]], base=0, channel_multiplier=0,
                   allow_small_or_imprecise_dtypes=True).then_inc(ln1_step, 1)

            def ln1_chain(tiles, before):
                mean, var = moments[:, tiles, 0], moments[:, tiles, 1]
                steps = [
                    lambda: g.tensor_scalar(ln1[:, V_EPS, tiles], var, LN_EPS, None, ALU.add),
                    lambda: g.tensor_tensor(ln1[:, STD, tiles], var, p_half[:, tiles], ALU.pow),
                    lambda: g.tensor_tensor(ln1[:, RSTD, tiles], ln1[:, V_EPS, tiles], p_mhalf[:, tiles], ALU.pow),
                    lambda: g.tensor_tensor(ln1[:, RMS, tiles], ln1[:, STD, tiles], ln1[:, RSTD, tiles], ALU.mult),
                    lambda: g.tensor_scalar(ln1[:, STD, tiles], ln1[:, RMS, tiles], RMS_EPS, None, ALU.add),
                    lambda: g.tensor_tensor(ln1[:, INV, tiles], ln1[:, STD, tiles], p_mone[:, tiles], ALU.pow),
                    lambda: g.tensor_tensor(ln1[:, SCALE, tiles], ln1[:, INV, tiles], ln1[:, RSTD, tiles], ALU.mult),
                    lambda: g.tensor_scalar(ln1[:, ONE_RSTD, tiles], ln1[:, RSTD, tiles], 1.0, None, ALU.add),
                    lambda: g.tensor_tensor(ln1[:, NEG_SHIFT, tiles], mean, ln1[:, RSTD, tiles], ALU.mult),
                    lambda: g.tensor_scalar(ln1[:, SHIFT, tiles], ln1[:, NEG_SHIFT, tiles], -1.0, None, ALU.mult),
                ]
                assert len(steps) == LN1_STEPS
                for i, step in enumerate(steps):
                    pool.wait_ge(ln1_step, before + i)
                    step().then_inc(ln1_step, 1)

            pool.wait_ge(moments_done, TPB)
            ln1_chain(slice(0, TPB), 2)
            pool.wait_ge(moments_done, TILES)
            ln1_chain(slice(TPB, TILES), LN1_STEPS + 2)

            def split(dst_hi, dst_lo, src, done, count):
                g.tensor_copy(dst_hi, src).then_inc(done, 1)
                pool.wait_ge(done, count + 1)
                g.tensor_tensor(dst_lo, src, dst_hi, ALU.subtract).then_inc(done, 1)

            pool.wait_ge(ld_woa, 16)
            split(woa_hi[:, :, :], woa_lo[:, :, :], woa_sb[:, :, :], woa_split, 0)

            def ln_rstd(var_ap, step_sem, count):
                g.tensor_scalar(var_eps[:, :], var_ap, LN_EPS, None, ALU.add).then_inc(step_sem, 1)
                pool.wait_ge(step_sem, count + 1)
                g.tensor_tensor(rstd[:, :], var_eps[:, :], p_mhalf[:, 0:TPB], ALU.pow).then_inc(step_sem, 1)

            def ln2(n):
                pool.wait_ge(ln2_moments, TPB * (n + 1))
                ln_rstd(moments_b[:, :, 1], ln2_step, 2 * n)

            for n in range(NB):
                if n == 0:
                    pool.wait_ge(ln1_step, 2 * LN1_STEPS + 2)
                pool.wait_ge(xn_done, TPB * (n + 1))
                for t in range(TPB):
                    i = TPB * n + t
                    g.tensor_scalar(X[:, i, :], X[:, i, :], ln1[:, ONE_RSTD, i:i + 1], ln1[:, SHIFT, i:i + 1],
                                    ALU.mult, ALU.add).then_inc(shortcut_done, 1)
                if n + 1 < NB:
                    pool.wait_ge(t_full, t_job("xn", n) + 1)
                    for t in range(TPB * (n + 1), TPB * (n + 2)):
                        g.tensor_scalar(xn[:, t % TPB, :], X[:, t, :], moments[:, t, 0:1], ln1[:, SCALE, t:t + 1],
                                        ALU.subtract, ALU.mult).then_inc(xn_done, 1)
                if n:
                    ln2(n - 1)
                    pool.wait_ge(ln2_step, 2 * n)
                    for t in range(TPB):
                        g.tensor_scalar(y2[:, t, :], X[:, TPB * (n - 1) + t, :], moments_b[:, t, 0:1], rstd[:, t:t + 1],
                                        ALU.subtract, ALU.mult).then_inc(y2_done, 1)
                pool.wait_ge(o_hi_done, n + 1)
                g.tensor_tensor(o_lo[:, :, :], acc[:, n % 2, :, :], o_hi[:, :, :], ALU.subtract).then_inc(o_lo_done, 1)
            pool.wait_ge(filled, FILLS)

            def third_norm(m):
                wait_alone(pool, ln3_moments, m * TPB + TPB)
                g.tensor_scalar(var_eps[:, :], moments_b[:, :, 1], LN_EPS, None, ALU.add).then_inc(ln3_step, 1)
                if not isinstance(m, int) or m > 0:
                    wait_alone(pool, sent, m * 16 * TOPK * TPB)
                pool.wait_ge(ln3_step, m * 2 + 1)
                g.tensor_tensor(rstd[:, :], var_eps[:, :], p_mhalf[:, 0:TPB], ALU.pow).then_inc(ln3_step, 1)
                g.tensor_copy(rows[:, :, :, P].bitcast(I32),
                              batch4(dest, m).rearrange("p a k t -> p (a k) t")).then_inc(dest_done, 1)

            def batch4(t, m):
                return t[:, m:m + 1, :, :] if isinstance(m, int) else t[:, bass.ds(m, 1), :, :]

            def scatter(m, t):
                if t == 0:
                    pool.wait_ge(dest_done, m + 1)
                    pool.sem_inc(waits_passed, 1)
                    wait_alone(pool, y3_twice, m + 1)
                    wait_alone(pool, route, m * ROUTE_STEPS + ROUTE_STEPS + 1)
                for k in range(TOPK):
                    g.indirect_dma_start(
                        out=xs, out_offset=bass.IndirectOffsetOnAxis(ap=slot_i[:, t, k:k + 1], axis=0),
                        in_=rows[:, k, t, :], in_offset=None).then_inc(sent, 16)

            def attention(n, m):
                for k in range(H):
                    if m is None and k == POOL_LN2:
                        ln2(NB - 1)
                    if m is not None and k == POOL_NORM:
                        third_norm(m)
                    for t in range(TPB):
                        if m is not None and k == SCATTER[t]:
                            scatter(m, t)
                    if k not in LATE_LO:
                        f = n * H + k
                        pool.wait_ge(q_hi_done, f + 1)
                        wait_past(pool, num_done, (f - 3) * TPB)
                        g.tensor_tensor(q_lo[:, k % 4, :], q[:, k % 2, :], q_hi[:, k % 4, :], ALU.subtract).then_inc(q_lo_done, 1)
            def last_routing():
                third_norm(NB - 1)

            over_batches(pool, attention, last_routing)

            def take_meta(s, j, turn):
                wait_alone(pool, ld_xb[j], turn * 16 + 16)
                if not isinstance(s, int) or s >= RING:
                    wait_alone(pool, y_sent[j], turn * 16)
                g.tensor_copy(meta[:, j, :], xb[:, j, P:P + 2].bitcast(I32)).then_inc(meta_done, 1)

            def send(s, j, turn):
                wait_alone(pool, yo_done, s + 1)
                g.indirect_dma_start(
                    out=ys, out_offset=bass.IndirectOffsetOnAxis(ap=meta[:, j, 0:1], axis=0),
                    in_=yo[:, j, :], in_offset=None, bounds_check=NO_DEST - 1, oob_is_err=False).then_inc(y_sent[j], 16)

            pipeline(pool, [(0, take_meta), (3, send)],
                     beside={6 + t: [lambda t=t: scatter(NB - 1, t)] for t in range(TPB)})

        @block.scalar
        def _(act):
            a = nc.scalar
            for n in range(NB):
                act.dma_start(X[:, TPB * n:TPB * (n + 1), :], x_view[n, :, :, :]).then_inc(ld_x[n], 16)
            a.preload_act_table(ACT.Silu)

            def copy(dst, src, **kw):
                return a.activation(dst, src, ACT.Copy, **kw)

            for g in range(NG):
                act.wait_ge(wk_full, g + 1)
                copy(feat_hi[:, POS * g:POS * (g + 1)], fold_bank[g], scale=RATIO).then_inc(wk_hi_done, 1)
            act.wait_ge(ld_ctx, 16)
            copy(ctxT_hi[:, :], ctxT_sb[:, :]).then_inc(ctx_hi_done, 1)
            for g in range(NG):
                act.wait_ge(wvo_full, g + 1)
                copy(wvo_hi[:, POS * g:POS * (g + 1)], fold_bank[g]).then_inc(wvo_hi_done, 1)
            act.wait_ge(ld_wuv, 16)
            copy(wuv_hi[:, :], wuv_sb).then_inc(wuv_hi_done, 1)
            act.wait_ge(ld_small, 16 * 5)
            act.wait_ge(consts, CONSTS)

            def y2T_high(n):
                act.wait_ge(t_full, t_job("y2", n) + 1)
                copy(y2T_hi[:, n, :], t_bank).then_inc(y2T_hi_done, 1)

            def mixer_output(n):
                act.wait_ge(o_full, n + 1)
                if n:
                    act.wait_ge(t_full, t_job("out", n - 1) + 1)
                a.activation(outT[:, :], o_bank, ACT.Identity, bias=bias_o[:, 0:1]).then_inc(outT_done, 1)

            def wq_high(g):
                act.wait_ge(wq_full, g + 1)
                copy(feat_hi[:, POS * g:POS * (g + 1)], uv_bank[g % 2], scale=RATIO).then_inc(wq_hi_done, 1)

            for n in range(NB):
                def values(i):
                    f = NG * n + i
                    act.wait_ge(vw_full, f + 1)
                    if f >= 2:
                        act.wait_ge(ks_full, 2 * (f - 1))
                    copy(vw[:, i % 2, :, 0:P], kv_bank[1][0:CTX, :].rearrange("p (h d) -> p h d", h=G)).then_inc(vw_done, 1)

                def kvw_high(u):
                    act.wait_ge(ks_full, UNITS * n + u + 1)
                    copy(kvw_hi[:, n, 2 * HA * u:2 * HA * (u + 1)], ks_bank[u % 2][:, 0:2 * HA]).then_inc(ks_hi_done, 1)

                values(0)
                act.wait_ge(t_full, t_job("xn", n) + 1)
                if n:
                    act.wait_ge(uv_full, 4 * n)
                copy(xnT_hi[:, :], t_bank).then_inc(xnT_hi_done, 1)
                values(1)
                for i in range(4):
                    act.wait_ge(uv_full, 4 * n + i + 1)
                    if n and i == 2:
                        act.wait_ge(o_prod, n)
                    dst, bias = (v_hist[:, n, i, :], bias_v) if i < 2 else (u_sb[:, i - 2, :], bias_u)
                    a.activation(dst, uv_bank[i % 2], ACT.Silu, bias=bias[:, i % 2:i % 2 + 1]).then_inc(uv_evac, 1)
                    if n and i == 0:
                        mixer_output(n - 1)
                kvw_high(0)
                kvw_high(1)
                values(2)
                kvw_high(2)
                kvw_high(3)
                values(3)
                kvw_high(4)
                kvw_high(5)
                kvw_high(6)
                kvw_high(7)
                if n == NB - 1:
                    wq_high(0)
                    wq_high(1)
                if n:
                    y2T_high(n - 1)
                act.wait_ge(o_prod, n + 1)
                if n:
                    act.wait_ge(o_full, n)
                copy(o_hi[:, :, :], acc[:, n % 2, :, :]).then_inc(o_hi_done, 1)
            wq_high(2)
            wq_high(3)

            a.preload_act_table(ACT.Exp)
            act.wait_ge(ks_free, UNITS * NB)
            act.wait_ge(wq_lo_done, NG)

            def q_high(f, slot):
                act.wait_ge(q_done, f + 1)
                wait_past(act, num_done, (f - 3) * TPB)
                copy(q_hi[:, slot % 4, :], q[:, slot % 2, :]).then_inc(q_hi_done, 1)

            def turned_rows(m):
                act.wait_ge(tb_full, m + 1)
                copy(y3T[:, :], t_bank).then_inc(y3T_done, 1)

            def second_rows(m):
                act.wait_ge(y3_done, m * TPB + TPB)
                copy(rows[:, 1, :, 0:P], rows[:, 0, :, 0:P]).then_inc(y3_twice, 1)

            def exponentials(m):
                act.wait_ge(route, m * ROUTE_STEPS + 3)
                a.activation(l_exp[:, :, :], l_sub[:, :, :], ACT.Exp).then_inc(exp_done, 1)

            def attention(n, m):
                for k in range(H):
                    f = n * H + k
                    act.wait_ge(z_full, f + 1)
                    wait_past(act, q_done, f - 1)
                    a.activation(relu_z[:, k % 2, :], z_bank[k % 2], ACT.Relu).then_inc(relu_done, 1)
                    if k or m is not None:
                        q_high(f - 1, (k - 1) % H)
                    wait_lo(act, n, k - 2)
                    act.wait_ge(relu_done, f + 1)
                    copy(q[:, k % 2, :], relu_z[:, k % 2, :], bias=RELU_EPS).then_inc(q_done, 1)
                    if m is None and k in SPLIT:
                        e = SPLIT.index(k)
                        act.wait_ge(ld_moe[e % 2], 32 * (e // 2 + 1))
                        copy(wgu_hi[:, e, :], wgu_raw[:, e % 2, :]).then_inc(moe_hi_done, 1)
                        copy(wd_hi[:, e, :], wd_raw[:, e % 2, :]).then_inc(moe_hi_done, 1)
                    if m is None and k == PE_MIXER:
                        mixer_output(NB - 1)
                    if m is None and k == ACT_Y2:
                        y2T_high(NB - 1)
                    if m is not None and k == ACT_Y3:
                        turned_rows(m)
                        second_rows(m)
                    if m is not None and k == ACT_EXP:
                        exponentials(m)

            def last_routing():
                q_high(NB * H - 1, H - 1)

            over_batches(act, attention, last_routing)

            a.preload_act_table(ACT.Silu)

            def x_high(s, j, turn):
                act.wait_ge(tx_full, s + 1)
                copy(xT_hi[:, j % 2, :], tx_bank[:, 0:P]).then_inc(xT_hi_done, 1)

            def gate(s, j, turn):
                act.wait_ge(gu_full, s + 1)
                a.activation(silu_g[:, j % 2, :], gu_bank[j % 2][:, 0:HID], ACT.Silu).then_inc(silu_done, 1)

            def h_high(s, j, turn):
                act.wait_ge(th_full, s + 1)
                copy(hT_hi[:, j % 2, :], th_bank[j % 2][:, 0:HID]).then_inc(hT_hi_done, 1)

            def weigh(s, j, turn):
                act.wait_ge(dn_full, s + 1)
                act.wait_ge(meta_done, s + 1)
                a.activation(yo[:, j, :], dn_bank[:, 0:P], ACT.Copy,
                             scale=meta[:, j, 1:2].bitcast(F32)).then_inc(yo_done, 1)

            pipeline(act, [(0, x_high), (1, gate), (2, h_high), (3, weigh)], beside={
                1: [lambda: turned_rows(NB - 1), lambda: second_rows(NB - 1)],
                2: [lambda: a.preload_act_table(ACT.Exp), lambda: exponentials(NB - 1),
                    lambda: a.preload_act_table(ACT.Silu)]})

        @block.vector
        def _(dve):
            v = nc.vector

            def lo(dst, src, hi, scale=1.0, op=ALU.mult):
                return v.scalar_tensor_tensor(dst, src, scale, hi, op, ALU.subtract)

            def first_moments(n):
                dve.wait_ge(ld_x[n], 16)
                for t in range(TPB * n, TPB * (n + 1)):
                    v.bn_stats(stats[:, t, :], X[:, t, :]).then_inc(stats_done, 1)
                dve.wait_ge(stats_done, TPB * (n + 1))
                for t in range(TPB * n, TPB * (n + 1)):
                    v.bn_aggr(moments[:, t, :], stats[:, t, :]).then_inc(moments_done, 1)

            def wk_low(g):
                dve.wait_ge(wk_hi_done, g + 1)
                part = slice(POS * g, POS * (g + 1))
                lo(feat_lo[:, part], fold_bank[g], feat_hi[:, part], RATIO).then_inc(wk_lo_done, 1)

            def wvo_low(g):
                dve.wait_ge(wvo_hi_done, g + 1)
                part = slice(POS * g, POS * (g + 1))
                lo(wvo_lo[:, part], fold_bank[g], wvo_hi[:, part]).then_inc(wvo_lo_done, 1)

            first_moments(0)
            wk_low(0)
            wk_low(1)
            first_moments(1)
            wk_low(2)
            wk_low(3)
            dve.wait_ge(ctx_hi_done, 1)
            lo(ctxT_lo[:, :], ctxT_sb[:, :], ctxT_hi[:, :]).then_inc(ctx_lo_done, 1)
            first_moments(2)
            wvo_low(0)
            wvo_low(1)
            first_moments(3)
            wvo_low(2)
            wvo_low(3)
            dve.wait_ge(wuv_hi_done, 1)
            lo(wuv_lo[:, :], wuv_sb, wuv_hi[:, :]).then_inc(wuv_lo_done, 1)

            dve.wait_ge(ln1_step, LN1_STEPS + 2)
            for t in range(TPB):
                v.tensor_scalar(xn[:, t, :], X[:, t, :], moments[:, t, 0:1], ln1[:, SCALE, t:t + 1],
                                ALU.subtract, ALU.mult).then_inc(xn_done, 1)
            steps = [0]

            def conv(ins):
                steps[0] += 1
                ins.then_inc(conv_step, 1)

            def residual(n):
                dve.wait_ge(t_full, t_job("out", n) + 1)
                dve.wait_ge(shortcut_done, TPB * (n + 1))
                part = X[:, TPB * n:TPB * (n + 1), :].rearrange("p t c -> p (t c)")
                v.tensor_tensor(part, part, t_bank, ALU.add).then_inc(t_free, 1)
                dve.wait_ge(t_free, t_job("out", n) + 1)
                for t in range(TPB):
                    v.bn_stats(stats[:, t, :], X[:, TPB * n + t, :]).then_inc(ln2_stats, 1)
                dve.wait_ge(ln2_stats, TPB * (n + 1))
                for t in range(TPB):
                    v.bn_aggr(moments_b[:, t, :], stats[:, t, :]).then_inc(ln2_moments, 1)

            def second_norm(n):
                dve.wait_ge(ln2_step, 2 * (n + 1))
                for t in range(TPB):
                    v.tensor_scalar(y2[:, t, :], X[:, TPB * n + t, :], moments_b[:, t, 0:1], rstd[:, t:t + 1],
                                    ALU.subtract, ALU.mult).then_inc(y2_done, 1)

            def y2T_low(n):
                dve.wait_ge(y2T_hi_done, n + 1)
                lo(y2T_lo[:, n, :], t_bank, y2T_hi[:, n, :]).then_inc(t_free, 1)

            def wq_low(g):
                dve.wait_ge(wq_hi_done, g + 1)
                part = slice(POS * g, POS * (g + 1))
                lo(feat_lo[:, part], uv_bank[g % 2], feat_hi[:, part], RATIO).then_inc(wq_lo_done, 1)

            for n in range(NB):
                def keys(i):
                    f = NG * n + i
                    dve.wait_ge(kp_full, f + 1)
                    if f >= 2:
                        dve.wait_ge(ks_full, 2 * (f - 1))
                    v.tensor_scalar(kp[:, i % 2, :], kv_bank[0][0:CTX, :], 0.0, RELU_EPS, ALU.max, ALU.add).then_inc(kp_done, 1)

                def kvw_low(u):
                    dve.wait_ge(ks_hi_done, UNITS * n + u + 1)
                    part = slice(2 * HA * u, 2 * HA * (u + 1))
                    lo(kvw_lo[:, n, part], ks_bank[u % 2][:, 0:2 * HA], kvw_hi[:, n, part]).then_inc(ks_free, 1)

                def convolve(m):
                    for j in range(2):
                        if m == n:
                            conv(v.tensor_scalar(acc[:, n % 2, j, :], v_hist[:, 0, j, :], coef_sb[:, j, m:m + 1], None, ALU.mult))
                        else:
                            dve.wait_ge(conv_step, steps[0] - 1)
                            conv(v.scalar_tensor_tensor(acc[:, n % 2, j, :], v_hist[:, n - m, j, :], coef_sb[:, j, m:m + 1],
                                                        acc[:, n % 2, j, :], ALU.mult, ALU.add))

                keys(0)
                dve.wait_ge(xnT_hi_done, n + 1)
                lo(xnT_lo[:, :], t_bank, xnT_hi[:, :]).then_inc(t_free, 1)
                keys(1)
                if n >= 2:
                    dve.wait_ge(o_lo_done, n - 1)
                if n:
                    convolve(n)
                    residual(n - 1)
                kvw_low(0)
                kvw_low(1)
                if n >= 2:
                    convolve(n - 1)
                keys(2)
                if n >= 3:
                    convolve(n - 2)
                kvw_low(2)
                kvw_low(3)
                keys(3)
                kvw_low(4)
                kvw_low(5)
                dve.wait_ge(uv_evac, 4 * n + 4)
                convolve(0)
                kvw_low(6)
                kvw_low(7)
                if n == NB - 1:
                    wq_low(0)
                    wq_low(1)
                if n:
                    y2T_low(n - 1)
                dve.wait_ge(conv_step, steps[0])
                v.tensor_tensor(acc[:, n % 2, :, :], acc[:, n % 2, :, :], u_sb[:, :, :], ALU.mult).then_inc(o_prod, 1)

            wq_low(2)
            wq_low(3)

            v.memset(l_max[:, :], 0.0).then_inc(route, 1)

            def over(ap, dim, shape):
                return ap.unsqueeze(dim).broadcast_to(shape)
            logits = o_bank[:, 0:TPB * E].rearrange("p (t e) -> p t e", e=E)
            rank = o_bank[:, 64:64 + TPB * E].rearrange("p (t e) -> p t e", e=E)
            total = o_bank[:, 128:128 + E]

            tcount = [0]

            def table_steps(first, count, start, stop):
                for make, wait in blocks_table(first, count)[start:stop]:
                    if wait and tcount[0]:
                        dve.wait_ge(table_step, tcount[0])
                    tcount[0] += 1
                    make().then_inc(table_step, 1)
            o = slice(0, 1)

            def blocks_table(first, count):
                steps = []

                def tstep(make, wait=True):
                    steps.append((make, wait))
                early = first == 0
                sh = [1, count, E]
                ge, oh, mul = t_ge[o, :, 0:count, :], t_oh[o, 0:count, :], t_mul[o, :, 0:count, :]
                tstep(lambda: v.scalar_tensor_tensor(t_val[o, :], iota_e[o, :], -float(CAP), base[o, :], ALU.mult, ALU.add))
                tstep(lambda: v.tensor_scalar(t_cnt[o, :], t_val[o, :], 0.0 if early else float(P - 1), None, ALU.add))
                tstep(lambda: v.tensor_scalar(t_cnt[o, :], t_cnt[o, :], 7, None, ALU.arith_shift_right))
                tstep(lambda: v.tensor_copy(t_nb[o, :], t_cnt[o, :]))
                if not early:
                    tstep(lambda: v.tensor_tensor(t_nb[o, :], t_nb[o, :], t_used[o, :], ALU.subtract))
                tstep(lambda: v.tensor_tensor(t_prod[o, :, :], tri[o, :, :], t_nb[o, :].unsqueeze(1).broadcast_to([1, E, E]), ALU.mult))
                tstep(lambda: v.tensor_reduce(t_end[o, :], t_prod[o, :, :], AX.X, ALU.add))
                tstep(lambda: v.tensor_tensor(t_start[o, :], t_end[o, :], t_nb[o, :], ALU.subtract))
                if not early:
                    tstep(lambda: v.tensor_tensor(t_tmp[o, :], t_start[o, :], t_used[o, :], ALU.subtract))
                from_start = t_start if early else t_tmp
                tstep(lambda: v.tensor_scalar(t_val[o, :], from_start[o, :], -float(P), None, ALU.mult))
                tstep(lambda: v.scalar_tensor_tensor(t_val[o, :], iota_e[o, :], float(CAP), t_val[o, :], ALU.mult, ALU.add))
                tstep(lambda: v.tensor_scalar(t_sum[o, 0, 0:E], t_start[o, :], float(P), -float(PAD_ROW), ALU.mult, ALU.add), False)
                tstep(lambda: v.tensor_scalar(t_sum[o, 1, 0:E], t_end[o, :], float(P), -float(PAD_ROW), ALU.mult, ALU.add), False)
                for i in range(2):
                    tstep(lambda i=i: v.tensor_tensor(ge[:, i, :, :], seq[o, 0:count].unsqueeze(2).broadcast_to(sh),
                                                  t_sum[o, i, 0:E].unsqueeze(1).broadcast_to(sh), ALU.is_ge), i == 0)
                tstep(lambda: v.tensor_tensor(oh, ge[:, 0, :, :], ge[:, 1, :, :], ALU.subtract))
                tstep(lambda: v.tensor_tensor(mul[:, 0, :, :], oh, t_val[o, :].unsqueeze(1).broadcast_to(sh), ALU.mult))
                tstep(lambda: v.tensor_tensor(mul[:, 1, :, :], oh, iota_e[o, :].unsqueeze(1).broadcast_to(sh), ALU.mult), False)
                tstep(lambda: v.tensor_reduce(t_sum[o, 0, 0:count], oh, AX.X, ALU.add), False)
                tstep(lambda: v.tensor_reduce(t_sum[o, 1:3, 0:count], mul, AX.X, ALU.add))
                tstep(lambda: v.tensor_tensor(t_sum[o, 0, 0:count], t_sum[o, 0, 0:count], seq[o, 0:count], ALU.mult), False)
                tstep(lambda: v.tensor_tensor(t_sum[o, 1, 0:count], t_sum[o, 1, 0:count], t_sum[o, 0, 0:count], ALU.add))
                tstep(lambda: v.tensor_scalar(table[o, first:first + count], t_sum[o, 1, 0:count], float(PAD_ROW), None, ALU.add))
                assert len(steps) == (ROWS_EARLY if early else ROWS_LATE - WORDS_EARLY - 3)
                words = slice(first // RING, (first + count) // RING)
                tstep(lambda: v.tensor_tensor(t_sum[o, 2, 0:count], t_sum[o, 2, 0:count],
                                              shifts[o, 0:count // RING, :].rearrange("p a b -> p (a b)"), ALU.mult), False)
                tstep(lambda: v.tensor_reduce(t_sum[o, 0, 0:count // RING],
                                              t_sum[o, 2, 0:count].rearrange("p (a b) -> p a b", b=RING), AX.X, ALU.add))
                tstep(lambda: v.tensor_copy(word_of[o, words], t_sum[o, 0, 0:count // RING]))
                assert len(steps) == (WORDS_EARLY if early else WORDS_LATE - WORDS_EARLY - 3)
                if early:
                    tstep(lambda: v.tensor_scalar(t_tmp[o, :], t_end[o, :], float(EARLY), None, ALU.min))
                    tstep(lambda: v.tensor_scalar(t_nb[o, :], t_start[o, :], float(EARLY), None, ALU.min), False)
                    tstep(lambda: v.tensor_tensor(t_used[o, :], t_tmp[o, :], t_nb[o, :], ALU.subtract))
                return steps

            def weighted_sum(n, h):
                f = n * H + h
                dve.wait_ge(num_done, f * TPB + TPB)
                banks = num[:, 2 * (h % 2):2 * (h % 2) + 2, 0:2 * HA].rearrange("p b (t c) -> p b t c", t=2)
                v.reciprocal(rden[:, h % 2, :].rearrange("p (b t) -> p b t", t=2), banks[:, :, :, P]).then_inc(rden_done, 1)
                wait_past(dve, att_done, f * TPB)
                dve.wait_ge(rden_done, f + 1)
                for t in range(TPB):
                    v.scalar_tensor_tensor(tile_of(n, t), banks[:, t // 2, t % 2, 0:P], rden[:, h % 2, t:t + 1], tile_of(n, t),
                                           ALU.mult, ALU.add).then_inc(att_done, 1)

            def third_moments(m):
                wait_alone(dve, att_done, m * H * TPB + H * TPB)
                for t in range(TPB):
                    v.bn_stats(stats[:, t, :], tile_of(m, t)).then_inc(ln3_stats, 1)
                wait_alone(dve, ln3_stats, m * TPB + TPB)
                for t in range(TPB):
                    v.bn_aggr(moments_b[:, t, :], stats[:, t, :]).then_inc(ln3_moments, 1)

            def third_norm(m):
                dve.wait_ge(ln3_step, m * 2 + 2)
                for t in range(TPB):
                    v.tensor_scalar(rows[:, 0, t, 0:P], tile_of(m, t), moments_b[:, t, 0:1], rstd[:, t:t + 1],
                                    ALU.subtract, ALU.mult).then_inc(y3_done, 1)

            def routing(m):
                count = [0]

                def step(make, wait=True):
                    if wait:
                        wait_alone(dve, route, m * ROUTE_STEPS + count[0] + 1)
                    count[0] += 1
                    make().then_inc(route, 1)
                kk, ke, e3 = [P, TPB, TOPK], [P, TPB, TOPK, E], [P, TPB, E]

                def softmax_start():
                    dve.wait_ge(logits_full, m + 1)
                    step(lambda: v.tensor_reduce(l_max[:, :], logits, AX.X, ALU.max), False)
                    step(lambda: v.tensor_tensor(l_sub[:, :, :], logits, over(l_max[:, :], 2, e3), ALU.subtract))

                def softmax_sum():
                    dve.wait_ge(exp_done, m + 1)
                    step(lambda: v.tensor_reduce(l_sum[:, :], l_exp[:, :, :], AX.X, ALU.add), False)
                    step(lambda: v.reciprocal(l_sum[:, :], l_sum[:, :]))

                def softmax_end():
                    step(lambda: v.tensor_tensor(prob[:, :, :], l_exp[:, :, :], over(l_sum[:, :], 2, e3), ALU.mult))

                def top():
                    for t in range(TPB):
                        step(lambda: v.max(top_v[:, t, :], prob[:, t, :]), t == 0)

                def top_index():
                    for t in range(TPB):
                        step(lambda: v.max_index(top_i[:, t, :], top_v[:, t, :], prob[:, t, :]), t == 0)

                def choose():
                    step(lambda: v.tensor_copy(top_f[:, :, :], top_i[:, :, 0:TOPK]))
                    step(lambda: v.tensor_tensor(chosen[:, :, :, :], over(top_f[:, :, :], 3, ke),
                                                 iota_e[:, :].unsqueeze(1).unsqueeze(1).broadcast_to(ke), ALU.is_equal))

                def take():
                    step(lambda: v.tensor_tensor(taken[:, :, :], chosen[:, :, 0, :], chosen[:, :, 1, :], ALU.add))
                    step(lambda: v.tensor_tensor(w_sum[:, :], top_v[:, :, 0], top_v[:, :, 1], ALU.add), False)

                def weights():
                    step(lambda: v.reciprocal(w_sum[:, :], w_sum[:, :]))
                    step(lambda: v.tensor_tensor(rows[:, :, :, P + 1].rearrange("p k t -> p t k"), top_v[:, :, 0:TOPK],
                                                 over(w_sum[:, :], 2, kk), ALU.mult))

                def slots():
                    dve.wait_ge(rank_full, m + 1)
                    step(lambda: v.tensor_tensor(slot_e[:, :, :], rank, over(base[:, :], 1, e3), ALU.add), False)
                    step(lambda: v.tensor_tensor(slot_k[:, :, :, :], chosen[:, :, :, :], over(slot_e[:, :, :], 2, ke), ALU.mult))

                def places():
                    step(lambda: v.tensor_reduce(slot_f[:, :, :], slot_k[:, :, :, :], AX.X, ALU.add))
                    step(lambda: v.tensor_tensor(base[:, :], base[:, :], total, ALU.add), False)
                    step(lambda: v.tensor_copy(slot_i[:, :, :], slot_f[:, :, :]))
                    assert count[0] == ROUTE_STEPS, count[0]
                return [softmax_start, softmax_sum, softmax_end, top, top_index, choose, take, weights, slots, places]

            def attention(n, m):
                if m is not None:
                    third_moments(m)
                    steps = list(zip(DVE_ROUTE, routing(m), strict=True))
                for k in range(H):
                    if k + 2 in LATE_LO:
                        low_part(n, k + 2)
                    if m is None and k == 0:
                        residual(NB - 1)
                    weighted_sum(n, k)
                    if m is None and k == 0:
                        second_norm(NB - 1)
                    if m is None and k == DVE_Y2:
                        y2T_low(NB - 1)
                    if m is None and k in DVE_SPLIT:
                        e = DVE_SPLIT.index(k)
                        dve.wait_ge(moe_hi_done, 2 * e + 2)
                        v.tensor_tensor(wgu_lo[:, e, :], wgu_raw[:, e % 2, :], wgu_hi[:, e, :], ALU.subtract).then_inc(moe_split, 1)
                        v.tensor_tensor(wd_lo[:, e, :], wd_raw[:, e % 2, :], wd_hi[:, e, :], ALU.subtract).then_inc(moe_split, 1)
                    if m is not None:
                        if k == DVE_NORM:
                            third_norm(m)
                        for at, step in steps:
                            if at == k:
                                step()
                        if isinstance(n, int) and k >= H - 6:
                            i = 5 * (k - (H - 6))
                            table_steps(0, EARLY, i, i + 5)

            def low_part(n, h):
                f = n * H + h
                dve.wait_ge(q_hi_done, f + 1)
                wait_past(dve, num_done, (f - 3) * TPB)
                v.tensor_tensor(q_lo[:, h % 4, :], q[:, h % 2, :], q_hi[:, h % 4, :], ALU.subtract).then_inc(q_lo_late, 1)

            def last_routing():
                third_moments(NB - 1)

            over_batches(dve, attention, last_routing)

            def x_low(s, j, turn):
                dve.wait_ge(xT_hi_done, s + 1)
                lo(xT_lo[:, j % 2, :], tx_bank[:, 0:P], xT_hi[:, j % 2, :]).then_inc(xT_lo_done, 1)

            def hidden(s, j, turn):
                dve.wait_ge(silu_done, s + 1)
                v.tensor_tensor(hid[:, j % 2, :], gu_bank[j % 2][:, HID:2 * HID], silu_g[:, j % 2, :], ALU.mult).then_inc(hid_done, 1)

            def h_low(s, j, turn):
                dve.wait_ge(hT_hi_done, s + 1)
                lo(hT_lo[:, j % 2, :], th_bank[j % 2][:, 0:HID], hT_hi[:, j % 2, :]).then_inc(hT_lo_done, 1)

            part = routing(NB - 1)
            pipeline(dve, [(0, x_low), (1, hidden), (2, h_low)], beside={
                0: [lambda: third_norm(NB - 1)], 2: part[0:1], 3: part[1:4], 4: part[4:8], 6: part[8:10],
                **{7 + i: [lambda i=i: table_steps(EARLY, LATE, 8 * i, 8 * i + 8)] for i in range(4)}})
            for n in range(NB):
                dve.wait_ge(ld_y[n], 16 * TOPK)
                part = X[:, TPB * n:TPB * (n + 1), :].rearrange("p t c -> p (t c)")
                for k in range(TOPK):
                    v.tensor_tensor(part, part, y_back[:, k, n, :], ALU.add).then_inc(add_step, 1)
                    if k == 0:
                        dve.wait_ge(add_step, 2 * n + 1)

        @block.tensor
        def _(pe):
            def transposes(dst, srcs):
                for i, src in enumerate(srcs):
                    last = nc.tensor.transpose(dst[:, P * i:P * (i + 1)], src, ident[:, :])
                return last

            pe.wait_ge(ld_proj, 16)

            def project(ps, w, g):
                for h in range(G * g, G * (g + 1)):
                    last = nc.tensor.matmul(ps[:, M * (h % G):M * (h % G + 1)], w[0:DH, h, :], projT_sb[:, :],
                                            start=True, stop=True)
                return last
            for g in range(NG):
                pe.wait_ge(ld_wkv[g], 16)
                project(fold_bank[g], wkv_sb, g).then_inc(wk_full, 1)
            pe.wait_ge(ld_wqo, 16)
            for g in range(NG):
                pe.wait_ge(wk_lo_done, g + 1)
                for h in range(G * g, G * (g + 1)):
                    last = nc.tensor.matmul(fold_bank[g][:, P * (h % G):P * (h % G + 1)], wkv_sb[DH:P, h, :],
                                            wqo_sb[DH:P, h, :], start=True, stop=True)
                last.then_inc(wvo_full, 1)

            def turn(kind, n):
                if t_job(kind, n):
                    pe.wait_ge(t_free, t_job(kind, n))

            def out_back(n):
                pe.wait_ge(outT_done, n + 1)
                turn("out", n)
                transposes(t_bank, [outT[:, P * t:P * (t + 1)] for t in range(TPB)]).then_inc(t_full, 1)

            def mixer_out(n):
                pe.wait_ge(o_lo_done, n + 1)
                if n == 0:
                    pe.wait_ge(woa_split, 2)
                else:
                    pe.wait_ge(outT_done, n)
                for j in range(2):
                    last = split_matmul(o_bank, woa_hi[:, j, :], woa_lo[:, j, :], o_hi[:, j, :], o_lo[:, j, :],
                                        start=j == 0, stop=j == 1)
                last.then_inc(o_full, 1)

            def y2_back(n):
                pe.wait_ge(y2_done, TPB * (n + 1))
                turn("y2", n)
                transposes(t_bank, [y2[:, t, :] for t in range(TPB)]).then_inc(t_full, 1)

            for n in range(NB):
                c_hi, c_lo = (c[:, CTX * n:CTX * (n + 1)] for c in (ctxT_hi, ctxT_lo))

                def context(i):
                    f = NG * n + i
                    part = slice(POS * i, POS * (i + 1))
                    if n == 0:
                        pe.wait_ge(wk_lo_done, i + 1)
                    if f:
                        pe.wait_ge(kp_done, f)
                    split_matmul(kv_bank[0][0:CTX, :], c_hi, c_lo, feat_hi[:, part], feat_lo[:, part]).then_inc(kp_full, 1)
                    if n == 0:
                        pe.wait_ge(wvo_lo_done, i + 1)
                    if f:
                        pe.wait_ge(vw_done, f)
                    split_matmul(kv_bank[1][0:CTX, :], c_hi, c_lo, wvo_hi[:, part], wvo_lo[:, part]).then_inc(vw_full, 1)

                def kvw(u):
                    job = UNITS * n + u
                    if job >= 2:
                        pe.wait_ge(ks_free, job - 1)
                    pe.wait_ge(kp_done, NG * n + u // 2 + 1)
                    pe.wait_ge(vw_done, NG * n + u // 2 + 1)
                    for i in range(2):
                        h = 2 * (u % 2) + i
                        last = nc.tensor.matmul(ks_bank[u % 2][:, HA * i:HA * (i + 1)], kp[:, (u // 2) % 2, M * h:M * (h + 1)],
                                                vw[:, (u // 2) % 2, h, :], start=True, stop=True)
                    last.then_inc(ks_full, 1)

                if n == 0:
                    pe.wait_ge(ctx_lo_done, 1)
                context(0)
                if n == 0:
                    pe.wait_ge(consts, CONSTS)
                pe.wait_ge(xn_done, TPB * (n + 1))
                turn("xn", n)
                transposes(t_bank, [xn[:, t, :] for t in range(TPB)]).then_inc(t_full, 1)
                context(1)
                if n == 0:
                    pe.wait_ge(wuv_lo_done, 1)
                pe.wait_ge(t_free, t_job("xn", n) + 1)
                for i in range(4):
                    if 4 * n + i >= 2:
                        pe.wait_ge(uv_evac, 4 * n + i - 1)
                    w = slice(P * ((i + 2) % 4), P * ((i + 2) % 4 + 1))
                    split_matmul(uv_bank[i % 2], wuv_hi[:, w], wuv_lo[:, w], xnT_hi[:, :], xnT_lo[:, :]).then_inc(uv_full, 1)
                    if n and i == 0:
                        mixer_out(n - 1)
                if n:
                    out_back(n - 1)
                kvw(0)
                kvw(1)
                context(2)
                kvw(2)
                kvw(3)
                context(3)
                kvw(4)
                kvw(5)
                if n:
                    y2_back(n - 1)
                kvw(6)
                kvw(7)
            pe.wait_ge(uv_evac, 4 * NB)
            for g in range(NG):
                if g >= 2:
                    pe.wait_ge(wq_lo_done, g - 1)
                project(uv_bank[g % 2], wqo_sb, g).then_inc(wq_full, 1)

            pe.wait_ge(wq_lo_done, NG)
            pe.wait_ge(ks_free, UNITS * NB)

            def features(n, h):
                wait_past(pe, relu_done, n * H + h - 1)
                part = slice(M * h, M * (h + 1))
                split_matmul(z_bank[h % 2], feat_hi[:, part], feat_lo[:, part], batch(y2T_hi, n), batch(y2T_lo, n)
                             ).then_inc(z_full, 1)

            def numerators(n, h):
                f = n * H + h
                wait_lo(pe, n, h)
                kh, kl = (batch(k[:, :, HA * h:HA * (h + 1)], n) for k in (kvw_hi, kvw_lo))
                for t in range(TPB):
                    part = slice(P * t, P * (t + 1))
                    if t % 2 == 0:
                        wait_past(pe, att_done, (f - 2) * TPB + t + 2)
                    split_matmul(num[:, 2 * (h % 2) + t // 2, HA * (t % 2):HA * (t % 2 + 1)], q_hi[:, h % 4, part], q_lo[:, h % 4, part], kh, kl).then_inc(num_done, 1)

            def turn_rows(m):
                pe.wait_ge(y3_done, m * TPB + TPB)
                transposes(t_bank, [rows[:, 0, t, 0:P] for t in range(TPB)]).then_inc(tb_full, 1)

            def router_logits(m):
                pe.wait_ge(y3T_done, m + 1)
                pe.wait_ge(route, m * ROUTE_STEPS + 1)
                for t in range(TPB):
                    last = nc.tensor.matmul(o_bank[:, E * t:E * (t + 1)], y3T[:, P * t:P * (t + 1)], router_sb[:, :],
                                            start=t == 0, stop=t == TPB - 1, skip_group_check=True)
                last.then_inc(logits_full, 1)

            def ranks(m):
                pe.wait_ge(route, m * ROUTE_STEPS + TAKEN_STEP + 1)
                nc.tensor.matmul(o_bank[:, 64:64 + TPB * E], before[:, :], taken[:, :, :].rearrange("p t e -> p (t e)"),
                                 start=True, stop=False, skip_group_check=True)
                for t in range(TPB):
                    if t + 1 < TPB:
                        nc.tensor.matmul(o_bank[:, 64 + E * (t + 1):64 + E * TPB].rearrange("p (a e) -> p a e", e=E), ones_bf[:, :],
                                         taken[:, t, :].unsqueeze(1).broadcast_to([P, TPB - 1 - t, E]),
                                         start=False, stop=False, skip_group_check=True)
                    last = nc.tensor.matmul(o_bank[:, 128:128 + E], ones_bf[:, :], taken[:, t, :],
                                            start=False, stop=t == TPB - 1, skip_group_check=True)
                last.then_inc(rank_full, 1)

            def attention(n, m):
                for k in range(H):
                    features(n, k)
                    if k >= LAG:
                        numerators(n, k - LAG)
                    elif m is not None:
                        numerators(m, k - LAG + H)
                    if m is None:
                        if k == PE_MIXER:
                            mixer_out(NB - 1)
                        if k == PE_OUT:
                            out_back(NB - 1)
                        if k == PE_Y2:
                            y2_back(NB - 1)
                        if k == H - 1:
                            pe.wait_ge(t_free, 3 * NB)
                    else:
                        if k == PE_Y3:
                            turn_rows(m)
                        if k == PE_LOGITS:
                            router_logits(m)
                        if k == PE_RANKS:
                            ranks(m)

            def last_routing():
                for h in range(H - LAG, H):
                    numerators(NB - 1, h)

            over_batches(pe, attention, last_routing)

            pe.wait_ge(table_step, WORDS_EARLY)
            pe.wait_ge(att_done, NB * H * TPB)
            pe.wait_ge(moe_split, 2 * E)

            def turn_x(s, j, turn, offset):
                pe.wait_ge(ld_xb[j], turn * 16 + 16)
                wait_past(pe, xT_lo_done, s)
                nc.tensor.transpose(tx_bank[:, 0:P], xb[:, j, 0:P], ident[:, :]).then_inc(tx_full, 1)

            def gate_up(s, j, turn, offset):
                e = expert(offset)
                pe.wait_ge(xT_lo_done, s + 1)
                if not isinstance(s, int) or s >= 2:
                    pe.wait_ge(hid_done, s - 1)
                split_matmul(gu_bank[j % 2], xT_hi[:, j % 2, :], xT_lo[:, j % 2, :], batch_r(wgu_hi, e), batch_r(wgu_lo, e)
                             ).then_inc(gu_full, 1)

            def turn_h(s, j, turn, offset):
                pe.wait_ge(hid_done, s + 1)
                if not isinstance(s, int) or s >= 2:
                    pe.wait_ge(hT_lo_done, s - 1)
                transposes(th_bank[j % 2], [hid[:, j % 2, P * c:P * (c + 1)] for c in range(2)]).then_inc(th_full, 1)

            def down(s, j, turn, offset):
                e = expert(offset)
                pe.wait_ge(hT_lo_done, s + 1)
                wait_past(pe, yo_done, s)
                for c in range(2):
                    part = slice(P * c, P * (c + 1))
                    last = split_matmul(dn_bank[:, 0:P], hT_hi[:, j % 2, part], hT_lo[:, j % 2, part],
                                        wd_hi[:, bass.ds(e, 1), part].rearrange("p a c -> p (a c)"),
                                        wd_lo[:, bass.ds(e, 1), part].rearrange("p a c -> p (a c)"),
                                        start=c == 0, stop=c == 1)
                last.then_inc(dn_full, 1)

            words = []

            def load_experts(i):
                words[:] = [pe.value_load(word_of[0:1, bass.ds(w, 1)]) if not isinstance(w, int) or 0 <= w < BLOCKS // RING
                            else None for w in (i - 1, i)]

            def expert(offset):
                word = words[0] if offset < 0 else words[1]
                return ((word >> (EBITS * (offset % RING))) & (E - 1)).with_bounds(min_val=0, max_val=E - 1)

            def batch_r(t, e):
                return t[:, bass.ds(e, 1), :].rearrange("p a c -> p (a c)")

            pipeline(pe, [(0, turn_x), (1, gate_up), (2, turn_h), (3, down)], load_experts, beside={
                1: [lambda: turn_rows(NB - 1), lambda: router_logits(NB - 1)], 5: [lambda: ranks(NB - 1)]},
                late=lambda: pe.wait_ge(table_step, WORDS_LATE))




def kernel(**inputs):
    import numpy as np
    import concourse.bacc as bacc
    from concourse.bass_utils import run_bass_kernel_spmd

    w = {k.replace("L0_", ""): np.asarray(v) for k, v in inputs.items()}
    coef = np.concatenate([w["attn_zero"], w["attn_pos"][:, :NB - 1]], axis=1)
    arrays = {
        "x": w["x"],
        "ctxT": w["ctx_1024"].transpose(2, 0, 1).reshape(P, NB * CTX),
        "wuv": np.concatenate([w["attn_Wu"].T, w["attn_Wv"].T], axis=1),
        "bu": w["attn_bu"].reshape(2, P).T,
        "bv": w["attn_bv"].reshape(2, P).T,
        "woaT": w["attn_Wo"].T.reshape(2, P, P).transpose(1, 0, 2),
        "bo": w["attn_bo"].reshape(P, 1),
        "coef": np.repeat(coef, MHD, axis=0).reshape(2, P, NB).transpose(1, 0, 2),
        "wkv": np.concatenate([w["xattn_Wk"].transpose(2, 1, 0), w["xattn_Wv"].transpose(2, 1, 0)], axis=0),
        "wqo": np.concatenate([w["xattn_Wq"].transpose(2, 1, 0), w["xattn_Wo"].transpose(1, 0, 2)], axis=0),
        "projT": w["xattn_proj"].T,
        "router": w["ffn_router_w"].T,
        "wgu": np.concatenate([w["ffn_w_gate"].transpose(2, 0, 1), w["ffn_w_up"].transpose(2, 0, 1)], axis=2),
        "wd": w["ffn_w_down"].transpose(2, 0, 1).reshape(2, P, E, P).transpose(1, 2, 0, 3).reshape(P, E, HID),
    }
    nc = bacc.Bacc("TRN2", target_bir_lowering=False, num_devices=1)
    feed, args = {}, []
    for name, a in arrays.items():
        feed["in_" + name] = np.ascontiguousarray(a)
        args.append(nc.dram_tensor("in_" + name, a.shape, F32, kind="ExternalInput").ap())
    out = nc.dram_tensor("out", (NB, POS, P), F32, kind="ExternalOutput").ap()
    dispatched = nc.dram_tensor("dispatched", (PAD_ROW + P, ROW), F32, kind="Internal").ap()
    expert_out = nc.dram_tensor("expert_out", (TOPK * TOKENS, P), F32, kind="Internal").ap()
    decoder_kernel(nc, *args, out, dispatched, expert_out)
    r = run_bass_kernel_spmd(nc, [feed], core_ids=[0])
    return r.results[0]["out"]
```
